# Optimizing a Trainium2 kernel written in Bass

```python
import numpy as np
import jax
import jax.numpy as jnp

def _softmax(x, axis=-1):
    return jax.nn.softmax(x, axis=axis)

def _gelu(x):
    return jax.nn.gelu(x, approximate=True)

def _silu(x):
    return jax.nn.silu(x)

def _sigmoid(x):
    return jax.nn.sigmoid(x)

def _layernorm(x, axis=-1, eps=1e-05):
    m = jnp.mean(x, axis=axis, keepdims=True)
    v = jnp.var(x, axis=axis, keepdims=True)
    return (x - m) / jnp.sqrt(v + eps)

def _scatter_add(tgt, idx, src, axis=0):
    return tgt.at[idx].add(src)

def _segment_sum(src, seg, n):
    return jax.ops.segment_sum(src, seg, n)
kernel_name = 'mk_seq_postln_d2_jaxref_r4_043220'

def setup_inputs(seed: int=0):
    np.random.seed(seed)
    _w = jnp.asarray

    def _L0_attn_setup():
        import jax, jax.numpy as jnp
        import numpy as np
        D_MODEL = 256
        LN_EPS = 1e-05
        DEN_EPS = 1e-06

        def _layer_norm(x, g, b):
            mu = jnp.mean(x, axis=-1, keepdims=True)
            var = jnp.mean(jnp.square(x - mu), axis=-1, keepdims=True)
            return (x - mu) * jax.lax.rsqrt(var + LN_EPS) * g + b
        key = jax.random.key(seed)
        ks = jax.random.split(key, 7)
        s = 1.0 / np.sqrt(D_MODEL)
        x = jax.random.normal(ks[0], (4, 512, D_MODEL), dtype=jnp.float32)
        qkv_w = jax.random.uniform(ks[1], (D_MODEL, 3 * D_MODEL), jnp.float32, -s, s)
        qkv_b = jax.random.uniform(ks[2], (3 * D_MODEL,), jnp.float32, -s, s)
        gate_w = jax.random.uniform(ks[3], (D_MODEL, D_MODEL), jnp.float32, -s, s)
        gate_b = jax.random.uniform(ks[4], (D_MODEL,), jnp.float32, -s, s)
        ln_g = jnp.ones((D_MODEL,), jnp.float32)
        ln_b = jnp.zeros((D_MODEL,), jnp.float32)
        return {'x': x, 'qkv_w': qkv_w, 'qkv_b': qkv_b, 'gate_w': gate_w, 'gate_b': gate_b, 'ln_g': ln_g, 'ln_b': ln_b}
    _L0_attn_in = _L0_attn_setup()

    def _L0_ffn_setup():
        import jax, jax.numpy as jnp
        import numpy as np
        B, N, DIM = (2, 512, 256)
        HEADS, DIM_HEAD, EXPERTS = (8, 64, 8)
        SCALE = DIM_HEAD ** (-0.5)
        key = jax.random.key(seed)
        ks = jax.random.split(key, 6)
        dim_inner = HEADS * DIM_HEAD
        return {'x': jax.random.normal(ks[0], (B, N, DIM), jnp.float32), 'w_q': jax.random.normal(ks[1], (DIM, dim_inner), jnp.float32) * 0.02, 'w_k': jax.random.normal(ks[2], (DIM, dim_inner), jnp.float32) * 0.02, 'w_gate': jax.random.normal(ks[3], (DIM, HEADS * EXPERTS), jnp.float32) * 0.02, 'value_experts': jax.random.normal(ks[4], (EXPERTS, HEADS, DIM, DIM_HEAD), jnp.float32) * 0.02, 'output_experts': jax.random.normal(ks[5], (EXPERTS, HEADS, DIM_HEAD, DIM), jnp.float32) * 0.02}
    _L0_ffn_in = _L0_ffn_setup()

    def _L1_attn_setup():
        import jax, jax.numpy as jnp
        import numpy as np
        NUM_HEADS = 16
        LN_EPS = 1e-05

        def _gelu(x):
            return jax.nn.gelu(x, approximate=False)
        key = jax.random.key(seed)
        ks = jax.random.split(key, 12)
        B, S, E = (2, 512, 256)
        H = E // 2
        s = lambda fan_in: 1.0 / np.sqrt(fan_in)
        inp = {'x': jax.random.normal(ks[0], (B, S, E), jnp.float32), 'Wq': jax.random.normal(ks[1], (E, E), jnp.float32) * s(E), 'bq': jnp.zeros((E,), jnp.float32), 'Wk': jax.random.normal(ks[2], (E, E), jnp.float32) * s(E), 'bk': jnp.zeros((E,), jnp.float32), 'Wv': jax.random.normal(ks[3], (E, E), jnp.float32) * s(E), 'bv': jnp.zeros((E,), jnp.float32), 'Wo': jax.random.normal(ks[4], (E, E), jnp.float32) * s(E), 'bo': jnp.zeros((E,), jnp.float32), 'dp_w1': jax.random.normal(ks[5], (E, H), jnp.float32) * s(E), 'dp_b1': jnp.zeros((H,), jnp.float32), 'ln_g': jnp.ones((H,), jnp.float32), 'ln_b': jnp.zeros((H,), jnp.float32), 'dp_w2': jax.random.normal(ks[6], (H, 1), jnp.float32) * s(H), 'dp_b2': jnp.zeros((1,), jnp.float32), 'g_w1': jax.random.normal(ks[7], (1, 16), jnp.float32), 'g_b1': jnp.zeros((16,), jnp.float32), 'g_w2': jax.random.normal(ks[8], (16, 1), jnp.float32) * s(16), 'g_b2': jnp.zeros((1,), jnp.float32)}
        return inp
    _L1_attn_in = _L1_attn_setup()

    def _L1_ffn_setup():
        import jax, jax.numpy as jnp
        import numpy as np
        D_IN, D_HID = (256, 1024)

        def _ternary(key, shape):
            return jax.random.randint(key, shape, -1, 2).astype(jnp.float32)

        def _tlin(x, w, s):
            return jnp.einsum('bsi,oi->bso', x, w) * s
        key = jax.random.key(seed)
        ks = jax.random.split(key, 12)
        inv = lambda fan: 1.0 / np.sqrt(fan).astype(np.float32)
        return {'x': jax.random.normal(ks[0], (4, 512, D_IN), dtype=jnp.float32), 'w1_w': _ternary(ks[1], (D_HID, D_IN)), 'w1_s': jax.random.uniform(ks[2], (D_HID,), dtype=jnp.float32) * inv(D_IN), 'w2_w': _ternary(ks[3], (D_HID, D_IN)), 'w2_s': jax.random.uniform(ks[4], (D_HID,), dtype=jnp.float32) * inv(D_IN), 'h1_w': _ternary(ks[5], (D_HID, D_HID)), 'h1_s': jax.random.uniform(ks[6], (D_HID,), dtype=jnp.float32) * inv(D_HID), 'h2_w': _ternary(ks[7], (D_HID, D_HID)), 'h2_s': jax.random.uniform(ks[8], (D_HID,), dtype=jnp.float32) * inv(D_HID), 'w3_w': _ternary(ks[9], (D_IN, D_HID)), 'w3_s': jax.random.uniform(ks[10], (D_IN,), dtype=jnp.float32) * inv(D_HID)}
    _L1_ffn_in = _L1_ffn_setup()
    _d = {'L0_attn_x': _L0_attn_in['x'], 'L0_attn_qkv_w': _L0_attn_in['qkv_w'], 'L0_attn_qkv_b': _L0_attn_in['qkv_b'], 'L0_attn_gate_w': _L0_attn_in['gate_w'], 'L0_attn_gate_b': _L0_attn_in['gate_b'], 'L0_attn_ln_g': _L0_attn_in['ln_g'], 'L0_attn_ln_b': _L0_attn_in['ln_b'], 'L0_ffn_w_q': _L0_ffn_in['w_q'], 'L0_ffn_w_k': _L0_ffn_in['w_k'], 'L0_ffn_w_gate': _L0_ffn_in['w_gate'], 'L0_ffn_value_experts': _L0_ffn_in['value_experts'], 'L0_ffn_output_experts': _L0_ffn_in['output_experts'], 'L1_attn_Wq': _L1_attn_in['Wq'], 'L1_attn_bq': _L1_attn_in['bq'], 'L1_attn_Wk': _L1_attn_in['Wk'], 'L1_attn_bk': _L1_attn_in['bk'], 'L1_attn_Wv': _L1_attn_in['Wv'], 'L1_attn_bv': _L1_attn_in['bv'], 'L1_attn_Wo': _L1_attn_in['Wo'], 'L1_attn_bo': _L1_attn_in['bo'], 'L1_attn_dp_w1': _L1_attn_in['dp_w1'], 'L1_attn_dp_b1': _L1_attn_in['dp_b1'], 'L1_attn_ln_g': _L1_attn_in['ln_g'], 'L1_attn_ln_b': _L1_attn_in['ln_b'], 'L1_attn_dp_w2': _L1_attn_in['dp_w2'], 'L1_attn_dp_b2': _L1_attn_in['dp_b2'], 'L1_attn_g_w1': _L1_attn_in['g_w1'], 'L1_attn_g_b1': _L1_attn_in['g_b1'], 'L1_attn_g_w2': _L1_attn_in['g_w2'], 'L1_attn_g_b2': _L1_attn_in['g_b2'], 'L1_ffn_w1_w': _L1_ffn_in['w1_w'], 'L1_ffn_w1_s': _L1_ffn_in['w1_s'], 'L1_ffn_w2_w': _L1_ffn_in['w2_w'], 'L1_ffn_w2_s': _L1_ffn_in['w2_s'], 'L1_ffn_h1_w': _L1_ffn_in['h1_w'], 'L1_ffn_h1_s': _L1_ffn_in['h1_s'], 'L1_ffn_h2_w': _L1_ffn_in['h2_w'], 'L1_ffn_h2_s': _L1_ffn_in['h2_s'], 'L1_ffn_w3_w': _L1_ffn_in['w3_w'], 'L1_ffn_w3_s': _L1_ffn_in['w3_s']}
    _x0 = _d['L0_attn_x']
    _d['L0_attn_x'] = jax.random.normal(jax.random.fold_in(jax.random.key(seed), 1), (4, 1024, 256), dtype=_x0.dtype)
    del _x0
    return _d

def reference(L0_attn_x, L0_attn_qkv_w, L0_attn_qkv_b, L0_attn_gate_w, L0_attn_gate_b, L0_attn_ln_g, L0_attn_ln_b, L0_ffn_w_q, L0_ffn_w_k, L0_ffn_w_gate, L0_ffn_value_experts, L0_ffn_output_experts, L1_attn_Wq, L1_attn_bq, L1_attn_Wk, L1_attn_bk, L1_attn_Wv, L1_attn_bv, L1_attn_Wo, L1_attn_bo, L1_attn_dp_w1, L1_attn_dp_b1, L1_attn_ln_g, L1_attn_ln_b, L1_attn_dp_w2, L1_attn_dp_b2, L1_attn_g_w1, L1_attn_g_b1, L1_attn_g_w2, L1_attn_g_b2, L1_ffn_w1_w, L1_ffn_w1_s, L1_ffn_w2_w, L1_ffn_w2_s, L1_ffn_h1_w, L1_ffn_h1_s, L1_ffn_h2_w, L1_ffn_h2_s, L1_ffn_w3_w, L1_ffn_w3_s):

    def _L0_attn_ref(x, qkv_w, qkv_b, gate_w, gate_b, ln_g, ln_b):
        import jax, jax.numpy as jnp
        import numpy as np
        D_MODEL = 256
        LN_EPS = 1e-05
        DEN_EPS = 1e-06

        def _layer_norm(x, g, b):
            mu = jnp.mean(x, axis=-1, keepdims=True)
            var = jnp.mean(jnp.square(x - mu), axis=-1, keepdims=True)
            return (x - mu) * jax.lax.rsqrt(var + LN_EPS) * g + b
        B, T, D = x.shape
        xn = _layer_norm(x, ln_g, ln_b)
        qkv = xn @ qkv_w + qkv_b
        q, k, v = jnp.split(qkv, 3, axis=-1)
        gate = jax.nn.sigmoid(xn @ gate_w + gate_b)
        k = k * gate
        q = jax.nn.elu(q) + 1.0
        k = jax.nn.elu(k) + 1.0
        attn = jnp.einsum('btd,bsd->bts', q, k)
        mask = jnp.tril(jnp.ones((T, T), dtype=attn.dtype))
        attn = attn * mask
        out_num = jnp.einsum('bts,bsd->btd', attn, v)
        k_cumsum = jnp.cumsum(k, axis=1)
        out_den = jnp.sum(q * k_cumsum, axis=-1, keepdims=True) + DEN_EPS
        return out_num / out_den

    def _L0_ffn_ref(x, w_q, w_k, w_gate, value_experts, output_experts):
        import jax, jax.numpy as jnp
        import numpy as np
        B, N, DIM = (2, 512, 256)
        HEADS, DIM_HEAD, EXPERTS = (8, 64, 8)
        SCALE = DIM_HEAD ** (-0.5)
        b, n, _ = x.shape
        q = (x @ w_q).reshape(b, n, HEADS, DIM_HEAD).transpose(0, 2, 1, 3)
        k = (x @ w_k).reshape(b, n, HEADS, DIM_HEAD).transpose(0, 2, 1, 3)
        gates = jax.nn.sigmoid((x @ w_gate).reshape(b, n, HEADS, EXPERTS).transpose(0, 2, 1, 3))
        sel = jnp.argmax(gates, axis=-1)
        gm = jax.nn.one_hot(sel, EXPERTS, dtype=x.dtype) * gates
        values = jnp.einsum('bhne,ehdk,bnd->bhnk', gm, value_experts, x)
        sim = jnp.einsum('bhid,bhjd->bhij', q * SCALE, k)
        causal_mask = jnp.triu(jnp.ones((n, n), dtype=bool), 1)
        sim = jnp.where(causal_mask, jnp.finfo(sim.dtype).min, sim)
        attn = jax.nn.softmax(sim, axis=-1)
        out = jnp.einsum('bhij,bhjk->bhik', attn, values)
        out = jnp.einsum('bhne,ehkd,bhnk->bhnd', gm, output_experts, out)
        return out.sum(axis=1)

    def _L1_attn_ref(x, Wq, bq, Wk, bk, Wv, bv, Wo, bo, dp_w1, dp_b1, ln_g, ln_b, dp_w2, dp_b2, g_w1, g_b1, g_w2, g_b2):
        import jax, jax.numpy as jnp
        import numpy as np
        NUM_HEADS = 16
        LN_EPS = 1e-05

        def _gelu(x):
            return jax.nn.gelu(x, approximate=False)
        B, S, E = x.shape
        Hn = NUM_HEADS
        Dh = E // Hn
        scale = Dh ** (-0.5)
        Q = (x @ Wq + bq).reshape(B, S, Hn, Dh)
        K = (x @ Wk + bk).reshape(B, S, Hn, Dh)
        V = (x @ Wv + bv).reshape(B, S, Hn, Dh)
        logits = jnp.einsum('bqhd,bkhd->bhqk', Q, K) * scale
        causal = jnp.tril(jnp.ones((S, S), bool))
        logits = jnp.where(causal, logits, -jnp.inf)
        attn = jax.nn.softmax(logits, axis=-1)
        h = x @ dp_w1 + dp_b1
        mu = h.mean(-1, keepdims=True)
        var = ((h - mu) ** 2).mean(-1, keepdims=True)
        h = (h - mu) / jnp.sqrt(var + LN_EPS) * ln_g + ln_b
        drift = (_gelu(h) @ dp_w2 + dp_b2)[..., 0]
        g = _gelu(drift[..., None] * g_w1[0] + g_b1)
        gate = jnp.tanh(g @ g_w2 + g_b2)[..., 0]
        gated = attn * gate[:, None, None, :]
        out = jnp.einsum('bhqk,bkhd->bqhd', gated, V).reshape(B, S, E)
        return out @ Wo + bo

    def _L1_ffn_ref(x, w1_w, w1_s, w2_w, w2_s, h1_w, h1_s, h2_w, h2_s, w3_w, w3_s):
        import jax, jax.numpy as jnp
        import numpy as np
        D_IN, D_HID = (256, 1024)

        def _ternary(key, shape):
            return jax.random.randint(key, shape, -1, 2).astype(jnp.float32)

        def _tlin(x, w, s):
            return jnp.einsum('bsi,oi->bso', x, w) * s
        h = jax.nn.silu(_tlin(x, w1_w, w1_s)) * _tlin(x, w2_w, w2_s)
        h = jax.nn.gelu(_tlin(h, h1_w, h1_s), approximate=False)
        h = jax.nn.gelu(_tlin(h, h2_w, h2_s), approximate=False)
        return _tlin(h, w3_w, w3_s)
    x = L0_attn_x
    x = _layernorm(x + _L0_attn_ref(x, L0_attn_qkv_w, L0_attn_qkv_b, L0_attn_gate_w, L0_attn_gate_b, L0_attn_ln_g, L0_attn_ln_b), axis=-1)
    x = _layernorm(x + _L0_ffn_ref(x, L0_ffn_w_q, L0_ffn_w_k, L0_ffn_w_gate, L0_ffn_value_experts, L0_ffn_output_experts), axis=-1)
    x = _layernorm(x + _L1_attn_ref(x, L1_attn_Wq, L1_attn_bq, L1_attn_Wk, L1_attn_bk, L1_attn_Wv, L1_attn_bv, L1_attn_Wo, L1_attn_bo, L1_attn_dp_w1, L1_attn_dp_b1, L1_attn_ln_g, L1_attn_ln_b, L1_attn_dp_w2, L1_attn_dp_b2, L1_attn_g_w1, L1_attn_g_b1, L1_attn_g_w2, L1_attn_g_b2), axis=-1)
    x = _layernorm(x + _L1_ffn_ref(x, L1_ffn_w1_w, L1_ffn_w1_s, L1_ffn_w2_w, L1_ffn_w2_s, L1_ffn_h1_w, L1_ffn_h1_s, L1_ffn_h2_w, L1_ffn_h2_s, L1_ffn_w3_w, L1_ffn_w3_s), axis=-1)
    return x

_drawn_inputs = setup_inputs


def setup_inputs(seed=0):
    import zlib

    import numpy as np

    out = dict(_drawn_inputs(seed))
    spreads = {'L0_attn_ln_g': (1.0, 0.6),
     'L0_attn_ln_b': (0.0, 0.1),
     'L1_attn_bq': (0.0, 0.8),
     'L1_attn_bk': (0.0, 2.0),
     'L1_attn_bv': (0.0, 0.8),
     'L1_attn_bo': (0.0, 0.1),
     'L1_attn_dp_b1': (0.0, 0.8),
     'L1_attn_ln_g': (1.0, 0.6),
     'L1_attn_ln_b': (0.0, 0.8),
     'L1_attn_g_b1': (0.0, 0.411)}
    factors = {'L0_attn_gate_w': 8.0,
     'L0_attn_gate_b': 21.663,
     'L0_ffn_w_q': 8.0,
     'L0_ffn_w_k': 8.0,
     'L0_ffn_w_gate': 8.0,
     'L0_ffn_value_experts': 8.0,
     'L0_ffn_output_experts': 8.0,
     'L1_attn_Wq': 4.0,
     'L1_attn_Wk': 3.945,
     'L1_attn_Wv': 2.674,
     'L1_attn_g_w1': 4.078,
     'L1_ffn_w1_w': 8.0,
     'L1_ffn_w1_s': 8.0,
     'L1_ffn_w2_w': 8.0,
     'L1_ffn_w2_s': 8.0,
     'L1_ffn_h1_w': 8.0,
     'L1_ffn_h1_s': 8.0,
     'L1_ffn_h2_w': 8.0,
     'L1_ffn_h2_s': 8.0,
     'L1_ffn_w3_w': 8.0,
     'L1_ffn_w3_s': 8.0}
    for name, (base, spread) in spreads.items():
        noise = np.random.default_rng([zlib.crc32(name.encode()), seed]).standard_normal(out[name].shape)
        drawn = base * np.exp(spread * noise) if base else spread * noise
        out[name] = jnp.asarray(drawn.astype(out[name].dtype))
    for name, factor in factors.items():
        out[name] = (out[name] * factor).astype(out[name].dtype)
    return out
```

```python
from collections import namedtuple
from contextlib import ExitStack


import numpy as np

import concourse.bass as bass
from concourse import mybir

ALU = mybir.AluOpType
ACT = mybir.ActivationFunctionType
F32 = mybir.dt.float32
F32R = mybir.dt.float32r
BF16 = mybir.dt.bfloat16
AX_X = mybir.AxisListType.X

P = 128
D = 256
KC = D // P
SEQS = 4
T = 1024
NT = T // P
HALF = 512
NH = T // HALF
EPS = 1e-5
DEN_EPS = 1e-6

H0, DH0, NE = 8, 64, 8
SCALE0 = DH0 ** -0.5
H1, DH1 = 16, 16
SCALE1 = DH1 ** -0.5
G1 = 4
HID = 1024
HC = HID // P


class Memory:

    def __init__(self, nc, ctx):
        def sb(name, shape, dt=F32):
            return ctx.enter_context(nc.sbuf_tensor("sb_" + name, shape, dt))

        self.ps = ctx.enter_context(nc.psum_tensor("sums", [P, 8 * HALF], F32))
        self.x, self.xT = sb("x", [P, NT, D]), sb("xT", [P, KC, T])
        self.y, self.ys, self.y2 = None, 0, None
        self.stats, self.moments = sb("stats", [P, NT, 6]), sb("moments", [P, NT, 2])
        self.sd, self.rstd, self.eps = sb("sd", [P, NT]), sb("rstd", [P, NT]), sb("eps", [P, 1])
        self.ident, self.ident16 = sb("ident", [P, P]), sb("ident16", [P, P], BF16)
        self.mask_kq, self.mask_qk = sb("mask_kq", [P, P], BF16), sb("mask_qk", [P, P], BF16)
        self.negones = sb("negones", [P, P], F32R)


def bank(ps, n, lo=0, hi=HALF, rows=slice(0, P)):
    return ps[rows, n * HALF + lo:n * HALF + hi]


def halves(lo, hi):
    return [(max(lo, h * HALF), min(hi, (h + 1) * HALF)) for h in range(NH) if max(lo, h * HALF) < min(hi, (h + 1) * HALF)]


class Chain:

    def __init__(self, engine, sem):
        self.engine, self.sem, self.n = engine, sem, 0

    def __call__(self, instruction):
        self.n += 1
        instruction.then_inc(self.sem, 1)
        self.engine.wait_ge(self.sem, self.n)


def signals(nc, ctx, stage, names):
    return namedtuple(stage, names)(*(ctx.enter_context(nc.semaphore(f"{stage}_{n}")) for n in names.split()))


def clear(pool, stale):
    for sem in stale:
        pool.sem_clear(sem)



NORM = "src_in stats moments sd chain x_norm transposed xT_ready out_done"


def give_y(nc, own, m):
    m.ys += 1
    m.y = own.enter_context(nc.sbuf_tensor(f"sb_y{m.ys}", [P, NT, D], F32))


def inverse_sd(step, dve, m, r, var, sd):
    step(dve.reciprocal(r[:, :], sd[:, :]))
    step(dve.tensor_tensor(sd[:, :], r[:, :], r[:, :], ALU.mult))
    step(dve.scalar_tensor_tensor(sd[:, :], var, m.eps[:, 0:1], sd[:, :], ALU.add, ALU.mult))
    step(dve.tensor_scalar(sd[:, :], sd[:, :], -0.5, 1.5, ALU.mult, ALU.add))
    step(dve.tensor_tensor(r[:, :], r[:, :], sd[:, :], ALU.mult))


def norm_stage(nc, m, s, stale, src, dst=None, affine=None):
    with ExitStack() as own, nc.Block() as block:
        if not affine:
            give_y(nc, own, m)
        raw = m.x if affine else m.y
        xn = m.y2 if affine else m.x

        @block.sync
        def _(sp):
            for h in range(2):
                sp.dma_start(raw[:, 4 * h:4 * h + 4, :], src[:, 4 * h:4 * h + 4, :]).then_inc(s.src_in, 16)
            if dst is not None:
                for h in range(2):
                    sp.wait_ge(s.x_norm, 4 * h + 4)
                    sp.dma_start(dst[:, 4 * h:4 * h + 4, :], xn[:, 4 * h:4 * h + 4, :]).then_inc(s.out_done, 16)
                sp.wait_ge(s.out_done, 32)

        @block.vector
        def _(dve):
            dve.wait_ge(s.src_in, 32)
            for t in range(NT):
                dve.bn_stats(m.stats[:, t, :], raw[:, t, :]).then_inc(s.stats, 1)
            dve.wait_ge(s.stats, NT)
            for t in range(NT):
                dve.bn_aggr(m.moments[:, t, :], m.stats[:, t, :]).then_inc(s.moments, 1)
            dve.wait_ge(s.sd, 1)
            inverse_sd(Chain(dve, s.chain), dve, m, m.rstd, m.moments[:, :, 1], m.sd)
            for t in range(NT):
                dve.tensor_scalar(xn[:, t, :], raw[:, t, :], m.moments[:, t, 0:1], m.rstd[:, t:t + 1],
                                  ALU.subtract, ALU.mult).then_inc(s.x_norm, 1)

        @block.scalar
        def _(act):
            act.wait_ge(s.moments, NT)
            act.activation(m.sd[:, :], m.moments[:, :, 1], ACT.Sqrt, bias=m.eps[:, 0:1]).then_inc(s.sd, 1)
            if dst is None:
                for t in range(NT):
                    act.wait_ge(s.transposed, t + 1)
                    for c in range(KC):
                        out, got = m.xT[:, c, t * P:(t + 1) * P], bank(m.ps, t % 2, c * P, (c + 1) * P)
                        if affine:
                            act.activation(out, got, ACT.Identity, scale=affine[0][:, c:c + 1],
                                           bias=affine[1][:, c:c + 1]).then_inc(s.xT_ready, 1)
                        else:
                            act.copy(out, got).then_inc(s.xT_ready, 1)

        @block.gpsimd
        def _(pool):
            clear(pool, stale)

        @block.tensor
        def _(pe):
            if dst is None:
                for t in range(NT):
                    pe.wait_ge(s.x_norm, t + 1)
                    if t >= 2:
                        pe.wait_ge(s.xT_ready, KC * (t - 1))
                    for c in range(KC):
                        last = pe.transpose(bank(m.ps, t % 2, c * P, (c + 1) * P), xn[:, t, c * P:(c + 1) * P], m.ident[:, :])
                    last.then_inc(s.transposed, 1)



PROJ1 = "gate_mm qk_mm v_mm gate_read half_gate k_gated min_ready relu_ready exp_ready v_read qkT_ready chain"
ATTN1 = "score_mm score_copied masked out_mm den y_ready y_out rden"


def layer1(nc, ctx, m, I, src, dst):
    sb = lambda name, shape, dt=F32: ctx.enter_context(nc.sbuf_tensor("l1_" + name, shape, dt))
    wqkv, wgate = sb("wqkv", [P, KC, 3 * D]), sb("wgate", [P, KC, D])
    bqkv, bgate, hbgate = sb("bqkv", [P, 6]), sb("bgate", [P, KC]), sb("hbgate", [P, KC])
    bv, lng, lnb = sb("bv", [P, D]), sb("lng", [P, KC]), sb("lnb", [P, KC])
    qT, kT = sb("qT", [P, KC, T]), sb("kT", [P, KC, T])
    v = sb("v", [P, NT, D + 2])
    gate = sb("gate", [P, 2 * NH, HALF])
    kg = sb("kg", [P, 2 * NH, HALF])
    neg = sb("neg", [P, 4 * NH, HALF])
    AT = sb("AT", [P, NT, T])
    den = sb("den", [P, NT, 2])
    ld = signals(nc, ctx, "l1_load", "weights ones hb")
    s0 = signals(nc, ctx, "l1_norm", NORM)
    s1 = signals(nc, ctx, "l1_proj", PROJ1)
    s2 = signals(nc, ctx, "l1_attn", ATTN1)

    with nc.Block() as block:
        @block.sync
        def _(sp):
            pairs = [(wqkv, "wqkv"), (wgate, "wgate"), (bqkv, "bqkv"), (bgate, "bgate"), (bv, "bv"), (lng, "lng"), (lnb, "lnb")]
            for tile, name in pairs:
                sp.dma_start(tile[:], I[name]).then_inc(ld.weights, 16)
            sp.wait_ge(ld.weights, 16 * len(pairs))

        @block.vector
        def _(dve):
            dve.memset(v[:, :, D:D + 2], 1.0).then_inc(ld.ones, 1)
            dve.wait_ge(ld.weights, 16 * 7)
            dve.tensor_scalar(hbgate[:, :], bgate[:, :], 0.5, None, ALU.mult).then_inc(ld.hb, 1)

    NG = KC * NH
    with nc.Fori(0, SEQS) as b:
        norm_stage(nc, m, s0, s2, src[b], affine=(lng, lnb))

        with nc.Block() as block:
            s = s1

            @block.gpsimd
            def _(pool):
                clear(pool, s0)
                for j in range(2 * NG):
                    n, c = divmod(j // 2, KC)
                    pool.wait_ge(s.exp_ready, j + 1)
                    out = (kT if j % 2 == 0 else qT)[:, c, n * HALF:(n + 1) * HALF]
                    pool.wait_ge(s.relu_ready, j + 1)
                    pool.tensor_tensor(out, out, neg[:, j, :], ALU.add).then_inc(s.qkT_ready, 1)

            @block.tensor
            def _(pe):
                def product(out, w, lo, n):
                    for c in range(KC):
                        last = pe.matmul(out, w[:, c, lo:lo + P], m.xT[:, c, n * HALF:(n + 1) * HALF],
                                         start=(c == 0), stop=(c == KC - 1))
                    return last

                for g in range(NG):
                    n, c = divmod(g, KC)
                    if g >= 2:
                        pe.wait_ge(s.gate_read, g - 1)
                    product(bank(m.ps, 2 + g % 2), wgate, c * P, n).then_inc(s.gate_mm, 1)
                    if g >= 2:
                        pe.wait_ge(s.relu_ready, 2 * (g - 1))
                    product(bank(m.ps, 4 + g % 2), wqkv, D + c * P, n).then_inc(s.qk_mm, 1)
                    product(bank(m.ps, 6 + g % 2), wqkv, c * P, n).then_inc(s.qk_mm, 1)
                for t in range(NT):
                    if t >= 2:
                        pe.wait_ge(s.v_read, t - 1)
                    for c in range(KC):
                        last = pe.matmul(bank(m.ps, t % 2, 0, D), m.xT[:, c, t * P:(t + 1) * P],
                                         wqkv[:, c, 2 * D:3 * D], start=(c == 0), stop=(c == KC - 1))
                    last.then_inc(s.v_mm, 1)

            @block.scalar
            def _(act):
                for g in range(NG):
                    c = g % KC
                    act.wait_ge(s.gate_mm, g + 1)
                    act.activation(gate[:, g, :], bank(m.ps, 2 + g % 2), ACT.Tanh, scale=0.5,
                                   bias=hbgate[:, c:c + 1]).then_inc(s.gate_read, 1)
                    for j in (2 * g, 2 * g + 1):
                        act.wait_ge(s.min_ready, j + 1)
                        act.activation(neg[:, j, :], neg[:, j, :], ACT.Exp).then_inc(s.exp_ready, 1)

            @block.vector
            def _(dve):
                for g in range(NG):
                    n, c = divmod(g, KC)
                    cols = slice(n * HALF, (n + 1) * HALF)
                    dve.wait_ge(s.gate_read, g + 1)
                    dve.tensor_scalar(gate[:, g, :], gate[:, g, :], 0.5, 0.5, ALU.mult, ALU.add).then_inc(s.half_gate, 1)
                    dve.wait_ge(s.half_gate, g + 1)
                    dve.wait_ge(s.qk_mm, 2 * g + 1)
                    dve.scalar_tensor_tensor(kg[:, g, :], bank(m.ps, 4 + g % 2), bqkv[:, 2 + c:3 + c], gate[:, g, :],
                                             ALU.add, ALU.mult).then_inc(s.k_gated, 1)
                    dve.wait_ge(s.k_gated, g + 1)
                    dve.tensor_scalar(neg[:, 2 * g, :], kg[:, g, :], 0.0, None, ALU.min).then_inc(s.min_ready, 1)
                    dve.tensor_scalar(kT[:, c, cols], kg[:, g, :], 0.0, None, ALU.max).then_inc(s.relu_ready, 1)
                    dve.wait_ge(s.qk_mm, 2 * g + 2)
                    q = bank(m.ps, 6 + g % 2)
                    dve.tensor_scalar(neg[:, 2 * g + 1, :], q, bqkv[:, c:c + 1], 0.0, ALU.add, ALU.min).then_inc(s.min_ready, 1)
                    dve.tensor_scalar(qT[:, c, cols], q, bqkv[:, c:c + 1], 0.0, ALU.add, ALU.max).then_inc(s.relu_ready, 1)
                for t in range(NT):
                    dve.wait_ge(s.v_mm, t + 1)
                    dve.tensor_tensor(v[:, t, 0:D], bank(m.ps, t % 2, 0, D), bv[:, :], ALU.add).then_inc(s.v_read, 1)

        with ExitStack() as own, nc.Block() as block:
            give_y(nc, own, m)
            s = s2

            @block.gpsimd
            def _(pool):
                clear(pool, s1)
                for k in range(NT):
                    pool.wait_ge(s.score_copied, k + 1)
                    diag = AT[:, k, k * P:(k + 1) * P]
                    pool.affine_select(out=diag, in_=diag, compare_op=ALU.is_ge, fill=0.0, base=0, pattern=[[1, P]],
                                       channel_multiplier=-1).then_inc(s.masked, 1)

            @block.tensor
            def _(pe):
                for k in range(NT + 1):
                    if k < NT:
                        if k >= 2:
                            pe.wait_ge(s.score_copied, k - 1)
                        for lo, hi in halves(k * P, T):
                            for c in range(KC):
                                last = pe.matmul(bank(m.ps, 2 * (k % 2), lo, hi), kT[:, c, k * P:(k + 1) * P],
                                                 qT[:, c, lo:hi], start=(c == 0), stop=(c == KC - 1))
                        last.then_inc(s.score_mm, 1)
                    if k >= 1:
                        t = k - 1
                        pe.wait_ge(s.masked, t + 1)
                        if t >= 2:
                            pe.wait_ge(s.y_ready, t - 1)
                        for k2 in range(t + 1):
                            last = pe.matmul(bank(m.ps, 4 + t % 2, 0, D + 2), AT[:, k2, t * P:(t + 1) * P], v[:, k2, :],
                                             start=(k2 == 0), stop=(k2 == t))
                        last.then_inc(s.out_mm, 1)

            @block.scalar
            def _(act):
                for k in range(NT):
                    act.wait_ge(s.score_mm, k + 1)
                    act.copy(AT[:, k, k * P:T], bank(m.ps, 2 * (k % 2), k * P, T)).then_inc(s.score_copied, 1)

            @block.vector
            def _(dve):
                for t in range(NT):
                    dve.wait_ge(s.out_mm, t + 1)
                    dve.tensor_scalar(den[:, t, 0:1], bank(m.ps, 4 + t % 2, D, D + 1), DEN_EPS, None, ALU.add).then_inc(s.den, 1)
                    dve.wait_ge(s.den, t + 1)
                    dve.reciprocal(den[:, t, 1:2], den[:, t, 0:1]).then_inc(s.rden, 1)
                    dve.wait_ge(s.rden, t + 1)
                    dve.scalar_tensor_tensor(m.y[:, t, :], bank(m.ps, 4 + t % 2, 0, D), den[:, t, 1:2], m.x[:, t, :],
                                             ALU.mult, ALU.add).then_inc(s.y_ready, 1)

            @block.sync
            def _(sp):
                store_y(sp, m, s, dst[b])


def store_y(sp, m, s, dst):
    for t in range(0, NT, 2):
        sp.wait_ge(s.y_ready, t + 2)
        sp.dma_start(dst[:, t:t + 2, :], m.y[:, t:t + 2, :]).then_inc(s.y_out, 16)
    sp.wait_ge(s.y_out, 16 * NT // 2)



GATES2 = ("logits exp_in exp_out chain gm_ready hilo gmT_mm gmT_ready value_mm value_masked v_ready")
ATTN2 = ("k_mm k_hi k_ready q_mm q_hi q_ready max_mm max_read shift_ready score_mm exp_ready pv_mm "
         "rden o_ready")
OUT2 = "sel_ready even_oe_in odd_oe_in mask_mm routed out_mm y_ready y_out"
CLAMP = 80.0


def layer2(nc, ctx, m, I, src, dst):
    sb = lambda name, shape, dt=F32: ctx.enter_context(nc.sbuf_tensor("l2_" + name, shape, dt))
    wq, wk, wg = sb("wq", [P, KC, H0 * P]), sb("wk", [P, KC, H0 * P]), sb("wg", [P, KC, H0 * NE])
    ve = sb("ve", [P, KC, H0, NE * DH0])
    prio = sb("prio", [P, NE])
    klo = sb("klo", [P, 1])
    pick = sb("pick", [P, H0 * NE])
    vx = sb("vx", [P, NT, H0, P])
    oT = sb("oT", [P, H0 // 2, T])
    gmT = sb("gmT", [P, T], F32R)
    vcol = lambda h: slice(DH0 * (h % 2), DH0 * (h % 2) + DH0)
    ones = lambda h: slice(DH0 * (1 - h % 2), DH0 * (1 - h % 2) + DH0)
    ld = signals(nc, ctx, "l2_load", "weights ones")
    s0 = signals(nc, ctx, "l2_norm", NORM)
    s1 = signals(nc, ctx, "l2_gates", GATES2)
    s2 = signals(nc, ctx, "l2_attn", ATTN2)
    s3 = signals(nc, ctx, "l2_out", OUT2)

    with nc.Block() as block:
        @block.sync
        def _(sp):
            pairs = [(wq, "wq2"), (wk, "wk2"), (wg, "wg2"), (ve, "ve2"), (prio, "prio"), (klo, "klo"), (pick, "pick")]
            for tile, name in pairs:
                sp.dma_start(tile[:], I[name]).then_inc(ld.weights, 16)
            sp.wait_ge(ld.weights, 16 * len(pairs))

        @block.vector
        def _(dve):
            dve.memset(vx[:, :, :, :], 1.0).then_inc(ld.ones, 1)

    def gates_and_values(own):
        sb = lambda name, shape, dt=F32: own.enter_context(nc.sbuf_tensor("l2a_" + name, shape, dt))
        N = NT * H0 * NE
        z, e, g, first = sb("z", [P, N]), sb("e", [P, N]), sb("g", [P, N]), sb("first", [P, N])
        gm, gm_hi, hilo = sb("gm", [P, N]), sb("gm_hi", [P, N], F32R), sb("hilo", [P, NT, 2, H0 * NE])
        top, win = sb("top", [P, NT * H0]), sb("win", [P, NT * H0])
        VM = 4
        vm = sb("vm", [P, VM, NE * DH0])
        RING = 6
        by_head = lambda x: x[:, :].rearrange("p (n e) -> p n e", e=NE)
        s = s1
        with nc.Block() as block:
            @block.gpsimd
            def _(pool):
                clear(pool, s0)

            @block.tensor
            def _(pe):
                for t in range(NT):
                    for c in range(KC):
                        last = pe.matmul(bank(m.ps, 7, t * 64, t * 64 + 64), m.xT[:, c, t * P:(t + 1) * P], wg[:, c, :],
                                         start=(c == 0), stop=(c == KC - 1))
                last.then_inc(s.logits, 1)
                for t in range(NT):
                    for h in range(H0):
                        n = t * H0 + h
                        if n >= RING:
                            pe.wait_ge(s.value_masked, n - RING + 1)
                        for c in range(KC):
                            last = pe.matmul(bank(m.ps, n % RING), m.xT[:, c, t * P:(t + 1) * P], ve[:, c, h, :],
                                             start=(c == 0), stop=(c == KC - 1))
                        last.then_inc(s.value_mm, 1)
                    if t == 1:
                        pe.wait_ge(s.hilo, 2)
                        for t2 in range(NT):
                            at = t2 * P
                            last = pe.transpose(bank(m.ps, 6, at, at + P), hilo[:, t2, :, :].rearrange("p a b -> p (a b)"),
                                                m.ident[:, :])
                            if t2 % 4 == 3:
                                last.then_inc(s.gmT_mm, 1)

            @block.scalar
            def _(act):
                act.wait_ge(s.exp_in, 1)
                act.activation(e[:, :], z[:, :], ACT.Exp).then_inc(s.exp_out, 1)
                for n in range(NH):
                    act.wait_ge(s.gmT_mm, n + 1)
                    act.copy(gmT[:, n * HALF:(n + 1) * HALF], bank(m.ps, 6 + n)).then_inc(s.gmT_ready, 1)

            @block.vector
            def _(dve):
                step = Chain(dve, s.chain)
                every = lambda x: x[:, :].unsqueeze(2).to_broadcast([P, NT * H0, NE])
                dve.wait_ge(s.logits, 1)
                dve.tensor_scalar(z[:, :], bank(m.ps, 7), -1.0, CLAMP, ALU.mult, ALU.min).then_inc(s.exp_in, 1)
                dve.wait_ge(s.exp_out, 1)
                step(dve.tensor_scalar(g[:, :], e[:, :], 1.0, None, ALU.add))
                step(dve.reciprocal(g[:, :], g[:, :]))
                step(dve.tensor_reduce(top[:, :], by_head(g), AX_X, ALU.max))
                step(dve.tensor_tensor(by_head(first), by_head(g), every(top), ALU.is_equal))
                step(dve.tensor_tensor(by_head(first), by_head(first),
                                       prio[:, :].unsqueeze(1).to_broadcast([P, NT * H0, NE]), ALU.mult))
                step(dve.tensor_reduce(win[:, :], by_head(first), AX_X, ALU.max))
                step(dve.tensor_tensor(by_head(first), by_head(first), every(win), ALU.is_equal))
                dve.tensor_tensor(gm[:, :], first[:, :], g[:, :], ALU.mult).then_inc(s.gm_ready, 1)
                dve.wait_ge(s.gm_ready, 1)
                step(dve.tensor_copy(gm_hi[:, :], gm[:, :]))
                tiles = lambda x: x.rearrange("p (t n) -> p t n", t=NT)
                dve.tensor_copy(hilo[:, :, 0, :], tiles(gm_hi[:, :].bitcast(F32))).then_inc(s.hilo, 1)
                dve.tensor_tensor(hilo[:, :, 1, :], tiles(gm[:, :]), tiles(gm_hi[:, :].bitcast(F32)),
                                  ALU.subtract).then_inc(s.hilo, 1)
                for t in range(NT):
                    for h in range(H0):
                        n = t * H0 + h
                        dve.wait_ge(s.value_mm, n + 1)
                        if n >= VM:
                            dve.wait_ge(s.v_ready, n - VM + 1)
                        mask = gm[:, n * NE:(n + 1) * NE].unsqueeze(2).to_broadcast([P, NE, DH0])
                        dve.tensor_tensor(vm[:, n % VM, :].rearrange("p (e k) -> p e k", e=NE),
                                          bank(m.ps, n % RING).rearrange("p (e k) -> p e k", e=NE), mask,
                                          ALU.mult).then_inc(s.value_masked, 1)
                        dve.wait_ge(s.value_masked, n + 1)
                        dve.tensor_reduce(vx[:, t, h, vcol(h)], vm[:, n % VM, :].rearrange("p (e k) -> p k e", e=NE),
                                          AX_X, ALU.add).then_inc(s.v_ready, 1)

    def attention(own):
        sb = lambda name, shape, dt=F32: own.enter_context(nc.sbuf_tensor("l2b_" + name, shape, dt))
        RK = 3
        kst, qst, qlo = (sb(n, [P, RK, T], F32R) for n in ("kst", "qst", "qlo"))
        shift = sb("shift", [P, 2, T], F32R)
        hi = sb("hi", [P, NH, HALF], F32R)
        prob = sb("prob", [P, 2, T])
        mx = sb("mx", [P, H0, NT])
        rden = sb("rden", [P, T])
        s = s2
        with nc.Block() as block:
            @block.tensor
            def _(pe):
                def project(h, w, n, mm):
                    for c in range(KC):
                        last = pe.matmul(bank(m.ps, 6 + n), w[:, c, h * P:(h + 1) * P], m.xT[:, c, n * HALF:(n + 1) * HALF],
                                         start=(c == 0), stop=(c == KC - 1))
                    last.then_inc(mm, 1)

                def maxima(h, t):
                    if t == 0:
                        pe.wait_ge(s.k_ready, 2 * h + 2)
                        pe.wait_ge(s.q_ready, 2 * h + 2)
                    if h + t:
                        pe.wait_ge(s.max_read, NT * h + t)
                    for lo, hi_ in halves(0, (t + 1) * P):
                        last = pe.matmul(bank(m.ps, 2, lo, hi_), qst[:, h % RK, t * P:(t + 1) * P], kst[:, h % RK, lo:hi_],
                                         start=True, stop=True)
                    last = pe.matmul(bank(m.ps, 2, t * P, (t + 1) * P), m.ident16[:, :], m.mask_qk[:, :],
                                     start=False, stop=True, skip_group_check=True)
                    last.then_inc(s.max_mm, 1)

                def scores(h, k):
                    if k == 0:
                        pe.wait_ge(s.shift_ready, h + 1)
                    if h + k:
                        pe.wait_ge(s.exp_ready, NT * h + k)
                    for lo, hi_ in halves(k * P, T):
                        out, keys = bank(m.ps, 0, lo, hi_), kst[:, h % RK, k * P:(k + 1) * P]
                        pe.matmul(out, keys, qst[:, h % RK, lo:hi_], start=True, stop=False)
                        pe.matmul(out, keys, qlo[:, h % RK, lo:hi_], start=False, stop=False)
                        if lo == k * P:
                            pe.matmul(bank(m.ps, 0, lo, lo + P), m.ident16[:, :], m.mask_kq[:, :], start=False, stop=False)
                        last = pe.matmul(out, m.negones[:, :], shift[:, h % 2, lo:hi_], start=False, stop=True)
                    last.then_inc(s.score_mm, 1)

                def weighted(h, k):
                    pe.wait_ge(s.exp_ready, NT * h + k + 1)
                    if k == 0 and h:
                        pe.wait_ge(s.o_ready, h)
                    for lo, hi_ in halves(k * P, T):
                        last = pe.matmul(bank(m.ps, 4, lo, hi_), vx[:, k, h, :], prob[:, k % 2, lo:hi_], start=(k == 0),
                                         stop=True, skip_group_check=True)
                    last.then_inc(s.pv_mm, 1)

                for step in range(H0 + 2):
                    h0, h1, h2 = step, step - 1, step - 2
                    for k in range(NT):
                        if h2 >= 0:
                            scores(h2, k)
                        if h0 < H0 and k in (0, 1):
                            if h0:
                                pe.wait_ge(s.q_ready, 2 * (h0 - 1) + k + 1)
                            project(h0, wk, k, s.k_mm)
                        if h0 < H0 and k in (3, 4):
                            pe.wait_ge(s.k_ready, 2 * h0 + k - 3 + 1)
                            project(h0, wq, k - 3, s.q_mm)
                        if 0 <= h1 < H0:
                            maxima(h1, k)
                        if h2 >= 0 and k >= 1:
                            weighted(h2, k - 1)
                    if h2 >= 0:
                        weighted(h2, NT - 1)

            @block.scalar
            def _(act):
                def k_hi(h, n):
                    act.wait_ge(s.k_mm, 2 * h + n + 1)
                    if h:
                        act.wait_ge(s.k_ready, 2 * (h - 1) + n + 1)
                    act.copy(hi[:, n, :], bank(m.ps, 6 + n)).then_inc(s.k_hi, 1)

                def q_hi(h, n):
                    act.wait_ge(s.q_mm, 2 * h + n + 1)
                    if h >= RK:
                        act.wait_ge(s.score_mm, NT * (h - RK + 1))
                    act.copy(qst[:, h % RK, n * HALF:(n + 1) * HALF], bank(m.ps, 6 + n)).then_inc(s.q_hi, 1)

                for step in range(H0 + 2):
                    h0, h2 = step, step - 2
                    for k in range(NT):
                        if h2 >= 0:
                            act.wait_ge(s.score_mm, NT * h2 + k + 1)
                            if NT * h2 + k >= 2:
                                act.wait_ge(s.pv_mm, NT * h2 + k - 1)
                            act.activation(prob[:, k % 2, k * P:T], bank(m.ps, 0, k * P, T), ACT.Exp,
                                           scale=SCALE0).then_inc(s.exp_ready, 1)
                        if h0 < H0 and k in (0, 1):
                            k_hi(h0, k)
                        if h0 < H0 and k in (3, 4):
                            q_hi(h0, k - 3)

            @block.vector
            def _(dve):
                for step in range(H0 + 2):
                    h0, h1, h2 = step, step - 1, step - 2
                    for k in range(NT):
                        if h0 < H0 and k in (0, 1):
                            cols = slice(k * HALF, (k + 1) * HALF)
                            dve.wait_ge(s.k_hi, 2 * h0 + k + 1)
                            if h0 >= RK:
                                dve.wait_ge(s.score_mm, NT * (h0 - RK + 1))
                            dve.scalar_tensor_tensor(kst[:, h0 % RK, cols], hi[:, k, :].bitcast(F32), klo[:, 0:1],
                                                     bank(m.ps, 6 + k), ALU.mult, ALU.add).then_inc(s.k_ready, 1)
                        if h0 < H0 and k in (3, 4):
                            n = k - 3
                            cols = slice(n * HALF, (n + 1) * HALF)
                            dve.wait_ge(s.q_hi, 2 * h0 + n + 1)
                            dve.tensor_tensor(qlo[:, h0 % RK, cols], bank(m.ps, 6 + n),
                                              qst[:, h0 % RK, cols].bitcast(F32), ALU.subtract).then_inc(s.q_ready, 1)
                        if 0 <= h1 < H0:
                            dve.wait_ge(s.max_mm, NT * h1 + k + 1)
                            dve.reduce_max(mx[:, h1, k:k + 1], bank(m.ps, 2, 0, (k + 1) * P), AX_X).then_inc(s.max_read, 1)
                    if h2 >= 0:
                        num, den = vcol(h2), ones(h2)
                        dve.wait_ge(s.pv_mm, NT * h2 + NT)
                        dve.reciprocal(rden[num, :], bank(m.ps, 4, 0, T, den)).then_inc(s.rden, 1)
                        dve.wait_ge(s.rden, h2 + 1)
                        dve.tensor_tensor(oT[num, h2 // 2, :], bank(m.ps, 4, 0, T, num), rden[num, :],
                                          ALU.mult).then_inc(s.o_ready, 1)

            @block.gpsimd
            def _(pool):
                clear(pool, s1)
                for h in range(H0):
                    pool.wait_ge(s.max_read, NT * (h + 1))
                    if h >= 2:
                        pool.wait_ge(s.score_mm, NT * (h - 1))
                    pool.tensor_tensor(shift[:, h % 2, :].rearrange("p (t q) -> p t q", t=NT),
                                       m.ident[:, :].unsqueeze(1).to_broadcast([P, NT, P]),
                                       mx[:, h, :].unsqueeze(2).to_broadcast([P, NT, P]), ALU.mult).then_inc(s.shift_ready, 1)

    def output_experts(own, b):
        sb = lambda name, shape, dt=F32: own.enter_context(nc.sbuf_tensor("l2c_" + name, shape, dt))
        sel = sb("sel", [P, H0 // 2 * NE, P], F32R)
        oe = sb("oe", [P, 2, NE, D])
        RT = 4
        routed = sb("routed", [P, RT, HALF])
        AHEAD = 2
        blocks = [(c, e, n) for c in range(H0 // 2) for e in range(NE) for n in range(NH)]
        per_c = NE * NH
        s = s3
        with nc.Block() as block:
            @block.sync
            def _(sp):
                for c in range(H0 // 2):
                    if c >= 2:
                        sp.wait_ge(s.out_mm, per_c * (c - 1))
                    sp.dma_start(oe[:, c % 2, :, :], I["oe2"][:, c]).then_inc((s.even_oe_in, s.odd_oe_in)[c % 2], 16)
                store_y(sp, m, s, dst[b])

            @block.gpsimd
            def _(pool):
                clear(pool, s2)

            @block.vector
            def _(dve):
                for c in range(H0 // 2):
                    cols = slice(c * NE * 2, (c + 1) * NE * 2)
                    dve.tensor_copy(sel[:, c * NE:(c + 1) * NE, :].rearrange("p n (a k) -> p (n a) k", a=2),
                                    pick[:, cols].unsqueeze(2).to_broadcast([P, NE * 2, DH0])).then_inc(s.sel_ready, 1)
                for i, (c, e, n) in enumerate(blocks):
                    dve.wait_ge(s.mask_mm, i + 1)
                    if i >= RT:
                        dve.wait_ge(s.out_mm, i - RT + 1)
                    dve.tensor_tensor(routed[:, i % RT, :], oT[:, c, n * HALF:(n + 1) * HALF], bank(m.ps, 4 + i % 4),
                                      ALU.mult).then_inc(s.routed, 1)
                dve.wait_ge(s.out_mm, len(blocks))
                for t in range(NT):
                    dve.tensor_tensor(m.y[:, t, :], m.x[:, t, :], m.ps[:, t * D:(t + 1) * D], ALU.add).then_inc(s.y_ready, 1)

            @block.tensor
            def _(pe):
                for i in range(len(blocks) + AHEAD):
                    if i < len(blocks):
                        c, e, n = blocks[i]
                        pe.wait_ge(s.sel_ready, c + 1)
                        if i >= 4:
                            pe.wait_ge(s.routed, i - 3)
                        pe.matmul(bank(m.ps, 4 + i % 4), sel[:, c * NE + e, :], gmT[:, n * HALF:(n + 1) * HALF],
                                  start=True, stop=True).then_inc(s.mask_mm, 1)
                    if i >= AHEAD:
                        c, e, n = blocks[i - AHEAD]
                        pe.wait_ge((s.even_oe_in, s.odd_oe_in)[c % 2], 16 * (c // 2 + 1))
                        pe.wait_ge(s.routed, i - AHEAD + 1)
                        for j in range(HALF // P):
                            t = n * (HALF // P) + j
                            last = pe.matmul(m.ps[:, t * D:(t + 1) * D], routed[:, (i - AHEAD) % RT, j * P:(j + 1) * P],
                                             oe[:, c % 2, e, :], start=(c == e == 0 and t % 2 == 0),
                                             stop=(c == H0 // 2 - 1 and e == NE - 1), skip_group_check=True)
                        last.then_inc(s.out_mm, 1)

    with nc.Fori(0, SEQS) as b:
        norm_stage(nc, m, s0, s3, src[b])
        with ExitStack() as own:
            gates_and_values(own)
        with ExitStack() as own:
            attention(own)
        with ExitStack() as own:
            give_y(nc, own, m)
            output_experts(own, b)



PROJ3 = ("qk_mm z_ready z_hi stack_ready h_mm v_mm v_read chain var_ready sd_ready hn_ready gelu_ready drift_ready "
         "g_ready g_gelu gate_in gate_ready vx_ready")
ATTN3 = "max_mm max_read shift_ready score_mm exp_ready pv_mm o_read"
OUT3 = "den_mm rden o_ready out_mm y_ready y_out"


def layer3(nc, ctx, m, I, src, dst):
    sb = lambda name, shape, dt=F32: ctx.enter_context(nc.sbuf_tensor("l3_" + name, shape, dt))
    GROUPS = H1 // G1
    R = 4 * DH1
    HPC = P // R
    QC = H1 // HPC
    HF = 128
    GF = 16
    wq, wk, wv, wo = sb("wq", [P, KC, QC * P]), sb("wk", [P, KC, QC * P]), sb("wv", [P, KC, D]), sb("wo", [P, GROUPS, D])
    bq, bk, bv, bo = sb("bq", [P, QC]), sb("bk", [P, QC]), sb("bv", [P, D]), sb("bo", [P, D])
    w1 = sb("w1", [P, KC, HF])
    hv = sb("hv", [P, 4, HF])
    gv = sb("gv", [P, 3, GF])
    b2 = sb("b2", [P, 2])
    qneg, kneg = sb("qneg", [P, 1]), sb("kneg", [P, 1])
    den_of = sb("den_of", [P, P])
    qst, kst = sb("qst", [P, QC, T], F32R), sb("kst", [P, QC, T], F32R)
    vx = sb("vx", [P, NT, H1, 2 * DH1])
    ld = signals(nc, ctx, "l3_load", "weights ones")
    s0 = signals(nc, ctx, "l3_norm", NORM)
    s1 = signals(nc, ctx, "l3_proj", PROJ3)
    s2 = signals(nc, ctx, "l3_attn", ATTN3)
    s3 = signals(nc, ctx, "l3_out", OUT3)

    with nc.Block() as block:
        @block.sync
        def _(sp):
            pairs = [(wq, "wq3"), (wk, "wk3"), (wv, "wv3"), (wo, "wo3"), (bq, "bq3"), (bk, "bk3"), (bv, "bv3"), (bo, "bo3"),
                     (w1, "w13"), (hv, "hv3"), (gv, "gv3"), (b2, "b23"), (qneg, "qneg3"), (kneg, "kneg3"), (den_of, "den_of")]
            for tile, name in pairs:
                sp.dma_start(tile[:], I[name]).then_inc(ld.weights, 16)
            sp.wait_ge(ld.weights, 16 * len(pairs))

        @block.vector
        def _(dve):
            dve.memset(vx[:, :, :, :], 1.0).then_inc(ld.ones, 1)

    def projections(own):
        sb = lambda name, shape, dt=F32: own.enter_context(nc.sbuf_tensor("l3a_" + name, shape, dt))
        RZ = 4
        z, zhi = sb("z", [P, RZ, HALF]), sb("zhi", [P, RZ, HALF], F32R)
        v = sb("v", [P, NT, D])
        h = sb("h", [P, NT, HF])
        g = sb("g", [P, NT, GF])
        st, mom, sd, r = sb("st", [P, NT, 6]), sb("mom", [P, NT, 2]), sb("sd", [P, NT]), sb("r", [P, NT])
        drift, gate = sb("drift", [P, NT]), sb("gate", [P, NT])
        items = [(c, n, kind) for c in range(QC) for n in range(NH) for kind in "qk"]
        s = s1
        with nc.Block() as block:
            @block.tensor
            def _(pe):
                for t in range(NT):
                    for c in range(KC):
                        last = pe.matmul(bank(m.ps, 4, t * HF, (t + 1) * HF), m.xT[:, c, t * P:(t + 1) * P], w1[:, c, :],
                                         start=(c == 0), stop=(c == KC - 1))
                    last.then_inc(s.h_mm, 1)
                for t in range(NT):
                    if t >= 2:
                        pe.wait_ge(s.v_read, t - 1)
                    for c in range(KC):
                        last = pe.matmul(bank(m.ps, 6 + t % 2, 0, D), m.xT[:, c, t * P:(t + 1) * P], wv[:, c, :],
                                         start=(c == 0), stop=(c == KC - 1))
                    last.then_inc(s.v_mm, 1)
                for i, (q, n, kind) in enumerate(items):
                    if i >= 4:
                        pe.wait_ge(s.z_ready, i - 3)
                    w = wq if kind == "q" else wk
                    for c in range(KC):
                        last = pe.matmul(bank(m.ps, i % 4), w[:, c, q * P:(q + 1) * P], m.xT[:, c, n * HALF:(n + 1) * HALF],
                                         start=(c == 0), stop=(c == KC - 1))
                    last.then_inc(s.qk_mm, 1)

            @block.scalar
            def _(act):
                act.wait_ge(s.var_ready, NT)
                act.activation(sd[:, :], mom[:, :, 1], ACT.Sqrt, bias=m.eps[:, 0:1]).then_inc(s.sd_ready, 1)
                act.wait_ge(s.hn_ready, 1)
                act.activation(h[:, :, :], h[:, :, :], ACT.Gelu).then_inc(s.gelu_ready, 1)
                act.wait_ge(s.g_ready, 1)
                act.activation(g[:, :, :], g[:, :, :], ACT.Gelu).then_inc(s.g_gelu, 1)
                act.wait_ge(s.gate_in, 1)
                act.activation(gate[:, :], drift[:, :], ACT.Tanh, bias=b2[:, 1:2]).then_inc(s.gate_ready, 1)
                for i, (q, n, kind) in enumerate(items):
                    act.wait_ge(s.qk_mm, i + 1)
                    if i >= RZ:
                        act.wait_ge(s.stack_ready, i - RZ + 1)
                    act.activation(z[:, i % RZ, :], bank(m.ps, i % 4), ACT.Identity,
                                   bias=(bq if kind == "q" else bk)[:, q:q + 1]).then_inc(s.z_ready, 1)

            @block.gpsimd
            def _(pool):
                clear(pool, s0)
                for i in range(len(items)):
                    pool.wait_ge(s.z_ready, i + 1)
                    if i >= RZ:
                        pool.wait_ge(s.stack_ready, i - RZ + 1)
                    pool.tensor_copy(zhi[:, i % RZ, :], z[:, i % RZ, :]).then_inc(s.z_hi, 1)

            @block.vector
            def _(dve):
                step = Chain(dve, s.chain)
                over_t = lambda row, w: row.unsqueeze(1).to_broadcast([P, NT, w])
                over_f = lambda col, w: col.unsqueeze(2).to_broadcast([P, NT, w])
                dve.wait_ge(s.h_mm, NT)
                step(dve.tensor_tensor(h[:, :, :], bank(m.ps, 4, 0, NT * HF).rearrange("p (t f) -> p t f", t=NT),
                                       over_t(hv[:, 0, :], HF), ALU.add))
                for t in range(NT):
                    last = dve.bn_stats(st[:, t, :], h[:, t, :])
                step(last)
                for t in range(NT):
                    dve.bn_aggr(mom[:, t, :], st[:, t, :]).then_inc(s.var_ready, 1)
                dve.wait_ge(s.sd_ready, 1)
                inverse_sd(step, dve, m, r, mom[:, :, 1], sd)
                step(dve.tensor_tensor(h[:, :, :], h[:, :, :], over_f(mom[:, :, 0], HF), ALU.subtract))
                step(dve.tensor_tensor(h[:, :, :], h[:, :, :], over_f(r[:, :], HF), ALU.mult))
                step(dve.tensor_tensor(h[:, :, :], h[:, :, :], over_t(hv[:, 1, :], HF), ALU.mult))
                dve.tensor_tensor(h[:, :, :], h[:, :, :], over_t(hv[:, 2, :], HF), ALU.add).then_inc(s.hn_ready, 1)
                for t in range(NT):
                    dve.wait_ge(s.v_mm, t + 1)
                    dve.tensor_tensor(v[:, t, :], bank(m.ps, 6 + t % 2, 0, D), bv[:, :], ALU.add).then_inc(s.v_read, 1)
                dve.wait_ge(s.gelu_ready, 1)
                step(dve.tensor_tensor(h[:, :, :], h[:, :, :], over_t(hv[:, 3, :], HF), ALU.mult))
                step(dve.tensor_reduce(drift[:, :], h[:, :, :], AX_X, ALU.add))
                step(dve.tensor_scalar(drift[:, :], drift[:, :], b2[:, 0:1], None, ALU.add))
                step(dve.tensor_tensor(g[:, :, :], over_f(drift[:, :], GF), over_t(gv[:, 0, :], GF), ALU.mult))
                dve.tensor_tensor(g[:, :, :], g[:, :, :], over_t(gv[:, 1, :], GF), ALU.add).then_inc(s.g_ready, 1)
                dve.wait_ge(s.g_gelu, 1)
                step(dve.tensor_tensor(g[:, :, :], g[:, :, :], over_t(gv[:, 2, :], GF), ALU.mult))
                dve.tensor_reduce(drift[:, :], g[:, :, :], AX_X, ALU.add).then_inc(s.gate_in, 1)
                dve.wait_ge(s.gate_ready, 1)
                dve.wait_ge(s.v_read, NT)
                for t in range(NT):
                    dve.tensor_scalar(vx[:, t, :, 0:DH1], v[:, t, :].rearrange("p (h k) -> p h k", h=H1), gate[:, t:t + 1],
                                      None, ALU.mult).then_inc(s.vx_ready, 1)
                for i, (q, n, kind) in enumerate(items):
                    dve.wait_ge(s.z_hi, i + 1)
                    dve.scalar_tensor_tensor((qst if kind == "q" else kst)[:, q, n * HALF:(n + 1) * HALF],
                                             zhi[:, i % RZ, :].bitcast(F32), (qneg if kind == "q" else kneg)[:, 0:1],
                                             z[:, i % RZ, :], ALU.mult, ALU.add).then_inc(s.stack_ready, 1)

    def attention(own, oraw):
        sb = lambda name, shape, dt=F32: own.enter_context(nc.sbuf_tensor("l3b_" + name, shape, dt))
        shift = sb("shift", [P, 2, G1, T], F32R)
        prob = sb("prob", [P, 2, G1, T])
        mx = sb("mx", [P, H1, NT])
        s = s2

        def rows(h):
            return slice(R * (h % HPC), R * (h % HPC) + R)

        order = [(g, k, i) for g in range(GROUPS) for k in range(NT) for i in range(G1)]
        with nc.Block() as block:
            @block.tensor
            def _(pe):
                def maxima(g, k, i, n):
                    h, rr = G1 * g + i, rows(G1 * g + i)
                    if n:
                        pe.wait_ge(s.max_read, n)
                    for lo, hi in halves(0, (k + 1) * P):
                        pe.matmul(bank(m.ps, 6, lo, hi), qst[rr, h // HPC, k * P:(k + 1) * P], kst[rr, h // HPC, lo:hi],
                                  start=True, stop=True)
                    pe.matmul(bank(m.ps, 6, k * P, (k + 1) * P), m.ident16[:, :], m.mask_qk[:, :], start=False, stop=True,
                              skip_group_check=True).then_inc(s.max_mm, 1)

                def scores(g, k, i, n):
                    h, rr = G1 * g + i, rows(G1 * g + i)
                    if n >= 2:
                        pe.wait_ge(s.exp_ready, n - 1)
                    if k == 0:
                        pe.wait_ge(s.shift_ready, G1 * NT * (g + 1))
                    for lo, hi in halves(k * P, T):
                        out = bank(m.ps, 2 + 2 * (n % 2), lo, hi)
                        pe.matmul(out, kst[rr, h // HPC, k * P:(k + 1) * P], qst[rr, h // HPC, lo:hi], start=True, stop=False)
                        if lo == k * P:
                            pe.matmul(bank(m.ps, 2 + 2 * (n % 2), lo, lo + P), m.ident16[:, :], m.mask_kq[:, :],
                                      start=False, stop=False)
                        last = pe.matmul(out, m.negones[:, :], shift[:, g % 2, i, lo:hi], start=False, stop=True)
                    last.then_inc(s.score_mm, 1)

                def weighted(g, k):
                    pe.wait_ge(s.exp_ready, G1 * (NT * g + k + 1))
                    if k == 0 and g:
                        pe.wait_ge(s.o_read, g)
                    for lo, hi in halves(k * P, T):
                        for i in range(G1):
                            last = pe.matmul(bank(m.ps, 0, lo, hi, slice(32 * i, 32 * i + 32)), vx[:, k, G1 * g + i, :],
                                             prob[:, k % 2, i, lo:hi], start=(k == 0), stop=True, skip_group_check=True)
                    last.then_inc(s.pv_mm, 1)

                for g in range(GROUPS + 1):
                    for k in range(NT):
                        for i in range(G1):
                            if g >= 1:
                                scores(g - 1, k, i, G1 * (NT * (g - 1) + k) + i)
                            if g < GROUPS:
                                maxima(g, k, i, G1 * (NT * g + k) + i)
                            if g >= 1 and k >= 1 and i == 1:
                                weighted(g - 1, k - 1)
                    if g >= 1:
                        weighted(g - 1, NT - 1)

            @block.scalar
            def _(act):
                for n, (g, k, i) in enumerate(order):
                    act.wait_ge(s.score_mm, n + 1)
                    if i == 0 and NT * g + k >= 2:
                        act.wait_ge(s.pv_mm, NT * g + k - 1)
                    act.activation(prob[:, k % 2, i, k * P:T], bank(m.ps, 2 + 2 * (n % 2), k * P, T), ACT.Exp,
                                   scale=SCALE1).then_inc(s.exp_ready, 1)

            @block.vector
            def _(dve):
                def group_out(g):
                    dve.wait_ge(s.pv_mm, NT * (g + 1))
                    dve.tensor_copy(oraw[:, g, :], bank(m.ps, 0, 0, T)).then_inc(s.o_read, 1)

                for n, (g, k, i) in enumerate(order):
                    dve.wait_ge(s.max_mm, n + 1)
                    dve.reduce_max(mx[:, G1 * g + i, k:k + 1], bank(m.ps, 6, 0, (k + 1) * P), AX_X).then_inc(s.max_read, 1)
                    if g >= 2 and k == 0 and i == 0:
                        group_out(g - 2)
                for g in range(GROUPS - 2, GROUPS):
                    group_out(g)

            @block.gpsimd
            def _(pool):
                clear(pool, s1)
                for n, (g, k, i) in enumerate(order):
                    pool.wait_ge(s.max_read, n + 1)
                    if g >= 2 and k == 0 and i == 0:
                        pool.wait_ge(s.score_mm, G1 * NT * (g - 1))
                    pool.tensor_scalar(shift[:, g % 2, i, k * P:(k + 1) * P], m.ident[:, :], mx[:, G1 * g + i, k:k + 1],
                                       None, ALU.mult).then_inc(s.shift_ready, 1)

    def output(own, oraw, b):
        sb = lambda name, shape, dt=F32: own.enter_context(nc.sbuf_tensor("l3c_" + name, shape, dt))
        rden = sb("rden", [P, GROUPS * NH, HALF])
        o = sb("o", [P, GROUPS, T])
        items = [(n, g) for n in range(NH) for g in range(GROUPS)]
        s = s3
        with nc.Block() as block:
            @block.tensor
            def _(pe):
                for j, (n, g) in enumerate(items):
                    if j >= 4:
                        pe.wait_ge(s.rden, j - 3)
                    pe.matmul(bank(m.ps, j % 4), den_of[:, :], oraw[:, g, n * HALF:(n + 1) * HALF],
                              start=True, stop=True).then_inc(s.den_mm, 1)
                for t in range(NT):
                    if t % 4 == 0:
                        pe.wait_ge(s.o_ready, GROUPS * (t // 4 + 1))
                    if t >= 4:
                        pe.wait_ge(s.y_ready, t - 3)
                    for g in range(GROUPS):
                        last = pe.matmul(bank(m.ps, 4 + t % 4, 0, D), o[:, g, t * P:(t + 1) * P], wo[:, g, :],
                                         start=(g == 0), stop=(g == GROUPS - 1))
                    last.then_inc(s.out_mm, 1)

            @block.vector
            def _(dve):
                for t in range(NT):
                    last = dve.tensor_tensor(m.x[:, t, :], m.x[:, t, :], bo[:, :], ALU.add)
                for j, (n, g) in enumerate(items):
                    dve.wait_ge(s.den_mm, j + 1)
                    dve.reciprocal(rden[:, j, :], bank(m.ps, j % 4)).then_inc(s.rden, 1)
                for t in range(NT):
                    dve.wait_ge(s.out_mm, t + 1)
                    dve.tensor_tensor(m.y[:, t, :], bank(m.ps, 4 + t % 4, 0, D), m.x[:, t, :], ALU.add).then_inc(s.y_ready, 1)

            @block.gpsimd
            def _(pool):
                clear(pool, s2)
                for j, (n, g) in enumerate(items):
                    cols = slice(n * HALF, (n + 1) * HALF)
                    pool.wait_ge(s.rden, j + 1)
                    pool.tensor_tensor(o[:, g, cols], oraw[:, g, cols], rden[:, j, :], ALU.mult).then_inc(s.o_ready, 1)

            @block.sync
            def _(sp):
                store_y(sp, m, s, dst[b])

    with nc.Fori(0, SEQS) as b:
        norm_stage(nc, m, s0, s3, src[b])
        with ExitStack() as own:
            projections(own)
        with ExitStack() as own:
            oraw = own.enter_context(nc.sbuf_tensor("l3_oraw", [P, GROUPS, T], F32))
            with ExitStack() as inner:
                attention(inner, oraw)
            with ExitStack() as inner:
                give_y(nc, inner, m)
                output(inner, oraw, b)



FFN4 = "mm silu_ready h_ready out_mm scaled y_ready y_out"


def layer4(nc, ctx, m, I, src, dst):
    sb = lambda name, shape, dt=F32: ctx.enter_context(nc.sbuf_tensor("l4_" + name, shape, dt))
    w1, w2 = sb("w1", [P, KC, HID]), sb("w2", [P, KC, HID])
    h1, h2, w3 = sb("h1", [P, HC, HID]), sb("h2", [P, HC, HID]), sb("w3", [P, HC, D])
    scale = sb("scale", [P, 4, HC])
    s3v = sb("s3", [P, D])
    ld = signals(nc, ctx, "l4_load", "weights")
    s0 = signals(nc, ctx, "l4_norm", NORM)
    s1 = signals(nc, ctx, "l4_ffn", FFN4)

    with nc.Block() as block:
        @block.sync
        def _(sp):
            pairs = [(w1, "w14"), (w2, "w24"), (h1, "h14"), (h2, "h24"), (w3, "w34"), (scale, "scale4"), (s3v, "s34")]
            for tile, name in pairs:
                sp.dma_start(tile[:], I[name]).then_inc(ld.weights, 16)
            sp.wait_ge(ld.weights, 16 * len(pairs))

    def net(own, b):
        sb = lambda name, shape, dt=F32: own.enter_context(nc.sbuf_tensor("l4a_" + name, shape, dt))
        sil = sb("sil", [P, 4, HALF])
        u = sb("u", [P, 3, HC, HALF])
        ys = sb("ys", [P, 2, D])
        per_n = 4 * HC
        s = s1

        def at(n, stage, o):
            return per_n * n + (2 * o if stage == 0 else 2 * HC + (stage - 1) * HC + o)

        def made(n, stage, o=0):
            return 3 * HC * n + HC * stage + o

        with nc.Block() as block:
            @block.tensor
            def _(pe):
                def product(i, w, kc, o, x):
                    if i >= 6:
                        j = i - 6
                        nn, r = divmod(j, per_n)
                        pe.wait_ge(s.h_ready, made(nn, 0, r // 2 + 1) if r < 2 * HC else made(nn, 1, r - 2 * HC + 1))
                    for c in range(kc):
                        last = pe.matmul(bank(m.ps, i % 6), w[:, c, o * P:(o + 1) * P], x(c), start=(c == 0), stop=(c == kc - 1))
                    last.then_inc(s.mm, 1)

                for n in range(NH):
                    for o in range(HC):
                        x = lambda c: m.xT[:, c, n * HALF:(n + 1) * HALF]
                        product(at(n, 0, o), w1, KC, o, x)
                        product(at(n, 0, o) + 1, w2, KC, o, x)
                    for stage, w in ((1, h1), (2, h2)):
                        pe.wait_ge(s.h_ready, made(n, stage))
                        for o in range(HC):
                            product(at(n, stage, o), w, HC, o, lambda c: u[:, stage - 1, c, :])
                    pe.wait_ge(s.h_ready, made(n, 3))
                    for j in range(HALF // P):
                        t = n * (HALF // P) + j
                        if t >= 2:
                            pe.wait_ge(s.scaled, t - 1)
                        for c in range(HC):
                            last = pe.matmul(bank(m.ps, 6 + t % 2, 0, D), u[:, 2, c, j * P:(j + 1) * P], w3[:, c, :],
                                             start=(c == 0), stop=(c == HC - 1))
                        last.then_inc(s.out_mm, 1)

            @block.scalar
            def _(act):
                for n in range(NH):
                    for o in range(HC):
                        i = at(n, 0, o)
                        act.wait_ge(s.mm, i + 1)
                        k = HC * n + o
                        if k >= 4:
                            act.wait_ge(s.h_ready, made((k - 4) // HC, 0, (k - 4) % HC + 1))
                        act.activation(sil[:, k % 4, :], bank(m.ps, i % 6), ACT.Silu, scale=scale[:, 0, o:o + 1]).then_inc(s.silu_ready, 1)
                    act.wait_ge(s.h_ready, made(n, 1))
                    for stage in (1, 2):
                        for o in range(HC):
                            i = at(n, stage, o)
                            act.wait_ge(s.mm, i + 1)
                            if stage == 2 and n and o == 0:
                                act.wait_ge(s.out_mm, HALF // P * n)
                            act.activation(u[:, stage, o, :], bank(m.ps, i % 6), ACT.Gelu,
                                           scale=scale[:, 1 + stage, o:o + 1]).then_inc(s.h_ready, 1)

            @block.vector
            def _(dve):
                for n in range(NH):
                    for o in range(HC):
                        i, k = at(n, 0, o) + 1, HC * n + o
                        dve.wait_ge(s.mm, i + 1)
                        dve.wait_ge(s.silu_ready, k + 1)
                        if n and o == 0:
                            dve.wait_ge(s.mm, at(n - 1, 1, HC))
                            dve.wait_ge(s.h_ready, made(n, 0))
                        dve.scalar_tensor_tensor(u[:, 0, o, :], bank(m.ps, i % 6), scale[:, 1, o:o + 1], sil[:, k % 4, :],
                                                 ALU.mult, ALU.mult).then_inc(s.h_ready, 1)
                    for j in range(HALF // P):
                        t = n * (HALF // P) + j
                        dve.wait_ge(s.out_mm, t + 1)
                        if t >= 2:
                            dve.wait_ge(s.y_ready, t - 1)
                        dve.tensor_tensor(ys[:, t % 2, :], bank(m.ps, 6 + t % 2, 0, D), s3v[:, :], ALU.mult).then_inc(s.scaled, 1)
                        dve.wait_ge(s.scaled, t + 1)
                        dve.tensor_tensor(m.y[:, t, :], ys[:, t % 2, :], m.x[:, t, :], ALU.add).then_inc(s.y_ready, 1)

            @block.gpsimd
            def _(pool):
                clear(pool, s0)

            @block.sync
            def _(sp):
                store_y(sp, m, s, dst[b])

    with nc.Fori(0, SEQS) as b:
        norm_stage(nc, m, s0, s1, src[b])
        with ExitStack() as own:
            give_y(nc, own, m)
            net(own, b)



def program(nc, I, layers, src, scratch, out):
    with ExitStack() as ctx:
        sb = lambda name, shape, dt=F32: ctx.enter_context(nc.sbuf_tensor("sb_" + name, shape, dt))
        m = Memory(nc, ctx)
        mask_kq, mask_qk = sb("mask_kq32", [P, P]), sb("mask_qk32", [P, P])
        ld = signals(nc, ctx, "load", "consts made")
        with nc.Block() as block:
            @block.sync
            def _(sp):
                for tile, name in ((m.ident, "ident"), (mask_kq, "mask_kq"), (mask_qk, "mask_qk")):
                    sp.dma_start(tile[:, :], I[name]).then_inc(ld.consts, 16)
                sp.wait_ge(ld.consts, 48)

            @block.vector
            def _(dve):
                dve.memset(m.eps[:, :], EPS).then_inc(ld.made, 1)
                dve.memset(m.x[:, 0, 0:P], -1.0).then_inc(ld.made, 1)
                dve.wait_ge(ld.made, 2)
                dve.tensor_copy(m.negones[:, :], m.x[:, 0, 0:P]).then_inc(ld.made, 1)
                dve.wait_ge(ld.consts, 48)
                dve.tensor_copy(m.ident16[:, :], m.ident[:, :]).then_inc(ld.made, 1)
                dve.tensor_copy(m.mask_kq[:, :], mask_kq[:, :]).then_inc(ld.made, 1)
                dve.tensor_copy(m.mask_qk[:, :], mask_qk[:, :]).then_inc(ld.made, 1)

        rows = lambda dram: dram.rearrange("(b t p) d -> b p t d", b=SEQS, p=P)
        here = src
        for n, layer in enumerate(layers):
            with ExitStack() as own:
                if layer is layer1:
                    m.y2 = own.enter_context(nc.sbuf_tensor("sb_affine_in", [P, NT, D], F32))
                layer(nc, own, m, I, rows(here), rows(scratch[n]))
            here = scratch[n]
        with ExitStack() as own:
            sa, sbb = signals(nc, own, "last_a", NORM), signals(nc, own, "last_b", "nothing")
            with nc.Fori(0, SEQS) as b:
                norm_stage(nc, m, sa, sbb, rows(here)[b], dst=rows(out)[b])
                with nc.Block() as block:
                    @block.gpsimd
                    def _(pool):
                        clear(pool, sa)



def lay(w):
    return w.reshape(w.shape[0] // P, P, -1).transpose(1, 0, 2)


def by_partition(v):
    return v.reshape(-1, P).T


def to_all(v):
    return np.broadcast_to(v.reshape(1, -1), (P, v.size))


def constants():
    k, q = np.meshgrid(np.arange(P), np.arange(P), indexing="ij")
    hidden = np.float32(-2.0 ** 100)
    return {
        "ident": np.eye(P, dtype=np.float32), "mask_kq": np.where(q < k, hidden, np.float32(0.0)),
        "mask_qk": np.where(k < q, hidden, np.float32(0.0)),
    }


def layout1(i):
    return {
        "wqkv": lay(i["L0_attn_qkv_w"]), "wgate": lay(i["L0_attn_gate_w"]), "bqkv": by_partition(i["L0_attn_qkv_b"]),
        "bgate": by_partition(i["L0_attn_gate_b"]), "bv": to_all(i["L0_attn_qkv_b"][2 * D:]),
        "lng": by_partition(i["L0_attn_ln_g"]), "lnb": by_partition(i["L0_attn_ln_b"]),
    }


def layout2(i):
    twice = lambda w: lay(np.broadcast_to(w.reshape(D, H0, 1, DH0), (D, H0, 2, DH0)).reshape(D, -1))
    pick = np.zeros((P, H0 // 2, NE, 2), np.float32)
    for c in range(H0 // 2):
        for e in range(NE):
            for a in range(2):
                pick[(2 * c + a) * NE + e::H0 * NE, c, e, a] = 1.0
    ve = i["L0_ffn_value_experts"].transpose(2, 1, 0, 3)
    oe = i["L0_ffn_output_experts"].reshape(NE, H0 // 2, P, D).transpose(2, 1, 0, 3)
    return {
        "wq2": twice(i["L0_ffn_w_q"]), "wk2": twice(i["L0_ffn_w_k"]), "wg2": lay(i["L0_ffn_w_gate"]),
        "ve2": lay(ve.reshape(D, -1)).reshape(P, KC, H0, NE * DH0), "oe2": oe,
        "prio": to_all(np.arange(NE, 0, -1, dtype=np.float32)),
        "klo": np.where(np.arange(P) < P // 2, 0.0, -1.0).astype(np.float32).reshape(P, 1), "pick": pick.reshape(P, -1),
    }


def layout3(i):
    fold = lambda w: w.reshape(-1, H1, 1, DH1)
    stack = lambda w: np.broadcast_to(fold(w), (fold(w).shape[0], H1, 4, DH1)).reshape(-1, 4 * D)
    part = np.arange(P) % (4 * DH1) // DH1
    wo = np.zeros((H1, 2 * DH1, D), np.float32)
    wo[:, :DH1] = i["L1_attn_Wo"].reshape(H1, DH1, D)
    r, c = np.meshgrid(np.arange(P), np.arange(P), indexing="ij")
    return {
        "wq3": lay(stack(i["L1_attn_Wq"])), "wk3": lay(stack(i["L1_attn_Wk"])), "wv3": lay(i["L1_attn_Wv"]),
        "wo3": lay(wo.reshape(-1, D)), "bq3": by_partition(stack(i["L1_attn_bq"])), "bk3": by_partition(stack(i["L1_attn_bk"])),
        "bv3": to_all(i["L1_attn_bv"]), "bo3": to_all(i["L1_attn_bo"]), "w13": lay(i["L1_attn_dp_w1"]),
        "hv3": np.stack([to_all(i["L1_attn_" + n]) for n in ("dp_b1", "ln_g", "ln_b", "dp_w2")], 1),
        "gv3": np.stack([to_all(i["L1_attn_" + n]) for n in ("g_w1", "g_b1", "g_w2")], 1),
        "b23": np.concatenate([to_all(i["L1_attn_dp_b2"]), to_all(i["L1_attn_g_b2"])], 1),
        "qneg3": np.where(part >= 2, -1.0, 0.0).astype(np.float32).reshape(P, 1),
        "kneg3": np.where(part % 2 == 1, -1.0, 0.0).astype(np.float32).reshape(P, 1),
        "den_of": ((r // 32 == c // 32) & (r % 32 == DH1 + c % DH1)).astype(np.float32),
    }


def layout4(i):
    n = lambda name: i["L1_ffn_" + name]
    return {
        "w14": lay(n("w1_w").T), "w24": lay(n("w2_w").T), "h14": lay(n("h1_w").T), "h24": lay(n("h2_w").T),
        "w34": lay(n("w3_w").T), "scale4": np.stack([by_partition(n(x)) for x in ("w1_s", "w2_s", "h1_s", "h2_s")], 1),
        "s34": to_all(n("w3_s")),
    }


def kernel(**inputs):
    import concourse.bacc as bacc
    from concourse.bass_utils import run_bass_kernel_spmd

    given = {name: np.asarray(a) for name, a in inputs.items()}
    arrays = {"tokens": given["L0_attn_x"].reshape(SEQS * T, D), **constants(), **layout1(given), **layout2(given),
              **layout3(given), **layout4(given)}
    arrays = {name: np.ascontiguousarray(a) for name, a in arrays.items()}
    nc = bacc.Bacc("TRN2", target_bir_lowering=False, num_devices=1)
    I = {name: nc.dram_tensor(name, a.shape, mybir.dt.from_np(a.dtype), kind="ExternalInput").ap() for name, a in arrays.items()}
    scratch = [nc.dram_tensor(f"sums{n}", (SEQS * T, D), F32, kind="Internal").ap() for n in range(1, 5)]
    out = nc.dram_tensor("normed", (SEQS * T, D), F32, kind="ExternalOutput").ap()
    program(nc, I, [layer1, layer2, layer3, layer4], I["tokens"], scratch, out)
    got = run_bass_kernel_spmd(nc, [arrays], core_ids=[0]).results[0]["normed"]
    return got.reshape(SEQS, T, D)
```

```python
from collections import namedtuple
from contextlib import ExitStack


import numpy as np

import concourse.bass as bass
from concourse import mybir

ALU = mybir.AluOpType
ACT = mybir.ActivationFunctionType
F32 = mybir.dt.float32
F32R = mybir.dt.float32r
BF16 = mybir.dt.bfloat16
AX_X = mybir.AxisListType.X

P = 128
D = 256
KC = D // P
SEQS = 4
T = 1024
NT = T // P
HALF = 512
NH = T // HALF
EPS = 1e-5
DEN_EPS = 1e-6

H0, DH0, NE = 8, 64, 8
SCALE0 = DH0 ** -0.5
H1, DH1 = 16, 16
SCALE1 = DH1 ** -0.5
G1 = 4
HID = 1024
HC = HID // P


class Memory:

    def __init__(self, nc, ctx):
        def sb(name, shape, dt=F32):
            return ctx.enter_context(nc.sbuf_tensor("sb_" + name, shape, dt))

        self.ps = ctx.enter_context(nc.psum_tensor("sums", [P, 8 * HALF], F32))
        self.x = sb("x", [P, NT, D])
        self.nx = sb("nx", [P, NT, D])
        self.stats, self.moments = sb("stats", [P, NT, 6]), sb("moments", [P, NT, 2])
        self.sd, self.rstd, self.eps = sb("sd", [P, NT]), sb("rstd", [P, NT]), sb("eps", [P, 1])
        self.ident, self.ident16 = sb("ident", [P, P]), sb("ident16", [P, P], BF16)
        self.mask_kq, self.mask_qk = sb("mask_kq", [P, P], BF16), sb("mask_qk", [P, P], BF16)
        self.negones = sb("negones", [P, P], F32R)
        self.weight_copies, self.weights_copied = None, None


def bank(ps, n, lo=0, hi=HALF, rows=slice(0, P)):
    return ps[rows, n * HALF + lo:n * HALF + hi]


def halves(lo, hi):
    return [(max(lo, h * HALF), min(hi, (h + 1) * HALF)) for h in range(NH) if max(lo, h * HALF) < min(hi, (h + 1) * HALF)]


class Chain:

    def __init__(self, engine, sem):
        self.engine, self.sem, self.n = engine, sem, 0

    def __call__(self, instruction):
        self.n += 1
        instruction.then_inc(self.sem, 1)
        self.engine.wait_ge(self.sem, self.n)


def signals(nc, ctx, stage, names):
    return namedtuple(stage, names)(*(ctx.enter_context(nc.semaphore(f"{stage}_{n}")) for n in names.split()))


def clear(pool, stale):
    for sem in stale:
        pool.sem_clear(sem)



FETCH = " nx_in nx_stats nx_moments nx_sd nx_chain nx_ready"
ENTRY = " transposed xT_ready x_copied"


def inverse_sd(step, dve, m, r, var, sd):
    step(dve.reciprocal(r, sd))
    step(dve.tensor_tensor(sd, r, r, ALU.mult))
    step(dve.scalar_tensor_tensor(sd, var, m.eps[:, 0:1], sd, ALU.add, ALU.mult))
    step(dve.tensor_scalar(sd, sd, -0.5, 1.5, ALU.mult, ALU.add))
    step(dve.tensor_tensor(r, r, sd, ALU.mult))


def fetch_load(sp, m, s, src):
    sp.dma_start(m.nx[:, :, :], src).then_inc(s.nx_in, 16)


def fetch_stats(dve, m, s):
    dve.wait_ge(s.nx_in, 16)
    for t in range(NT):
        last = dve.bn_stats(m.stats[:, t, :], m.nx[:, t, :])
    last.then_inc(s.nx_stats, 1)
    dve.wait_ge(s.nx_stats, 1)
    for t in range(NT):
        last = dve.bn_aggr(m.moments[:, t, :], m.stats[:, t, :])
    last.then_inc(s.nx_moments, 1)


def fetch_sd(act, m, s):
    act.wait_ge(s.nx_moments, 1)
    act.activation(m.sd[:, :], m.moments[:, :, 1], ACT.Sqrt, bias=m.eps[:, 0:1]).then_inc(s.nx_sd, 1)


def fetch_norm(dve, m, s):
    dve.wait_ge(s.nx_sd, 1)
    inverse_sd(Chain(dve, s.nx_chain), dve, m, m.rstd[:, :], m.moments[:, :, 1], m.sd[:, :])
    for t in range(NT):
        last = dve.tensor_scalar(m.nx[:, t, :], m.nx[:, t, :], m.moments[:, t, 0:1], m.rstd[:, t:t + 1],
                                 ALU.subtract, ALU.mult)
    last.then_inc(s.nx_ready, 1)


def fetch_first(nc, m, s, src):
    with nc.Block() as block:
        @block.sync
        def _(sp):
            fetch_load(sp, m, s, src)

        @block.vector
        def _(dve):
            fetch_stats(dve, m, s)
            fetch_norm(dve, m, s)

        @block.scalar
        def _(act):
            fetch_sd(act, m, s)

    with nc.Block() as block:
        @block.gpsimd
        def _(pool):
            clear(pool, s)


ENTRY_BANKS = 4


def entry_transpose(pe, m, s):
    for t in range(NT):
        if t >= ENTRY_BANKS:
            pe.wait_ge(s.xT_ready, t - ENTRY_BANKS + 1)
        for c in range(KC):
            last = pe.transpose(bank(m.ps, t % ENTRY_BANKS, c * P, (c + 1) * P), m.nx[:, t, c * P:(c + 1) * P], m.ident[:, :])
        last.then_inc(s.transposed, 1)


def entry_copy(act, m, s, xT, affine=None):
    for t in range(NT):
        act.wait_ge(s.transposed, t + 1)
        if affine:
            for c in range(KC):
                last = act.activation(xT[:, c, t * P:(t + 1) * P], bank(m.ps, t % ENTRY_BANKS, c * P, (c + 1) * P),
                                      ACT.Identity, scale=affine[0][:, c:c + 1], bias=affine[1][:, c:c + 1])
        else:
            last = act.copy(xT[:, :, t * P:(t + 1) * P],
                            bank(m.ps, t % ENTRY_BANKS, 0, D).rearrange("p (c q) -> p c q", c=KC))
        last.then_inc(s.xT_ready, 1)


def entry_residual(pool, m, s):
    pool.tensor_copy(m.x[:, :, :], m.nx[:, :, :]).then_inc(s.x_copied, 1)


def store(sp, s, tile, dst):
    for t in range(0, NT, 2):
        sp.wait_ge(s.y_ready, t + 2)
        sp.dma_start(dst[:, t:t + 2, :], tile[:, t:t + 2, :]).then_inc(s.y_out, 16)
    sp.wait_ge(s.y_out, 16 * NT // 2)



PROJ1 = "x_in transposed xT_ready gate_mm qk_mm v_mm gate_read half_gate k_gated min_ready relu_ready exp_ready v_read qkT_ready chain"
ATTN1 = "score_mm score_copied masked out_mm den y_ready y_out rden" + FETCH


def layer1(nc, ctx, m, I, src, dst):
    sb = lambda name, shape, dt=F32: ctx.enter_context(nc.sbuf_tensor("l1_" + name, shape, dt))
    wqkv, wgate = sb("wqkv", [P, KC, 3 * D]), sb("wgate", [P, KC, D])
    bqkv, bgate, hbgate = sb("bqkv", [P, 6]), sb("bgate", [P, KC]), sb("hbgate", [P, KC])
    bv, lng, lnb = sb("bv", [P, D]), sb("lng", [P, KC]), sb("lnb", [P, KC])
    qT, kT = sb("qT", [P, KC, T]), sb("kT", [P, KC, T])
    v = sb("v", [P, NT, D + 2])
    gate = sb("gate", [P, 2 * NH, HALF])
    kg = sb("kg", [P, 2 * NH, HALF])
    neg = sb("neg", [P, 4 * NH, HALF])
    AT = sb("AT", [P, NT, T])
    den = sb("den", [P, NT, 2])
    ld = signals(nc, ctx, "l1_load", "weights ones hb")
    s0 = signals(nc, ctx, "l1_first", FETCH)
    xT, y = sb("xT", [P, KC, T]), sb("y", [P, NT, D])
    s1 = signals(nc, ctx, "l1_proj", PROJ1)
    s2 = signals(nc, ctx, "l1_attn", ATTN1)

    with nc.Block() as block:
        @block.sync
        def _(sp):
            pairs = [(wqkv, "wqkv"), (wgate, "wgate"), (bqkv, "bqkv"), (bgate, "bgate"), (bv, "bv"), (lng, "lng"), (lnb, "lnb")]
            for tile, name in pairs:
                sp.dma_start(tile[:], I[name]).then_inc(ld.weights, 16)
            sp.wait_ge(ld.weights, 16 * len(pairs))

        @block.vector
        def _(dve):
            dve.memset(v[:, :, D:D + 2], 1.0).then_inc(ld.ones, 1)
            dve.wait_ge(ld.weights, 16 * 7)
            dve.tensor_scalar(hbgate[:, :], bgate[:, :], 0.5, None, ALU.mult).then_inc(ld.hb, 1)

    fetch_first(nc, m, s0, src[0])
    NG = KC * NH
    with nc.Fori(0, SEQS) as b:
        with nc.Block() as block:
            s = s1

            @block.gpsimd
            def _(pool):
                clear(pool, s2)
                for j in range(2 * NG):
                    n, c = divmod(j // 2, KC)
                    pool.wait_ge(s.exp_ready, j + 1)
                    out = (kT if j % 2 == 0 else qT)[:, c, n * HALF:(n + 1) * HALF]
                    pool.wait_ge(s.relu_ready, j + 1)
                    pool.tensor_tensor(out, out, neg[:, j, :], ALU.add).then_inc(s.qkT_ready, 1)

            @block.sync
            def _(sp):
                sp.dma_start(m.x[:, :, :], src[b]).then_inc(s.x_in, 16)
                sp.wait_ge(s.x_in, 16)

            @block.tensor
            def _(pe):
                entry_transpose(pe, m, s)
                pe.wait_ge(s.xT_ready, NT)

                def product(out, w, lo, n):
                    for c in range(KC):
                        last = pe.matmul(out, w[:, c, lo:lo + P], xT[:, c, n * HALF:(n + 1) * HALF],
                                         start=(c == 0), stop=(c == KC - 1))
                    return last

                for g in range(NG):
                    n, c = divmod(g, KC)
                    if g >= 2:
                        pe.wait_ge(s.gate_read, g - 1)
                    product(bank(m.ps, 2 + g % 2), wgate, c * P, n).then_inc(s.gate_mm, 1)
                    if g >= 2:
                        pe.wait_ge(s.relu_ready, 2 * (g - 1))
                    product(bank(m.ps, 4 + g % 2), wqkv, D + c * P, n).then_inc(s.qk_mm, 1)
                    product(bank(m.ps, 6 + g % 2), wqkv, c * P, n).then_inc(s.qk_mm, 1)
                for t in range(NT):
                    if t >= 2:
                        pe.wait_ge(s.v_read, t - 1)
                    for c in range(KC):
                        last = pe.matmul(bank(m.ps, t % 2, 0, D), xT[:, c, t * P:(t + 1) * P],
                                         wqkv[:, c, 2 * D:3 * D], start=(c == 0), stop=(c == KC - 1))
                    last.then_inc(s.v_mm, 1)

            @block.scalar
            def _(act):
                entry_copy(act, m, s, xT, affine=(lng, lnb))
                for g in range(NG):
                    c = g % KC
                    act.wait_ge(s.gate_mm, g + 1)
                    act.activation(gate[:, g, :], bank(m.ps, 2 + g % 2), ACT.Tanh, scale=0.5,
                                   bias=hbgate[:, c:c + 1]).then_inc(s.gate_read, 1)
                    for j in (2 * g, 2 * g + 1):
                        act.wait_ge(s.min_ready, j + 1)
                        act.activation(neg[:, j, :], neg[:, j, :], ACT.Exp).then_inc(s.exp_ready, 1)

            @block.vector
            def _(dve):
                for g in range(NG):
                    n, c = divmod(g, KC)
                    cols = slice(n * HALF, (n + 1) * HALF)
                    dve.wait_ge(s.gate_read, g + 1)
                    dve.tensor_scalar(gate[:, g, :], gate[:, g, :], 0.5, 0.5, ALU.mult, ALU.add).then_inc(s.half_gate, 1)
                    dve.wait_ge(s.half_gate, g + 1)
                    dve.wait_ge(s.qk_mm, 2 * g + 1)
                    dve.scalar_tensor_tensor(kg[:, g, :], bank(m.ps, 4 + g % 2), bqkv[:, 2 + c:3 + c], gate[:, g, :],
                                             ALU.add, ALU.mult).then_inc(s.k_gated, 1)
                    dve.wait_ge(s.k_gated, g + 1)
                    dve.tensor_scalar(neg[:, 2 * g, :], kg[:, g, :], 0.0, None, ALU.min).then_inc(s.min_ready, 1)
                    dve.tensor_scalar(kT[:, c, cols], kg[:, g, :], 0.0, None, ALU.max).then_inc(s.relu_ready, 1)
                    dve.wait_ge(s.qk_mm, 2 * g + 2)
                    q = bank(m.ps, 6 + g % 2)
                    dve.tensor_scalar(neg[:, 2 * g + 1, :], q, bqkv[:, c:c + 1], 0.0, ALU.add, ALU.min).then_inc(s.min_ready, 1)
                    dve.tensor_scalar(qT[:, c, cols], q, bqkv[:, c:c + 1], 0.0, ALU.add, ALU.max).then_inc(s.relu_ready, 1)
                for t in range(NT):
                    dve.wait_ge(s.v_mm, t + 1)
                    dve.tensor_tensor(v[:, t, 0:D], bank(m.ps, t % 2, 0, D), bv[:, :], ALU.add).then_inc(s.v_read, 1)

        with nc.Block() as block:
            s = s2

            @block.gpsimd
            def _(pool):
                clear(pool, s1)
                for k in range(NT):
                    pool.wait_ge(s.score_copied, k + 1)
                    diag = AT[:, k, k * P:(k + 1) * P]
                    pool.affine_select(out=diag, in_=diag, compare_op=ALU.is_ge, fill=0.0, base=0, pattern=[[1, P]],
                                       channel_multiplier=-1).then_inc(s.masked, 1)

            @block.tensor
            def _(pe):
                for k in range(NT + 1):
                    if k < NT:
                        if k >= 2:
                            pe.wait_ge(s.score_copied, k - 1)
                        for lo, hi in halves(k * P, T):
                            for c in range(KC):
                                last = pe.matmul(bank(m.ps, 2 * (k % 2), lo, hi), kT[:, c, k * P:(k + 1) * P],
                                                 qT[:, c, lo:hi], start=(c == 0), stop=(c == KC - 1))
                        last.then_inc(s.score_mm, 1)
                    if k >= 1:
                        t = k - 1
                        pe.wait_ge(s.masked, t + 1)
                        if t >= 2:
                            pe.wait_ge(s.y_ready, t - 1)
                        for k2 in range(t + 1):
                            last = pe.matmul(bank(m.ps, 4 + t % 2, 0, D + 2), AT[:, k2, t * P:(t + 1) * P], v[:, k2, :],
                                             start=(k2 == 0), stop=(k2 == t))
                        last.then_inc(s.out_mm, 1)

            @block.scalar
            def _(act):
                for k in range(NT):
                    if k == 4:
                        fetch_sd(act, m, s)
                    act.wait_ge(s.score_mm, k + 1)
                    act.copy(AT[:, k, k * P:T], bank(m.ps, 2 * (k % 2), k * P, T)).then_inc(s.score_copied, 1)

            @block.vector
            def _(dve):
                fetch_stats(dve, m, s)
                for t in range(NT):
                    if t == 4:
                        fetch_norm(dve, m, s)
                    dve.wait_ge(s.out_mm, t + 1)
                    dve.tensor_scalar(den[:, t, 0:1], bank(m.ps, 4 + t % 2, D, D + 1), DEN_EPS, None, ALU.add).then_inc(s.den, 1)
                    dve.wait_ge(s.den, t + 1)
                    dve.reciprocal(den[:, t, 1:2], den[:, t, 0:1]).then_inc(s.rden, 1)
                    dve.wait_ge(s.rden, t + 1)
                    dve.scalar_tensor_tensor(y[:, t, :], bank(m.ps, 4 + t % 2, 0, D), den[:, t, 1:2], m.x[:, t, :],
                                             ALU.mult, ALU.add).then_inc(s.y_ready, 1)

            @block.sync
            def _(sp):
                fetch_load(sp, m, s, src[(b + 1) % SEQS])
                store(sp, s, y, dst[b])

    return ld, s0, s1, s2



GATES2 = ("transposed xT_ready x_copied logits exp_in exp_out chain gm_ready hilo gmT_mm gmT_ready value_mm value_masked v_ready")
ATTN2 = ("k_mm k_hi k_ready q_mm q_hi q_ready max_mm max_read shift_ready score_mm exp_ready pv_mm "
         "rden o_ready" + FETCH)
OUT2 = "sel_ready even_oe_in odd_oe_in mask_mm routed out_mm y_ready y_out"
CLAMP = 80.0


def layer2(nc, ctx, m, I, src, dst):
    sb = lambda name, shape, dt=F32: ctx.enter_context(nc.sbuf_tensor("l2_" + name, shape, dt))
    wq, wk, wg = sb("wq", [P, KC, H0 * P]), sb("wk", [P, KC, H0 * P]), sb("wg", [P, KC, H0 * NE])
    ve = sb("ve", [P, KC, H0, NE * DH0])
    prio = sb("prio", [P, NE])
    klo = sb("klo", [P, 1])
    pick = sb("pick", [P, H0 * NE])
    vx = sb("vx", [P, NT, H0, P])
    oT = sb("oT", [P, H0 // 2, T])
    gmT = sb("gmT", [P, T], F32R)
    vcol = lambda h: slice(DH0 * (h % 2), DH0 * (h % 2) + DH0)
    ones = lambda h: slice(DH0 * (1 - h % 2), DH0 * (1 - h % 2) + DH0)
    ld = signals(nc, ctx, "l2_load", "weights ones")
    s0 = signals(nc, ctx, "l2_first", FETCH)
    xT = sb("xT", [P, KC, T])
    s1 = signals(nc, ctx, "l2_gates", GATES2)
    s2 = signals(nc, ctx, "l2_attn", ATTN2)
    s3 = signals(nc, ctx, "l2_out", OUT2)

    with nc.Block() as block:
        @block.sync
        def _(sp):
            pairs = [(wq, "wq2"), (wk, "wk2"), (wg, "wg2"), (ve, "ve2"), (prio, "prio"), (klo, "klo"), (pick, "pick")]
            for tile, name in pairs:
                sp.dma_start(tile[:], I[name]).then_inc(ld.weights, 16)
            sp.wait_ge(ld.weights, 16 * len(pairs))

        @block.vector
        def _(dve):
            dve.memset(vx[:, :, :, :], 1.0).then_inc(ld.ones, 1)

    def gates_and_values(own):
        sb = lambda name, shape, dt=F32: own.enter_context(nc.sbuf_tensor("l2a_" + name, shape, dt))
        N = NT * H0 * NE
        z, e, g, first = sb("z", [P, N]), sb("e", [P, N]), sb("g", [P, N]), sb("first", [P, N])
        gm, gm_hi, hilo = sb("gm", [P, N]), sb("gm_hi", [P, N], F32R), sb("hilo", [P, NT, 2, H0 * NE])
        top, win = sb("top", [P, NT * H0]), sb("win", [P, NT * H0])
        VM = 4
        vm = sb("vm", [P, VM, NE * DH0])
        RING = 6
        by_head = lambda x: x[:, :].rearrange("p (n e) -> p n e", e=NE)
        s = s1
        with nc.Block() as block:
            @block.gpsimd
            def _(pool):
                clear(pool, s3)
                entry_residual(pool, m, s)

            @block.tensor
            def _(pe):
                entry_transpose(pe, m, s)
                for t in range(NT):
                    pe.wait_ge(s.xT_ready, t + 1)
                    for c in range(KC):
                        last = pe.matmul(bank(m.ps, 7, t * 64, t * 64 + 64), xT[:, c, t * P:(t + 1) * P], wg[:, c, :],
                                         start=(c == 0), stop=(c == KC - 1))
                last.then_inc(s.logits, 1)
                for t in range(NT):
                    for h in range(H0):
                        n = t * H0 + h
                        if n >= RING:
                            pe.wait_ge(s.value_masked, n - RING + 1)
                        for c in range(KC):
                            last = pe.matmul(bank(m.ps, n % RING), xT[:, c, t * P:(t + 1) * P], ve[:, c, h, :],
                                             start=(c == 0), stop=(c == KC - 1))
                        last.then_inc(s.value_mm, 1)
                    if t == 1:
                        pe.wait_ge(s.hilo, 2)
                        for t2 in range(NT):
                            at = t2 * P
                            last = pe.transpose(bank(m.ps, 6, at, at + P), hilo[:, t2, :, :].rearrange("p a b -> p (a b)"),
                                                m.ident[:, :])
                            if t2 % 4 == 3:
                                last.then_inc(s.gmT_mm, 1)

            @block.scalar
            def _(act):
                entry_copy(act, m, s, xT)
                act.wait_ge(s.exp_in, 1)
                act.activation(e[:, :], z[:, :], ACT.Exp).then_inc(s.exp_out, 1)
                for n in range(NH):
                    act.wait_ge(s.gmT_mm, n + 1)
                    act.copy(gmT[:, n * HALF:(n + 1) * HALF], bank(m.ps, 6 + n)).then_inc(s.gmT_ready, 1)

            @block.vector
            def _(dve):
                step = Chain(dve, s.chain)
                every = lambda x: x[:, :].unsqueeze(2).to_broadcast([P, NT * H0, NE])
                dve.wait_ge(s.logits, 1)
                dve.tensor_scalar(z[:, :], bank(m.ps, 7), -1.0, CLAMP, ALU.mult, ALU.min).then_inc(s.exp_in, 1)
                dve.wait_ge(s.exp_out, 1)
                step(dve.tensor_scalar(g[:, :], e[:, :], 1.0, None, ALU.add))
                step(dve.reciprocal(g[:, :], g[:, :]))
                step(dve.tensor_reduce(top[:, :], by_head(g), AX_X, ALU.max))
                step(dve.tensor_tensor(by_head(first), by_head(g), every(top), ALU.is_equal))
                step(dve.tensor_tensor(by_head(first), by_head(first),
                                       prio[:, :].unsqueeze(1).to_broadcast([P, NT * H0, NE]), ALU.mult))
                step(dve.tensor_reduce(win[:, :], by_head(first), AX_X, ALU.max))
                step(dve.tensor_tensor(by_head(first), by_head(first), every(win), ALU.is_equal))
                dve.tensor_tensor(gm[:, :], first[:, :], g[:, :], ALU.mult).then_inc(s.gm_ready, 1)
                dve.wait_ge(s.gm_ready, 1)
                step(dve.tensor_copy(gm_hi[:, :], gm[:, :]))
                tiles = lambda x: x.rearrange("p (t n) -> p t n", t=NT)
                dve.tensor_copy(hilo[:, :, 0, :], tiles(gm_hi[:, :].bitcast(F32))).then_inc(s.hilo, 1)
                dve.tensor_tensor(hilo[:, :, 1, :], tiles(gm[:, :]), tiles(gm_hi[:, :].bitcast(F32)),
                                  ALU.subtract).then_inc(s.hilo, 1)
                for t in range(NT):
                    for h in range(H0):
                        n = t * H0 + h
                        dve.wait_ge(s.value_mm, n + 1)
                        if n >= VM:
                            dve.wait_ge(s.v_ready, n - VM + 1)
                        mask = gm[:, n * NE:(n + 1) * NE].unsqueeze(2).to_broadcast([P, NE, DH0])
                        dve.tensor_tensor(vm[:, n % VM, :].rearrange("p (e k) -> p e k", e=NE),
                                          bank(m.ps, n % RING).rearrange("p (e k) -> p e k", e=NE), mask,
                                          ALU.mult).then_inc(s.value_masked, 1)
                        dve.wait_ge(s.value_masked, n + 1)
                        dve.tensor_reduce(vx[:, t, h, vcol(h)], vm[:, n % VM, :].rearrange("p (e k) -> p k e", e=NE),
                                          AX_X, ALU.add).then_inc(s.v_ready, 1)

    def attention(own, b):
        sb = lambda name, shape, dt=F32: own.enter_context(nc.sbuf_tensor("l2b_" + name, shape, dt))
        RK = 3
        kst, qst, qlo = (sb(n, [P, RK, T], F32R) for n in ("kst", "qst", "qlo"))
        shift = sb("shift", [P, 2, T], F32R)
        hi = sb("hi", [P, NH, HALF], F32R)
        prob = sb("prob", [P, 2, T])
        mx = sb("mx", [P, H0, NT])
        rden = sb("rden", [P, T])
        s = s2
        with nc.Block() as block:
            @block.tensor
            def _(pe):
                def project(h, w, n, mm):
                    for c in range(KC):
                        last = pe.matmul(bank(m.ps, 6 + n), w[:, c, h * P:(h + 1) * P], xT[:, c, n * HALF:(n + 1) * HALF],
                                         start=(c == 0), stop=(c == KC - 1))
                    last.then_inc(mm, 1)

                def maxima(h, t):
                    if t == 0:
                        pe.wait_ge(s.k_ready, 2 * h + 2)
                        pe.wait_ge(s.q_ready, 2 * h + 2)
                    if h + t:
                        pe.wait_ge(s.max_read, NT * h + t)
                    for lo, hi_ in halves(0, (t + 1) * P):
                        last = pe.matmul(bank(m.ps, 2, lo, hi_), qst[:, h % RK, t * P:(t + 1) * P], kst[:, h % RK, lo:hi_],
                                         start=True, stop=True)
                    last = pe.matmul(bank(m.ps, 2, t * P, (t + 1) * P), m.ident16[:, :], m.mask_qk[:, :],
                                     start=False, stop=True, skip_group_check=True)
                    last.then_inc(s.max_mm, 1)

                def scores(h, k):
                    if k == 0:
                        pe.wait_ge(s.shift_ready, h + 1)
                    if h + k:
                        pe.wait_ge(s.exp_ready, NT * h + k)
                    for lo, hi_ in halves(k * P, T):
                        out, keys = bank(m.ps, 0, lo, hi_), kst[:, h % RK, k * P:(k + 1) * P]
                        pe.matmul(out, keys, qst[:, h % RK, lo:hi_], start=True, stop=False)
                        pe.matmul(out, keys, qlo[:, h % RK, lo:hi_], start=False, stop=False)
                        if lo == k * P:
                            pe.matmul(bank(m.ps, 0, lo, lo + P), m.ident16[:, :], m.mask_kq[:, :], start=False, stop=False)
                        last = pe.matmul(out, m.negones[:, :], shift[:, h % 2, lo:hi_], start=False, stop=True)
                    last.then_inc(s.score_mm, 1)

                def weighted(h, k):
                    pe.wait_ge(s.exp_ready, NT * h + k + 1)
                    if k == 0 and h:
                        pe.wait_ge(s.o_ready, h)
                    for lo, hi_ in halves(k * P, T):
                        last = pe.matmul(bank(m.ps, 4, lo, hi_), vx[:, k, h, :], prob[:, k % 2, lo:hi_], start=(k == 0),
                                         stop=True, skip_group_check=True)
                    last.then_inc(s.pv_mm, 1)

                for step in range(H0 + 2):
                    h0, h1, h2 = step, step - 1, step - 2
                    for k in range(NT):
                        if h2 >= 0:
                            scores(h2, k)
                        if h0 < H0 and k in (0, 1):
                            if h0:
                                pe.wait_ge(s.q_ready, 2 * (h0 - 1) + k + 1)
                            project(h0, wk, k, s.k_mm)
                        if h0 < H0 and k in (3, 4):
                            pe.wait_ge(s.k_ready, 2 * h0 + k - 3 + 1)
                            project(h0, wq, k - 3, s.q_mm)
                        if 0 <= h1 < H0:
                            maxima(h1, k)
                        if h2 >= 0 and k >= 1:
                            weighted(h2, k - 1)
                    if h2 >= 0:
                        weighted(h2, NT - 1)

            @block.scalar
            def _(act):
                def k_hi(h, n):
                    act.wait_ge(s.k_mm, 2 * h + n + 1)
                    if h:
                        act.wait_ge(s.k_ready, 2 * (h - 1) + n + 1)
                    act.copy(hi[:, n, :], bank(m.ps, 6 + n)).then_inc(s.k_hi, 1)

                def q_hi(h, n):
                    act.wait_ge(s.q_mm, 2 * h + n + 1)
                    if h >= RK:
                        act.wait_ge(s.score_mm, NT * (h - RK + 1))
                    act.copy(qst[:, h % RK, n * HALF:(n + 1) * HALF], bank(m.ps, 6 + n)).then_inc(s.q_hi, 1)

                for step in range(H0 + 2):
                    h0, h2 = step, step - 2
                    if step == 1:
                        fetch_sd(act, m, s)
                    for k in range(NT):
                        if h2 >= 0:
                            act.wait_ge(s.score_mm, NT * h2 + k + 1)
                            if NT * h2 + k >= 2:
                                act.wait_ge(s.pv_mm, NT * h2 + k - 1)
                            act.activation(prob[:, k % 2, k * P:T], bank(m.ps, 0, k * P, T), ACT.Exp,
                                           scale=SCALE0).then_inc(s.exp_ready, 1)
                        if h0 < H0 and k in (0, 1):
                            k_hi(h0, k)
                        if h0 < H0 and k in (3, 4):
                            q_hi(h0, k - 3)

            @block.vector
            def _(dve):
                for step in range(H0 + 2):
                    h0, h1, h2 = step, step - 1, step - 2
                    if step == 1:
                        fetch_stats(dve, m, s)
                    if step == 2:
                        fetch_norm(dve, m, s)
                    for k in range(NT):
                        if h0 < H0 and k in (0, 1):
                            cols = slice(k * HALF, (k + 1) * HALF)
                            dve.wait_ge(s.k_hi, 2 * h0 + k + 1)
                            if h0 >= RK:
                                dve.wait_ge(s.score_mm, NT * (h0 - RK + 1))
                            dve.scalar_tensor_tensor(kst[:, h0 % RK, cols], hi[:, k, :].bitcast(F32), klo[:, 0:1],
                                                     bank(m.ps, 6 + k), ALU.mult, ALU.add).then_inc(s.k_ready, 1)
                        if h0 < H0 and k in (3, 4):
                            n = k - 3
                            cols = slice(n * HALF, (n + 1) * HALF)
                            dve.wait_ge(s.q_hi, 2 * h0 + n + 1)
                            dve.tensor_tensor(qlo[:, h0 % RK, cols], bank(m.ps, 6 + n),
                                              qst[:, h0 % RK, cols].bitcast(F32), ALU.subtract).then_inc(s.q_ready, 1)
                        if 0 <= h1 < H0:
                            dve.wait_ge(s.max_mm, NT * h1 + k + 1)
                            dve.reduce_max(mx[:, h1, k:k + 1], bank(m.ps, 2, 0, (k + 1) * P), AX_X).then_inc(s.max_read, 1)
                    if h2 >= 0:
                        num, den = vcol(h2), ones(h2)
                        dve.wait_ge(s.pv_mm, NT * h2 + NT)
                        dve.reciprocal(rden[num, :], bank(m.ps, 4, 0, T, den)).then_inc(s.rden, 1)
                        dve.wait_ge(s.rden, h2 + 1)
                        dve.tensor_tensor(oT[num, h2 // 2, :], bank(m.ps, 4, 0, T, num), rden[num, :],
                                          ALU.mult).then_inc(s.o_ready, 1)

            @block.sync
            def _(sp):
                fetch_load(sp, m, s, src[(b + 1) % SEQS])

            @block.gpsimd
            def _(pool):
                clear(pool, s1)
                for h in range(H0):
                    pool.wait_ge(s.max_read, NT * (h + 1))
                    if h >= 2:
                        pool.wait_ge(s.score_mm, NT * (h - 1))
                    pool.tensor_tensor(shift[:, h % 2, :].rearrange("p (t q) -> p t q", t=NT),
                                       m.ident[:, :].unsqueeze(1).to_broadcast([P, NT, P]),
                                       mx[:, h, :].unsqueeze(2).to_broadcast([P, NT, P]), ALU.mult).then_inc(s.shift_ready, 1)

    def output_experts(own, b):
        sb = lambda name, shape, dt=F32: own.enter_context(nc.sbuf_tensor("l2c_" + name, shape, dt))
        sel = sb("sel", [P, H0 // 2 * NE, P], F32R)
        oe = sb("oe", [P, 2, NE, D])
        RT = 4
        routed = sb("routed", [P, RT, HALF])
        y = sb("y", [P, NT, D])
        AHEAD = 2
        blocks = [(c, e, n) for c in range(H0 // 2) for e in range(NE) for n in range(NH)]
        per_c = NE * NH
        s = s3
        with nc.Block() as block:
            @block.sync
            def _(sp):
                for c in range(H0 // 2):
                    if c >= 2:
                        sp.wait_ge(s.out_mm, per_c * (c - 1))
                    sp.dma_start(oe[:, c % 2, :, :], I["oe2"][:, c]).then_inc((s.even_oe_in, s.odd_oe_in)[c % 2], 16)
                store(sp, s, y, dst[b])

            @block.gpsimd
            def _(pool):
                clear(pool, s2)

            @block.vector
            def _(dve):
                for c in range(H0 // 2):
                    cols = slice(c * NE * 2, (c + 1) * NE * 2)
                    dve.tensor_copy(sel[:, c * NE:(c + 1) * NE, :].rearrange("p n (a k) -> p (n a) k", a=2),
                                    pick[:, cols].unsqueeze(2).to_broadcast([P, NE * 2, DH0])).then_inc(s.sel_ready, 1)
                for i, (c, e, n) in enumerate(blocks):
                    dve.wait_ge(s.mask_mm, i + 1)
                    if i >= RT:
                        dve.wait_ge(s.out_mm, i - RT + 1)
                    dve.tensor_tensor(routed[:, i % RT, :], oT[:, c, n * HALF:(n + 1) * HALF], bank(m.ps, 4 + i % 4),
                                      ALU.mult).then_inc(s.routed, 1)
                dve.wait_ge(s.out_mm, len(blocks))
                for t in range(NT):
                    dve.tensor_tensor(y[:, t, :], m.x[:, t, :], m.ps[:, t * D:(t + 1) * D], ALU.add).then_inc(s.y_ready, 1)

            @block.tensor
            def _(pe):
                for i in range(len(blocks) + AHEAD):
                    if i < len(blocks):
                        c, e, n = blocks[i]
                        pe.wait_ge(s.sel_ready, c + 1)
                        if i >= 4:
                            pe.wait_ge(s.routed, i - 3)
                        pe.matmul(bank(m.ps, 4 + i % 4), sel[:, c * NE + e, :], gmT[:, n * HALF:(n + 1) * HALF],
                                  start=True, stop=True).then_inc(s.mask_mm, 1)
                    if i >= AHEAD:
                        c, e, n = blocks[i - AHEAD]
                        pe.wait_ge((s.even_oe_in, s.odd_oe_in)[c % 2], 16 * (c // 2 + 1))
                        pe.wait_ge(s.routed, i - AHEAD + 1)
                        for j in range(HALF // P):
                            t = n * (HALF // P) + j
                            last = pe.matmul(m.ps[:, t * D:(t + 1) * D], routed[:, (i - AHEAD) % RT, j * P:(j + 1) * P],
                                             oe[:, c % 2, e, :], start=(c == e == 0 and t % 2 == 0),
                                             stop=(c == H0 // 2 - 1 and e == NE - 1), skip_group_check=True)
                        last.then_inc(s.out_mm, 1)

    fetch_first(nc, m, s0, src[0])
    with nc.Fori(0, SEQS) as b:
        with ExitStack() as own:
            gates_and_values(own)
        with ExitStack() as own:
            attention(own, b)
        with ExitStack() as own:
            output_experts(own, b)

    return ld, s0, s1, s2, s3



PROJ3 = ("transposed xT_ready x_copied qk_mm z_ready stack_ready h_mm v_mm v_read chain var_ready sd_ready hn_ready gelu_ready drift_ready "
         "g_ready g_gelu gate_in gate_ready vx_ready")
ATTN3 = "max_mm max_read shift_ready score_mm exp_ready pv_mm o_read" + FETCH
OUT3 = "bias_added turned rden o_ready turned_back oT_ready out_mm y_ready y_out"


def layer3(nc, ctx, m, I, src, dst):
    sb = lambda name, shape, dt=F32: ctx.enter_context(nc.sbuf_tensor("l3_" + name, shape, dt))
    GROUPS = H1 // G1
    R = 4 * DH1
    HPC = P // R
    QC = H1 // HPC
    HF = 128
    GF = 16
    wq, wk, wv, wo = sb("wq", [P, KC, QC * P]), sb("wk", [P, KC, QC * P]), sb("wv", [P, KC, D]), sb("wo", [P, KC, D])
    bq, bk, bv, bo = sb("bq", [P, QC]), sb("bk", [P, QC]), sb("bv", [P, D]), sb("bo", [P, D])
    w1 = sb("w1", [P, KC, HF])
    hv = sb("hv", [P, 4, HF])
    gv = sb("gv", [P, 3, GF])
    b2 = sb("b2", [P, 2])
    qneg, kneg = sb("qneg", [P, 1]), sb("kneg", [P, 1])
    qst, kst = sb("qst", [P, QC, T], F32R), sb("kst", [P, QC, T], F32R)
    vx = sb("vx", [P, NT, H1, 2 * DH1])
    ld = signals(nc, ctx, "l3_load", "weights ones")
    s0 = signals(nc, ctx, "l3_first", FETCH)
    s1 = signals(nc, ctx, "l3_proj", PROJ3)
    s2 = signals(nc, ctx, "l3_attn", ATTN3)
    s3 = signals(nc, ctx, "l3_out", OUT3)

    with nc.Block() as block:
        @block.sync
        def _(sp):
            pairs = [(wq, "wq3"), (wk, "wk3"), (wv, "wv3"), (wo, "wo3"), (bq, "bq3"), (bk, "bk3"), (bv, "bv3"), (bo, "bo3"),
                     (w1, "w13"), (hv, "hv3"), (gv, "gv3"), (b2, "b23"), (qneg, "qneg3"), (kneg, "kneg3")]
            for tile, name in pairs:
                sp.dma_start(tile[:], I[name]).then_inc(ld.weights, 16)
            sp.wait_ge(ld.weights, 16 * len(pairs))

        @block.vector
        def _(dve):
            dve.memset(vx[:, :, :, :], 1.0).then_inc(ld.ones, 1)

    def projections(own):
        sb = lambda name, shape, dt=F32: own.enter_context(nc.sbuf_tensor("l3a_" + name, shape, dt))
        xT = sb("xT", [P, KC, T])
        RZ = 4
        z, zhi = sb("z", [P, RZ, HALF]), sb("zhi", [P, RZ, HALF], F32R)
        v = sb("v", [P, NT, D])
        h = sb("h", [P, NT, HF])
        g = sb("g", [P, NT, GF])
        st, mom, sd, r = sb("st", [P, NT, 6]), sb("mom", [P, NT, 2]), sb("sd", [P, NT]), sb("r", [P, NT])
        drift, gate = sb("drift", [P, NT]), sb("gate", [P, NT])
        items = [(c, n, kind) for c in range(QC) for n in range(NH) for kind in "qk"]
        s = s1
        with nc.Block() as block:
            @block.tensor
            def _(pe):
                entry_transpose(pe, m, s)
                for t in range(NT):
                    pe.wait_ge(s.xT_ready, t + 1)
                    for c in range(KC):
                        last = pe.matmul(bank(m.ps, 4, t * HF, (t + 1) * HF), xT[:, c, t * P:(t + 1) * P], w1[:, c, :],
                                         start=(c == 0), stop=(c == KC - 1))
                    last.then_inc(s.h_mm, 1)
                for t in range(NT):
                    if t >= 2:
                        pe.wait_ge(s.v_read, t - 1)
                    for c in range(KC):
                        last = pe.matmul(bank(m.ps, 6 + t % 2, 0, D), xT[:, c, t * P:(t + 1) * P], wv[:, c, :],
                                         start=(c == 0), stop=(c == KC - 1))
                    last.then_inc(s.v_mm, 1)
                for i, (q, n, kind) in enumerate(items):
                    if i >= 4:
                        pe.wait_ge(s.z_ready, i - 3)
                    w = wq if kind == "q" else wk
                    for c in range(KC):
                        last = pe.matmul(bank(m.ps, i % 4), w[:, c, q * P:(q + 1) * P], xT[:, c, n * HALF:(n + 1) * HALF],
                                         start=(c == 0), stop=(c == KC - 1))
                    last.then_inc(s.qk_mm, 1)

            @block.scalar
            def _(act):
                entry_copy(act, m, s, xT)
                act.wait_ge(s.var_ready, NT)
                act.activation(sd[:, :], mom[:, :, 1], ACT.Sqrt, bias=m.eps[:, 0:1]).then_inc(s.sd_ready, 1)
                act.wait_ge(s.hn_ready, 1)
                act.activation(h[:, :, :], h[:, :, :], ACT.Gelu).then_inc(s.gelu_ready, 1)
                act.wait_ge(s.g_ready, 1)
                act.activation(g[:, :, :], g[:, :, :], ACT.Gelu).then_inc(s.g_gelu, 1)
                act.wait_ge(s.gate_in, 1)
                act.activation(gate[:, :], drift[:, :], ACT.Tanh, bias=b2[:, 1:2]).then_inc(s.gate_ready, 1)
                for i, (q, n, kind) in enumerate(items):
                    act.wait_ge(s.qk_mm, i + 1)
                    if i >= RZ:
                        act.wait_ge(s.stack_ready, i - RZ + 1)
                    for out in (zhi, z):
                        last = act.activation(out[:, i % RZ, :], bank(m.ps, i % 4), ACT.Identity,
                                              bias=(bq if kind == "q" else bk)[:, q:q + 1])
                    last.then_inc(s.z_ready, 1)

            @block.gpsimd
            def _(pool):
                clear(pool, s3)
                entry_residual(pool, m, s)

            @block.vector
            def _(dve):
                step = Chain(dve, s.chain)
                over_t = lambda row, w: row.unsqueeze(1).to_broadcast([P, NT, w])
                over_f = lambda col, w: col.unsqueeze(2).to_broadcast([P, NT, w])
                dve.wait_ge(s.h_mm, NT)
                step(dve.tensor_tensor(h[:, :, :], bank(m.ps, 4, 0, NT * HF).rearrange("p (t f) -> p t f", t=NT),
                                       over_t(hv[:, 0, :], HF), ALU.add))
                for t in range(NT):
                    last = dve.bn_stats(st[:, t, :], h[:, t, :])
                step(last)
                for t in range(NT):
                    dve.bn_aggr(mom[:, t, :], st[:, t, :]).then_inc(s.var_ready, 1)
                dve.wait_ge(s.sd_ready, 1)
                inverse_sd(step, dve, m, r[:, :], mom[:, :, 1], sd[:, :])
                step(dve.tensor_tensor(h[:, :, :], h[:, :, :], over_f(mom[:, :, 0], HF), ALU.subtract))
                step(dve.tensor_tensor(h[:, :, :], h[:, :, :], over_f(r[:, :], HF), ALU.mult))
                step(dve.tensor_tensor(h[:, :, :], h[:, :, :], over_t(hv[:, 1, :], HF), ALU.mult))
                dve.tensor_tensor(h[:, :, :], h[:, :, :], over_t(hv[:, 2, :], HF), ALU.add).then_inc(s.hn_ready, 1)
                for t in range(NT):
                    dve.wait_ge(s.v_mm, t + 1)
                    dve.tensor_tensor(v[:, t, :], bank(m.ps, 6 + t % 2, 0, D), bv[:, :], ALU.add).then_inc(s.v_read, 1)
                dve.wait_ge(s.gelu_ready, 1)
                step(dve.tensor_tensor(h[:, :, :], h[:, :, :], over_t(hv[:, 3, :], HF), ALU.mult))
                step(dve.tensor_reduce(drift[:, :], h[:, :, :], AX_X, ALU.add))
                step(dve.tensor_scalar(drift[:, :], drift[:, :], b2[:, 0:1], None, ALU.add))
                step(dve.tensor_tensor(g[:, :, :], over_f(drift[:, :], GF), over_t(gv[:, 0, :], GF), ALU.mult))
                dve.tensor_tensor(g[:, :, :], g[:, :, :], over_t(gv[:, 1, :], GF), ALU.add).then_inc(s.g_ready, 1)
                dve.wait_ge(s.g_gelu, 1)
                step(dve.tensor_tensor(g[:, :, :], g[:, :, :], over_t(gv[:, 2, :], GF), ALU.mult))
                dve.tensor_reduce(drift[:, :], g[:, :, :], AX_X, ALU.add).then_inc(s.gate_in, 1)
                dve.wait_ge(s.gate_ready, 1)
                dve.wait_ge(s.v_read, NT)
                for t in range(NT):
                    dve.tensor_scalar(vx[:, t, :, 0:DH1], v[:, t, :].rearrange("p (h k) -> p h k", h=H1), gate[:, t:t + 1],
                                      None, ALU.mult).then_inc(s.vx_ready, 1)
                for i, (q, n, kind) in enumerate(items):
                    dve.wait_ge(s.z_ready, i + 1)
                    dve.scalar_tensor_tensor((qst if kind == "q" else kst)[:, q, n * HALF:(n + 1) * HALF],
                                             zhi[:, i % RZ, :].bitcast(F32), (qneg if kind == "q" else kneg)[:, 0:1],
                                             z[:, i % RZ, :], ALU.mult, ALU.add).then_inc(s.stack_ready, 1)

    def attention(own, oraw, b):
        sb = lambda name, shape, dt=F32: own.enter_context(nc.sbuf_tensor("l3b_" + name, shape, dt))
        shift = sb("shift", [P, 2, G1, T], F32R)
        prob = sb("prob", [P, 2, G1, T])
        mx = sb("mx", [P, H1, NT])
        s = s2
        WIDE = HALF // P
        units = [(k, (i,)) for k in range(WIDE) for i in range(G1)] + \
                [(k, (i, i + 1)) for k in range(WIDE, NT) for i in range(0, G1, 2)]
        U = len(units)

        def through(k):
            return sum(kk <= k for kk, _ in units)

        def rows(h):
            return slice(R * (h % HPC), R * (h % HPC) + R)

        def region(first, heads, lo, hi):
            if len(heads) == 1:
                return bank(m.ps, first, lo, hi)
            return m.ps[:, first * HALF:(first + 2) * HALF].rearrange("p (a n) -> p a n", a=2)[:, :, lo % HALF:lo % HALF + hi - lo]

        def max_banks(g, n):
            return (2, 4, 6)[n % 3] if g == 0 else 6

        with nc.Block() as block:
            @block.sync
            def _(sp):
                fetch_load(sp, m, s, src[(b + 1) % SEQS])

            @block.tensor
            def _(pe):
                def maxima(g, n, k, heads):
                    t = NT - 1 - k
                    if g == 0 and n >= 3:
                        pe.wait_ge(s.max_read, n - 2)
                    elif g:
                        pe.wait_ge(s.max_read, n)
                    for j, i in enumerate(heads):
                        h, rr = G1 * g + i, rows(G1 * g + i)
                        at = max_banks(g, n) + j
                        for lo, hi in halves(0, (t + 1) * P):
                            pe.matmul(bank(m.ps, at, lo, hi), qst[rr, h // HPC, t * P:(t + 1) * P], kst[rr, h // HPC, lo:hi],
                                      start=True, stop=True)
                        last = pe.matmul(bank(m.ps, at, t * P, (t + 1) * P), m.ident16[:, :], m.mask_qk[:, :],
                                         start=False, stop=True, skip_group_check=True)
                    last.then_inc(s.max_mm, 1)

                def scores(g, n, k, heads):
                    if n >= 2:
                        pe.wait_ge(s.exp_ready, n - 1)
                    if n % U == 0:
                        pe.wait_ge(s.shift_ready, U * (g + 1))
                    for j, i in enumerate(heads):
                        h, rr = G1 * g + i, rows(G1 * g + i)
                        for lo, hi in halves(k * P, T):
                            at = (2 + 2 * (n % 2) + j) * HALF - (HALF if len(heads) == 2 else 0)
                            out = m.ps[:, at + lo:at + hi]
                            pe.matmul(out, kst[rr, h // HPC, k * P:(k + 1) * P], qst[rr, h // HPC, lo:hi], start=True, stop=False)
                            if lo == k * P:
                                pe.matmul(m.ps[:, at + lo:at + lo + P], m.ident16[:, :], m.mask_kq[:, :], start=False, stop=False)
                            last = pe.matmul(out, m.negones[:, :], shift[:, g % 2, i, lo:hi], start=False, stop=True)
                    last.then_inc(s.score_mm, 1)

                def weighted(g, k):
                    pe.wait_ge(s.exp_ready, U * g + through(k))
                    if k == 0 and g:
                        pe.wait_ge(s.o_read, g)
                    for lo, hi in halves(k * P, T):
                        for i in range(G1):
                            last = pe.matmul(bank(m.ps, 0, lo, hi, slice(32 * i, 32 * i + 32)), vx[:, k, G1 * g + i, :],
                                             prob[:, k % 2, i, lo:hi], start=(k == 0), stop=True, skip_group_check=True)
                    last.then_inc(s.pv_mm, 1)

                for g in range(GROUPS + 1):
                    for n, (k, heads) in enumerate(units):
                        if g >= 1:
                            scores(g - 1, U * (g - 1) + n, k, heads)
                        if g < GROUPS:
                            maxima(g, U * g + n, k, heads)
                        if g >= 1 and k >= 1 and 1 in heads:
                            weighted(g - 1, k - 1)
                    if g >= 1:
                        weighted(g - 1, NT - 1)

            @block.scalar
            def _(act):
                for g in range(GROUPS):
                    if g == 1:
                        fetch_sd(act, m, s)
                    for n, (k, heads) in enumerate(units, U * g):
                        act.wait_ge(s.score_mm, n + 1)
                        if heads[0] == 0 and NT * g + k >= 2:
                            act.wait_ge(s.pv_mm, NT * g + k - 1)
                        out = prob[:, k % 2, heads[0], k * P:T] if len(heads) == 1 else prob[:, k % 2, heads[0]:heads[0] + 2, k * P:T]
                        act.activation(out, region(2 + 2 * (n % 2), heads, k * P, T), ACT.Exp, scale=SCALE1).then_inc(s.exp_ready, 1)

            @block.vector
            def _(dve):
                def group_out(g):
                    dve.wait_ge(s.pv_mm, NT * (g + 1))
                    dve.tensor_copy(oraw[:, g, :], bank(m.ps, 0, 0, T)).then_inc(s.o_read, 1)

                for g in range(GROUPS):
                    for n, (k, heads) in enumerate(units, U * g):
                        if g == 0 and n == 4:
                            fetch_stats(dve, m, s)
                        if g == 2 and n == U * g + 4:
                            fetch_norm(dve, m, s)
                        t, h = NT - 1 - k, G1 * g + heads[0]
                        dve.wait_ge(s.max_mm, n + 1)
                        out = mx[:, h, t:t + 1] if len(heads) == 1 else mx[:, h:h + 2, t]
                        dve.reduce_max(out, region(max_banks(g, n), heads, 0, (t + 1) * P), AX_X).then_inc(s.max_read, 1)
                        if g >= 2 and n == U * g:
                            group_out(g - 2)
                for g in range(GROUPS - 2, GROUPS):
                    group_out(g)

            @block.gpsimd
            def _(pool):
                clear(pool, s1)
                for g in range(GROUPS):
                    if g >= 2:
                        pool.wait_ge(s.score_mm, U * (g - 1))
                    for n, (k, heads) in enumerate(units, U * g):
                        t = NT - 1 - k
                        pool.wait_ge(s.max_read, n + 1)
                        for i in heads:
                            last = pool.tensor_scalar(shift[:, g % 2, i, t * P:(t + 1) * P], m.ident[:, :],
                                                      mx[:, G1 * g + i, t:t + 1], None, ALU.mult)
                        last.then_inc(s.shift_ready, 1)

    def output(own, oraw, b):
        sb = lambda name, shape, dt=F32: own.enter_context(nc.sbuf_tensor("l3c_" + name, shape, dt))
        y = sb("y", [P, NT, D])
        rden = sb("rden", [P, 2, H1])
        o = sb("o", [P, 2, D])
        oT = sb("oT", [P, 2, KC, P])
        s = s3
        with nc.Block() as block:
            @block.tensor
            def _(pe):
                for step in range(NT + 2):
                    if step < NT:
                        t = step
                        if t >= 2:
                            pe.wait_ge(s.o_ready, t - 1)
                        for g in range(GROUPS):
                            last = pe.transpose(bank(m.ps, t % 2, g * P, (g + 1) * P), oraw[:, g, t * P:(t + 1) * P], m.ident[:, :])
                        last.then_inc(s.turned, 1)
                    if 1 <= step <= NT:
                        t = step - 1
                        pe.wait_ge(s.o_ready, t + 1)
                        if t >= 2:
                            pe.wait_ge(s.oT_ready, t - 1)
                        for c in range(KC):
                            last = pe.transpose(bank(m.ps, 2 + t % 2, c * P, (c + 1) * P), o[:, t % 2, c * P:(c + 1) * P], m.ident[:, :])
                        last.then_inc(s.turned_back, 1)
                    if step >= 2:
                        t = step - 2
                        pe.wait_ge(s.oT_ready, t + 1)
                        if t >= 2:
                            pe.wait_ge(s.y_ready, t - 1)
                        for c in range(KC):
                            last = pe.matmul(bank(m.ps, 4 + t % 2, 0, D), oT[:, t % 2, c, :], wo[:, c, :],
                                             start=(c == 0), stop=(c == KC - 1))
                        last.then_inc(s.out_mm, 1)

            @block.scalar
            def _(act):
                for t in range(NT):
                    act.wait_ge(s.turned_back, t + 1)
                    if t >= 2:
                        act.wait_ge(s.out_mm, t - 1)
                    act.copy(oT[:, t % 2, :, :], bank(m.ps, 2 + t % 2, 0, D).rearrange("p (c q) -> p c q", c=KC)).then_inc(s.oT_ready, 1)

            @block.vector
            def _(dve):
                dve.tensor_tensor(m.x[:, :, :], m.x[:, :, :], bo[:, :].unsqueeze(1).to_broadcast([P, NT, D]), ALU.add).then_inc(s.bias_added, 1)
                for step in range(NT + 2):
                    if step < NT:
                        t = step
                        heads = bank(m.ps, t % 2).rearrange("p (h k) -> p h k", h=H1)
                        dve.wait_ge(s.turned, t + 1)
                        dve.reciprocal(rden[:, t % 2, :], heads[:, :, DH1]).then_inc(s.rden, 1)
                        dve.wait_ge(s.rden, t + 1)
                        if t >= 2:
                            dve.wait_ge(s.turned_back, t - 1)
                        dve.tensor_tensor(o[:, t % 2, :].rearrange("p (h k) -> p h k", h=H1), heads[:, :, 0:DH1],
                                          rden[:, t % 2, :].unsqueeze(2).to_broadcast([P, H1, DH1]), ALU.mult).then_inc(s.o_ready, 1)
                    if step >= 2:
                        t = step - 2
                        dve.wait_ge(s.bias_added, 1)
                        dve.wait_ge(s.out_mm, t + 1)
                        dve.tensor_tensor(y[:, t, :], bank(m.ps, 4 + t % 2, 0, D), m.x[:, t, :], ALU.add).then_inc(s.y_ready, 1)

            @block.gpsimd
            def _(pool):
                clear(pool, s2)

            @block.sync
            def _(sp):
                store(sp, s, y, dst[b])

    fetch_first(nc, m, s0, src[0])
    with nc.Fori(0, SEQS) as b:
        with ExitStack() as own:
            projections(own)
        with ExitStack() as own:
            oraw = own.enter_context(nc.sbuf_tensor("l3_oraw", [P, GROUPS, T], F32))
            with ExitStack() as inner:
                attention(inner, oraw, b)
            with ExitStack() as inner:
                output(inner, oraw, b)

    return ld, s0, s1, s2, s3



CHECK4 = "w1_in w2_in h1_in h2_in w3_in scales_in rounded compared worst total flag_ready"
NET4 = ("mm silu_ready mul_ready gelu_ready hi_ready h_ready out_mm scaled y_ready y_out x_hi "
        "y_stats y_moments y_sd y_chain" + ENTRY + FETCH)
WEIGHTS4 = [("w14", KC, HID), ("w24", KC, HID), ("h14", HC, HID), ("h24", HC, HID), ("w34", HC, D)]


def layer4(nc, ctx, m, I, src, dst):
    sb = lambda name, shape, dt=F32: ctx.enter_context(nc.sbuf_tensor("l4_" + name, shape, dt))
    weights = [sb(name, [P, c, n], F32R) for name, c, n in WEIGHTS4]
    w1, w2, h1, h2, w3 = weights
    scale = sb("scale", [P, 4, HC])
    s3v = sb("s3", [P, D])
    flag = sb("flag", [1, 1], mybir.dt.int32)
    ld = signals(nc, ctx, "l4_check", CHECK4)
    s0 = signals(nc, ctx, "l4_first", FETCH)
    s1 = signals(nc, ctx, "l4_net", NET4)

    with ExitStack() as own:
        own_sb = lambda name, shape, dt=F32: own.enter_context(nc.sbuf_tensor("l4c_" + name, shape, dt))
        W = 2048
        chunks = []
        for n, (name, c, cols) in enumerate(WEIGHTS4):
            chunks += [(n, lo) for lo in range(0, c * cols, W)]
        rounded, differs = own_sb("rounded", [P, 2, W], F32R), own_sb("differs", [P, 2, W])
        worst = own_sb("worst", [P, len(chunks) + 1])
        ones = own_sb("ones", [P, 1])
        arrived = (ld.w1_in, ld.w2_in, ld.h1_in, ld.h2_in, ld.w3_in)
        flat = lambda n: weights[n][:, :, :].rearrange("p c n -> p (c n)").bitcast(F32)
        with nc.Block() as block:
            @block.sync
            def _(sp):
                sp.wait_ge(m.weights_copied, 16 * len(WEIGHTS4))
                for n in range(len(WEIGHTS4)):
                    sp.dma_start(flat(n), m.weight_copies[n].rearrange("p c n -> p (c n)")).then_inc(arrived[n], 16)
                sp.dma_start(scale[:], I["scale4"]).then_inc(ld.scales_in, 16)
                sp.dma_start(s3v[:], I["s34"]).then_inc(ld.scales_in, 16)
                sp.wait_ge(ld.scales_in, 32)

            @block.scalar
            def _(act):
                for k, (n, lo) in enumerate(chunks):
                    act.wait_ge(arrived[n], 16)
                    if k >= 2:
                        act.wait_ge(ld.compared, k - 1)
                    act.copy(rounded[:, k % 2, :], flat(n)[:, lo:lo + W]).then_inc(ld.rounded, 1)

            @block.vector
            def _(dve):
                dve.memset(ones[:, :], 1.0)
                for k, (n, lo) in enumerate(chunks):
                    dve.wait_ge(ld.rounded, k + 1)
                    dve.wait_ge(arrived[n], 16)
                    if k >= 2:
                        dve.wait_ge(ld.worst, k - 1)
                    dve.tensor_tensor(differs[:, k % 2, :], flat(n)[:, lo:lo + W], rounded[:, k % 2, :].bitcast(F32),
                                      ALU.not_equal).then_inc(ld.compared, 1)
                    dve.wait_ge(ld.compared, k + 1)
                    dve.reduce_max(worst[:, k:k + 1], differs[:, k % 2, :], AX_X).then_inc(ld.worst, 1)
                K = len(chunks)
                dve.wait_ge(ld.worst, K)
                dve.reduce_max(worst[:, K:K + 1], worst[:, 0:K], AX_X).then_inc(ld.worst, 1)
                dve.wait_ge(ld.total, 1)
                dve.tensor_copy(flag[:, :], bank(m.ps, 0, 0, 1, slice(0, 1))).then_inc(ld.flag_ready, 1)

            @block.tensor
            def _(pe):
                pe.wait_ge(ld.worst, len(chunks) + 1)
                pe.matmul(bank(m.ps, 0, 0, 1, slice(0, 1)), worst[:, len(chunks):], ones[:, :], start=True,
                          stop=True).then_inc(ld.total, 1)

    def net(own, b):
        sb = lambda name, shape, dt=F32: own.enter_context(nc.sbuf_tensor("l4a_" + name, shape, dt))
        xhi, xlo = sb("xhi", [P, KC, T], F32R), sb("xlo", [P, KC, T], F32R)
        uhi, ulo = sb("uhi", [P, 2, HC, HALF], F32R), sb("ulo", [P, 2, HC, HALF], F32R)
        RT = 3
        sil, made = sb("sil", [P, 2, HALF]), sb("made", [P, RT, HALF])
        s = s1
        OUTS = HALF // P
        ystats, ymom = sb("ystats", [P, NH, OUTS, 6]), sb("ymom", [P, NH, OUTS, 2])
        ysd, yr = sb("ysd", [P, NH, OUTS]), sb("yr", [P, NH, OUTS])
        per_n = 4 * HC
        RB = 6

        def at(n, stage, o):
            return per_n * n + (2 * o if stage == 0 else 2 * HC + (stage - 1) * HC + o)

        def chunk(n, stage, o):
            return HC * (3 * n + stage) + o

        def slot(n, stage):
            return (3 * n + stage) % 2

        with nc.Block() as block:
            @block.tensor
            def _(pe):
                entry_transpose(pe, m, s)
                misfit = pe.value_load(flag[0:1, 0:1])

                def wait_free(i):
                    n, r = divmod(i - RB, per_n)
                    if r < 2 * HC:
                        pe.wait_ge(s.mul_ready if r % 2 else s.silu_ready, HC * n + r // 2 + 1)
                    else:
                        pe.wait_ge(s.gelu_ready, 2 * HC * n + r - 2 * HC + 1)

                def run(passes):
                    def product(i, w, kc, o, hi, lo, ready=None):
                        if i >= RB:
                            wait_free(i)
                        for c in range(kc):
                            if ready is not None:
                                pe.wait_ge(s.h_ready, ready + c + 1)
                            for part in (hi, lo):
                                last = passes(bank(m.ps, i % RB), w[:, c, o * P:(o + 1) * P], part(c), c == 0 and part is hi,
                                              c == kc - 1 and part is lo)
                        last.then_inc(s.mm, 1)

                    pe.wait_ge(s.xT_ready, NT)
                    for n in range(NH):
                        cols = slice(n * HALF, (n + 1) * HALF)
                        for o in range(HC):
                            for j, w in enumerate((w1, w2)):
                                product(at(n, 0, o) + j, w, KC, o, lambda c: xhi[:, c, cols], lambda c: xlo[:, c, cols])
                        for stage, w in ((1, h1), (2, h2)):
                            u = slot(n, stage - 1)
                            for o in range(HC):
                                product(at(n, stage, o), w, HC, o, lambda c: uhi[:, u, c, :], lambda c: ulo[:, u, c, :],
                                        ready=chunk(n, stage - 1, 0) if o == 0 else None)
                        u = slot(n, 2)
                        for j in range(OUTS):
                            t = n * OUTS + j
                            if t >= 2:
                                pe.wait_ge(s.scaled, t - 1)
                            for c in range(HC):
                                if j == 0:
                                    pe.wait_ge(s.h_ready, chunk(n, 2, c) + 1)
                                for part in (uhi, ulo):
                                    last = passes(bank(m.ps, 6 + t % 2, 0, D), part[:, u, c, j * P:(j + 1) * P], w3[:, c, :],
                                                  c == 0 and part is uhi, c == HC - 1 and part is ulo)
                            last.then_inc(s.out_mm, 1)

                with pe.If(misfit > 0):
                    run(lambda out, a, x, first, last: pe.matmul(out, a.bitcast(F32), x.bitcast(F32), start=first, stop=last))
                with pe.Else():
                    run(lambda out, a, x, first, last: pe.matmul(out, a, x, start=first, stop=last))

            @block.scalar
            def _(act):
                for t in range(NT):
                    act.wait_ge(s.transposed, t + 1)
                    act.copy(xhi[:, :, t * P:(t + 1) * P],
                             bank(m.ps, t % ENTRY_BANKS, 0, D).rearrange("p (c q) -> p c q", c=KC)).then_inc(s.x_hi, 1)
                def hi_part(n, stage, o, ready, count):
                    act.wait_ge(ready, count)
                    k = chunk(n, stage, o)
                    act.copy(uhi[:, slot(n, stage), o, :], made[:, k % RT, :]).then_inc(s.hi_ready, 1)

                for n in range(NH):
                    for o in range(HC + 1):
                        if o < HC:
                            i, k = at(n, 0, o), HC * n + o
                            act.wait_ge(s.mm, i + 1)
                            if k >= 2:
                                act.wait_ge(s.mul_ready, k - 1)
                            act.activation(sil[:, k % 2, :], bank(m.ps, i % RB), ACT.Silu,
                                           scale=scale[:, 0, o:o + 1]).then_inc(s.silu_ready, 1)
                        if o >= 1:
                            hi_part(n, 0, o - 1, s.mul_ready, HC * n + o)
                    for stage in (1, 2):
                        for o in range(HC):
                            i, k = at(n, stage, o), chunk(n, stage, o)
                            act.wait_ge(s.mm, i + 1)
                            act.wait_ge(s.h_ready, k - RT + 1)
                            act.activation(made[:, k % RT, :], bank(m.ps, i % RB), ACT.Gelu,
                                           scale=scale[:, 1 + stage, o:o + 1]).then_inc(s.gelu_ready, 1)
                            hi_part(n, stage, o, s.gelu_ready, HC * (2 * n + stage - 1) + o + 1)
                    if n == 0:
                        fetch_sd(act, m, s)
                    act.wait_ge(s.y_moments, n + 1)
                    act.activation(ysd[:, n, :], ymom[:, n, :, 1], ACT.Sqrt, bias=m.eps[:, 0:1]).then_inc(s.y_sd, 1)

            @block.vector
            def _(dve):
                step = Chain(dve, s.y_chain)

                def split(k, slot_, o):
                    dve.wait_ge(s.hi_ready, k + 1)
                    dve.tensor_tensor(ulo[:, slot_, o, :], made[:, k % RT, :], uhi[:, slot_, o, :].bitcast(F32),
                                      ALU.subtract).then_inc(s.h_ready, 1)

                def outputs(n):
                    for j in range(OUTS):
                        t = n * OUTS + j
                        dve.wait_ge(s.out_mm, t + 1)
                        dve.tensor_tensor(made[:, j % RT, 0:D], bank(m.ps, 6 + t % 2, 0, D), s3v[:, :], ALU.mult).then_inc(s.scaled, 1)
                        dve.wait_ge(s.scaled, t + 1)
                        step(dve.tensor_tensor(m.x[:, t, :], made[:, j % RT, 0:D], m.x[:, t, :], ALU.add))
                        last = dve.bn_stats(ystats[:, n, j, :], m.x[:, t, :])
                    last.then_inc(s.y_stats, 1)
                    dve.wait_ge(s.y_stats, n + 1)
                    for j in range(OUTS):
                        last = dve.bn_aggr(ymom[:, n, j, :], ystats[:, n, j, :])
                    last.then_inc(s.y_moments, 1)

                def normed(n):
                    dve.wait_ge(s.y_sd, n + 1)
                    inverse_sd(step, dve, m, yr[:, n, :], ymom[:, n, :, 1], ysd[:, n, :])
                    for j in range(OUTS):
                        t = n * OUTS + j
                        dve.tensor_scalar(m.x[:, t, :], m.x[:, t, :], ymom[:, n, j, 0:1], yr[:, n, j:j + 1], ALU.subtract,
                                          ALU.mult).then_inc(s.y_ready, 1)

                for t in range(NT):
                    dve.wait_ge(s.x_hi, t + 1)
                    cols = slice(t * P, (t + 1) * P)
                    dve.tensor_tensor(xlo[:, :, cols], bank(m.ps, t % ENTRY_BANKS, 0, D).rearrange("p (c q) -> p c q", c=KC),
                                      xhi[:, :, cols].bitcast(F32), ALU.subtract).then_inc(s.xT_ready, 1)
                dve.wait_ge(s.x_copied, 1)
                for n in range(NH):
                    for o in range(HC + 1):
                        if o < HC:
                            i, k = at(n, 0, o) + 1, chunk(n, 0, o)
                            dve.wait_ge(s.mm, i + 1)
                            dve.wait_ge(s.silu_ready, HC * n + o + 1)
                            if k >= RT:
                                dve.wait_ge(s.h_ready, k - RT + 1)
                            dve.scalar_tensor_tensor(made[:, k % RT, :], bank(m.ps, i % RB), scale[:, 1, o:o + 1],
                                                     sil[:, (HC * n + o) % 2, :], ALU.mult, ALU.mult).then_inc(s.mul_ready, 1)
                        if o >= 1:
                            split(chunk(n, 0, o - 1), slot(n, 0), o - 1)
                        if n == 1 and o == 1:
                            normed(0)
                            fetch_norm(dve, m, s)
                    for stage in (1, 2):
                        for o in range(HC):
                            split(chunk(n, stage, o), slot(n, stage), o)
                        if n == 0 and stage == 1:
                            fetch_stats(dve, m, s)
                    outputs(n)
                normed(NH - 1)

            @block.gpsimd
            def _(pool):
                entry_residual(pool, m, s)

            @block.sync
            def _(sp):
                sp.wait_ge(s.transposed, NT)
                sp.wait_ge(s.x_copied, 1)
                fetch_load(sp, m, s, src[(b + 1) % SEQS])
                store(sp, s, m.x, dst[b])

    fetch_first(nc, m, s0, src[0])
    with nc.Fori(0, SEQS) as b:
        with ExitStack() as own:
            net(own, b)
        with nc.Block() as block:
            @block.gpsimd
            def _(pool):
                clear(pool, s1)

    return ld, s0, s1



def program(nc, I, layers, src, scratch):
    with ExitStack() as ctx:
        sb = lambda name, shape, dt=F32: ctx.enter_context(nc.sbuf_tensor("sb_" + name, shape, dt))
        m = Memory(nc, ctx)
        mask_kq, mask_qk = sb("mask_kq32", [P, P]), sb("mask_qk32", [P, P])
        ld = signals(nc, ctx, "load", "consts made")
        with nc.Block() as block:
            @block.sync
            def _(sp):
                for tile, name in ((m.ident, "ident"), (mask_kq, "mask_kq"), (mask_qk, "mask_qk")):
                    sp.dma_start(tile[:, :], I[name]).then_inc(ld.consts, 16)
                sp.wait_ge(ld.consts, 48)

            @block.vector
            def _(dve):
                dve.memset(m.eps[:, :], EPS).then_inc(ld.made, 1)
                dve.memset(m.x[:, 0, 0:P], -1.0).then_inc(ld.made, 1)
                dve.wait_ge(ld.made, 2)
                dve.tensor_copy(m.negones[:, :], m.x[:, 0, 0:P]).then_inc(ld.made, 1)
                dve.wait_ge(ld.consts, 48)
                dve.tensor_copy(m.ident16[:, :], m.ident[:, :]).then_inc(ld.made, 1)
                dve.tensor_copy(m.mask_kq[:, :], mask_kq[:, :]).then_inc(ld.made, 1)
                dve.tensor_copy(m.mask_qk[:, :], mask_qk[:, :]).then_inc(ld.made, 1)

        m.weights_copied = ctx.enter_context(nc.semaphore("weights_copied"))
        m.weight_copies = [nc.dram_tensor("copy_" + name, (P, c, n), F32, kind="Internal").ap() for name, c, n in WEIGHTS4]
        with nc.Block() as block:
            @block.sync
            def _(sp):
                if layer4 in layers:
                    for copy, (name, _c, _n) in zip(m.weight_copies, WEIGHTS4):
                        sp.dma_start(copy, I[name]).then_inc(m.weights_copied, 16)

        rows = lambda dram: dram.rearrange("(b t p) d -> b p t d", b=SEQS, p=P)
        here = src
        for layer, there in zip(layers, scratch):
            with ExitStack() as own:
                used = layer(nc, own, m, I, rows(here), rows(there))
                with nc.Block() as block:
                    @block.gpsimd
                    def _(pool):
                        for stage in used:
                            clear(pool, stage)
            here = there



def lay(w):
    return w.reshape(w.shape[0] // P, P, -1).transpose(1, 0, 2)


def by_partition(v):
    return v.reshape(-1, P).T


def to_all(v):
    return np.broadcast_to(v.reshape(1, -1), (P, v.size))


def constants():
    k, q = np.meshgrid(np.arange(P), np.arange(P), indexing="ij")
    hidden = np.float32(-2.0 ** 100)
    return {
        "ident": np.eye(P, dtype=np.float32), "mask_kq": np.where(q < k, hidden, np.float32(0.0)),
        "mask_qk": np.where(k < q, hidden, np.float32(0.0)),
    }


def layout1(i):
    return {
        "wqkv": lay(i["L0_attn_qkv_w"]), "wgate": lay(i["L0_attn_gate_w"]), "bqkv": by_partition(i["L0_attn_qkv_b"]),
        "bgate": by_partition(i["L0_attn_gate_b"]), "bv": to_all(i["L0_attn_qkv_b"][2 * D:]),
        "lng": by_partition(i["L0_attn_ln_g"]), "lnb": by_partition(i["L0_attn_ln_b"]),
    }


def layout2(i):
    twice = lambda w: lay(np.broadcast_to(w.reshape(D, H0, 1, DH0), (D, H0, 2, DH0)).reshape(D, -1))
    pick = np.zeros((P, H0 // 2, NE, 2), np.float32)
    for c in range(H0 // 2):
        for e in range(NE):
            for a in range(2):
                pick[(2 * c + a) * NE + e::H0 * NE, c, e, a] = 1.0
    ve = i["L0_ffn_value_experts"].transpose(2, 1, 0, 3)
    oe = i["L0_ffn_output_experts"].reshape(NE, H0 // 2, P, D).transpose(2, 1, 0, 3)
    return {
        "wq2": twice(i["L0_ffn_w_q"]), "wk2": twice(i["L0_ffn_w_k"]), "wg2": lay(i["L0_ffn_w_gate"]),
        "ve2": lay(ve.reshape(D, -1)).reshape(P, KC, H0, NE * DH0), "oe2": oe,
        "prio": to_all(np.arange(NE, 0, -1, dtype=np.float32)),
        "klo": np.where(np.arange(P) < P // 2, 0.0, -1.0).astype(np.float32).reshape(P, 1), "pick": pick.reshape(P, -1),
    }


def layout3(i):
    fold = lambda w: w.reshape(-1, H1, 1, DH1)
    stack = lambda w: np.broadcast_to(fold(w), (fold(w).shape[0], H1, 4, DH1)).reshape(-1, 4 * D)
    part = np.arange(P) % (4 * DH1) // DH1
    return {
        "wq3": lay(stack(i["L1_attn_Wq"])), "wk3": lay(stack(i["L1_attn_Wk"])), "wv3": lay(i["L1_attn_Wv"]),
        "wo3": lay(i["L1_attn_Wo"]), "bq3": by_partition(stack(i["L1_attn_bq"])), "bk3": by_partition(stack(i["L1_attn_bk"])),
        "bv3": to_all(i["L1_attn_bv"]), "bo3": to_all(i["L1_attn_bo"]), "w13": lay(i["L1_attn_dp_w1"]),
        "hv3": np.stack([to_all(i["L1_attn_" + n]) for n in ("dp_b1", "ln_g", "ln_b", "dp_w2")], 1),
        "gv3": np.stack([to_all(i["L1_attn_" + n]) for n in ("g_w1", "g_b1", "g_w2")], 1),
        "b23": np.concatenate([to_all(i["L1_attn_dp_b2"]), to_all(i["L1_attn_g_b2"])], 1),
        "qneg3": np.where(part >= 2, -1.0, 0.0).astype(np.float32).reshape(P, 1),
        "kneg3": np.where(part % 2 == 1, -1.0, 0.0).astype(np.float32).reshape(P, 1),
    }


def layout4(i):
    n = lambda name: i["L1_ffn_" + name]
    return {
        "w14": lay(n("w1_w").T), "w24": lay(n("w2_w").T), "h14": lay(n("h1_w").T), "h24": lay(n("h2_w").T),
        "w34": lay(n("w3_w").T), "scale4": np.stack([by_partition(n(x)) for x in ("w1_s", "w2_s", "h1_s", "h2_s")], 1),
        "s34": to_all(n("w3_s")),
    }


def kernel(**inputs):
    import concourse.bacc as bacc
    from concourse.bass_utils import run_bass_kernel_spmd

    given = {name: np.asarray(a) for name, a in inputs.items()}
    arrays = {"tokens": given["L0_attn_x"].reshape(SEQS * T, D), **constants(), **layout1(given), **layout2(given),
              **layout3(given), **layout4(given)}
    arrays = {name: np.ascontiguousarray(a) for name, a in arrays.items()}
    nc = bacc.Bacc("TRN2", target_bir_lowering=False, num_devices=1)
    I = {name: nc.dram_tensor(name, a.shape, mybir.dt.from_np(a.dtype), kind="ExternalInput").ap() for name, a in arrays.items()}
    scratch = [nc.dram_tensor(f"sums{n}", (SEQS * T, D), F32, kind="Internal").ap() for n in range(1, 4)]
    out = nc.dram_tensor("normed", (SEQS * T, D), F32, kind="ExternalOutput").ap()
    program(nc, I, [layer1, layer2, layer3, layer4], I["tokens"], [*scratch, out])
    got = run_bass_kernel_spmd(nc, [arrays], core_ids=[0]).results[0]["normed"]
    return got.reshape(SEQS, T, D)
```

```python
from collections import namedtuple
from contextlib import ExitStack


import numpy as np

import concourse.bass as bass
from concourse import mybir

ALU = mybir.AluOpType
ACT = mybir.ActivationFunctionType
F32 = mybir.dt.float32
F32R = mybir.dt.float32r
BF16 = mybir.dt.bfloat16
AX_X = mybir.AxisListType.X

P = 128
D = 256
KC = D // P
SEQS = 4
T = 1024
NT = T // P
HALF = 512
NH = T // HALF
EPS = 1e-5
DEN_EPS = 1e-6

H0, DH0, NE = 8, 64, 8
SCALE0 = DH0 ** -0.5
H1, DH1 = 16, 16
SCALE1 = DH1 ** -0.5
G1 = 4
HID = 1024
HC = HID // P


class Memory:

    def __init__(self, nc, ctx):
        def sb(name, shape, dt=F32):
            return ctx.enter_context(nc.sbuf_tensor("sb_" + name, shape, dt))

        self.ps = ctx.enter_context(nc.psum_tensor("sums", [P, 8 * HALF], F32))
        self.x = sb("x", [P, NT, D])
        self.nx = sb("nx", [P, NT, D])
        self.stats, self.moments = sb("stats", [P, NT, 6]), sb("moments", [P, NT, 2])
        self.sd, self.rstd, self.eps = sb("sd", [P, NT]), sb("rstd", [P, NT]), sb("eps", [P, 1])
        self.ident, self.ident16 = sb("ident", [P, P]), sb("ident16", [P, P], BF16)
        self.mask_kq, self.mask_qk = sb("mask_kq", [P, P], BF16), sb("mask_qk", [P, P], BF16)
        self.negones = sb("negones", [P, P], F32R)
        self.weights_copy, self.weights_copied, self.weights_given = None, None, []
        self.misfit = sb("misfit", [P, 1])


def bank(ps, n, lo=0, hi=HALF, rows=slice(0, P)):
    return ps[rows, n * HALF + lo:n * HALF + hi]


def halves(lo, hi):
    return [(max(lo, h * HALF), min(hi, (h + 1) * HALF)) for h in range(NH) if max(lo, h * HALF) < min(hi, (h + 1) * HALF)]


class Chain:

    def __init__(self, engine, sem):
        self.engine, self.sem, self.n = engine, sem, 0

    def __call__(self, instruction):
        self.n += 1
        instruction.then_inc(self.sem, 1)
        self.engine.wait_ge(self.sem, self.n)


def signals(nc, ctx, stage, names):
    return namedtuple(stage, names)(*(ctx.enter_context(nc.semaphore(f"{stage}_{n}")) for n in names.split()))


def clear(pool, stale):
    for sem in stale:
        pool.sem_clear(sem)



FETCH = " nx_in nx_stats nx_moments nx_sd nx_chain nx_ready"
ENTRY = " transposed xT_ready x_copied"


def inverse_sd(step, dve, m, r, var, sd):
    step(dve.reciprocal(r, sd))
    step(dve.tensor_tensor(sd, r, r, ALU.mult))
    step(dve.scalar_tensor_tensor(sd, var, m.eps[:, 0:1], sd, ALU.add, ALU.mult))
    step(dve.tensor_scalar(sd, sd, -0.5, 1.5, ALU.mult, ALU.add))
    step(dve.tensor_tensor(r, r, sd, ALU.mult))


def fetch_load(sp, m, s, src):
    sp.dma_start(m.nx[:, :, :], src).then_inc(s.nx_in, 16)


def fetch_stats(dve, m, s):
    dve.wait_ge(s.nx_in, 16)
    for t in range(NT):
        last = dve.bn_stats(m.stats[:, t, :], m.nx[:, t, :])
    last.then_inc(s.nx_stats, 1)
    dve.wait_ge(s.nx_stats, 1)
    for t in range(NT):
        last = dve.bn_aggr(m.moments[:, t, :], m.stats[:, t, :])
    last.then_inc(s.nx_moments, 1)


def fetch_sd(act, m, s):
    act.wait_ge(s.nx_moments, 1)
    act.activation(m.sd[:, :], m.moments[:, :, 1], ACT.Sqrt, bias=m.eps[:, 0:1]).then_inc(s.nx_sd, 1)


def fetch_norm(dve, m, s):
    dve.wait_ge(s.nx_sd, 1)
    inverse_sd(Chain(dve, s.nx_chain), dve, m, m.rstd[:, :], m.moments[:, :, 1], m.sd[:, :])
    for t in range(NT):
        last = dve.tensor_scalar(m.nx[:, t, :], m.nx[:, t, :], m.moments[:, t, 0:1], m.rstd[:, t:t + 1],
                                 ALU.subtract, ALU.mult)
    last.then_inc(s.nx_ready, 1)


def fetch_first(nc, m, s, src, load, prepare):
    with nc.Block() as block:
        @block.sync
        def _(sp):
            fetch_load(sp, m, s, src)
            load(sp)

        @block.vector
        def _(dve):
            fetch_stats(dve, m, s)
            fetch_norm(dve, m, s)
            prepare(dve)

        @block.scalar
        def _(act):
            fetch_sd(act, m, s)

    with nc.Block() as block:
        @block.gpsimd
        def _(pool):
            clear(pool, s)

        @block.sync
        def _(sp):
            copy_weights(sp, m)


def copy_weights(sp, m):
    at = 0
    for given in m.weights_given:
        _p, c, n = given.shape
        sp.dma_start(m.weights_copy[:, at:at + c * n], given.rearrange("p c n -> p (c n)")).then_inc(m.weights_copied, 16)
        at += c * n
    m.weights_given = []


ENTRY_BANKS = 4


def entry_transpose(pe, m, s):
    for t in range(NT):
        if t >= ENTRY_BANKS:
            pe.wait_ge(s.xT_ready, t - ENTRY_BANKS + 1)
        for c in range(KC):
            last = pe.transpose(bank(m.ps, t % ENTRY_BANKS, c * P, (c + 1) * P), m.nx[:, t, c * P:(c + 1) * P], m.ident[:, :])
        last.then_inc(s.transposed, 1)


def entry_copy(act, m, s, xT, affine=None):
    for t in range(NT):
        act.wait_ge(s.transposed, t + 1)
        if affine:
            for c in range(KC):
                last = act.activation(xT[:, c, t * P:(t + 1) * P], bank(m.ps, t % ENTRY_BANKS, c * P, (c + 1) * P),
                                      ACT.Identity, scale=affine[0][:, c:c + 1], bias=affine[1][:, c:c + 1])
        else:
            last = act.copy(xT[:, :, t * P:(t + 1) * P],
                            bank(m.ps, t % ENTRY_BANKS, 0, D).rearrange("p (c q) -> p c q", c=KC))
        last.then_inc(s.xT_ready, 1)


def entry_residual(pool, m, s):
    pool.tensor_copy(m.x[:, :, :], m.nx[:, :, :]).then_inc(s.x_copied, 1)


def store(sp, s, tile, dst):
    for t in range(0, NT, 2):
        sp.wait_ge(s.y_ready, t + 2)
        sp.dma_start(dst[:, t:t + 2, :], tile[:, t:t + 2, :]).then_inc(s.y_out, 16)
    sp.wait_ge(s.y_out, 16 * NT // 2)



PROJ1 = "x_in transposed xT_ready gate_mm qk_mm v_mm gate_read half_gate k_gated min_ready relu_ready exp_ready v_read qkT_ready chain"
ATTN1 = "score_mm score_copied masked out_mm den y_ready y_out rden" + FETCH


def layer1(nc, ctx, m, I, src, dst):
    sb = lambda name, shape, dt=F32: ctx.enter_context(nc.sbuf_tensor("l1_" + name, shape, dt))
    wqkv, wgate = sb("wqkv", [P, KC, 3 * D]), sb("wgate", [P, KC, D])
    bqkv, bgate, hbgate = sb("bqkv", [P, 6]), sb("bgate", [P, KC]), sb("hbgate", [P, KC])
    bv, lng, lnb = sb("bv", [P, D]), sb("lng", [P, KC]), sb("lnb", [P, KC])
    qT, kT = sb("qT", [P, KC, T]), sb("kT", [P, KC, T])
    v = sb("v", [P, NT, D + 2])
    gate = sb("gate", [P, 2 * NH, HALF])
    kg = sb("kg", [P, 2 * NH, HALF])
    neg = sb("neg", [P, 4 * NH, HALF])
    AT = sb("AT", [P, NT, T])
    den = sb("den", [P, NT, 2])
    ld = signals(nc, ctx, "l1_load", "weights ones hb")
    s0 = signals(nc, ctx, "l1_first", FETCH)
    xT, y = sb("xT", [P, KC, T]), sb("y", [P, NT, D])
    s1 = signals(nc, ctx, "l1_proj", PROJ1)
    s2 = signals(nc, ctx, "l1_attn", ATTN1)

    def load(sp):
        pairs = [(wqkv, "wqkv"), (wgate, "wgate"), (bqkv, "bqkv"), (bgate, "bgate"), (bv, "bv"), (lng, "lng"), (lnb, "lnb")]
        for tile, name in pairs:
            sp.dma_start(tile[:], I[name]).then_inc(ld.weights, 16)
        sp.wait_ge(ld.weights, 16 * len(pairs))

    def prepare(dve):
        dve.memset(v[:, :, D:D + 2], 1.0).then_inc(ld.ones, 1)
        dve.wait_ge(ld.weights, 16 * 7)
        dve.tensor_scalar(hbgate[:, :], bgate[:, :], 0.5, None, ALU.mult).then_inc(ld.hb, 1)

    fetch_first(nc, m, s0, src[0], load, prepare)

    NG = KC * NH
    with nc.Fori(0, SEQS) as b:
        with nc.Block() as block:
            s = s1

            @block.gpsimd
            def _(pool):
                clear(pool, s2)
                for j in range(2 * NG):
                    n, c = divmod(j // 2, KC)
                    pool.wait_ge(s.exp_ready, j + 1)
                    out = (kT if j % 2 == 0 else qT)[:, c, n * HALF:(n + 1) * HALF]
                    pool.wait_ge(s.relu_ready, j + 1)
                    pool.tensor_tensor(out, out, neg[:, j, :], ALU.add).then_inc(s.qkT_ready, 1)

            @block.sync
            def _(sp):
                sp.dma_start(m.x[:, :, :], src[b]).then_inc(s.x_in, 16)
                sp.wait_ge(s.x_in, 16)

            @block.tensor
            def _(pe):
                entry_transpose(pe, m, s)
                pe.wait_ge(s.xT_ready, NT)

                def product(out, w, lo, n):
                    for c in range(KC):
                        last = pe.matmul(out, w[:, c, lo:lo + P], xT[:, c, n * HALF:(n + 1) * HALF],
                                         start=(c == 0), stop=(c == KC - 1))
                    return last

                for g in range(NG):
                    n, c = divmod(g, KC)
                    if g >= 2:
                        pe.wait_ge(s.gate_read, g - 1)
                    product(bank(m.ps, 2 + g % 2), wgate, c * P, n).then_inc(s.gate_mm, 1)
                    if g >= 2:
                        pe.wait_ge(s.relu_ready, 2 * (g - 1))
                    product(bank(m.ps, 4 + g % 2), wqkv, D + c * P, n).then_inc(s.qk_mm, 1)
                    product(bank(m.ps, 6 + g % 2), wqkv, c * P, n).then_inc(s.qk_mm, 1)
                for t in range(NT):
                    if t >= 2:
                        pe.wait_ge(s.v_read, t - 1)
                    for c in range(KC):
                        last = pe.matmul(bank(m.ps, t % 2, 0, D), xT[:, c, t * P:(t + 1) * P],
                                         wqkv[:, c, 2 * D:3 * D], start=(c == 0), stop=(c == KC - 1))
                    last.then_inc(s.v_mm, 1)

            @block.scalar
            def _(act):
                entry_copy(act, m, s, xT, affine=(lng, lnb))
                for g in range(NG):
                    c = g % KC
                    act.wait_ge(s.gate_mm, g + 1)
                    act.activation(gate[:, g, :], bank(m.ps, 2 + g % 2), ACT.Tanh, scale=0.5,
                                   bias=hbgate[:, c:c + 1]).then_inc(s.gate_read, 1)
                    for j in (2 * g, 2 * g + 1):
                        act.wait_ge(s.min_ready, j + 1)
                        act.activation(neg[:, j, :], neg[:, j, :], ACT.Exp).then_inc(s.exp_ready, 1)

            @block.vector
            def _(dve):
                for g in range(NG):
                    n, c = divmod(g, KC)
                    cols = slice(n * HALF, (n + 1) * HALF)
                    dve.wait_ge(s.gate_read, g + 1)
                    dve.tensor_scalar(gate[:, g, :], gate[:, g, :], 0.5, 0.5, ALU.mult, ALU.add).then_inc(s.half_gate, 1)
                    dve.wait_ge(s.half_gate, g + 1)
                    dve.wait_ge(s.qk_mm, 2 * g + 1)
                    dve.scalar_tensor_tensor(kg[:, g, :], bank(m.ps, 4 + g % 2), bqkv[:, 2 + c:3 + c], gate[:, g, :],
                                             ALU.add, ALU.mult).then_inc(s.k_gated, 1)
                    dve.wait_ge(s.k_gated, g + 1)
                    dve.tensor_scalar(neg[:, 2 * g, :], kg[:, g, :], 0.0, None, ALU.min).then_inc(s.min_ready, 1)
                    dve.tensor_scalar(kT[:, c, cols], kg[:, g, :], 0.0, None, ALU.max).then_inc(s.relu_ready, 1)
                    dve.wait_ge(s.qk_mm, 2 * g + 2)
                    q = bank(m.ps, 6 + g % 2)
                    dve.tensor_scalar(neg[:, 2 * g + 1, :], q, bqkv[:, c:c + 1], 0.0, ALU.add, ALU.min).then_inc(s.min_ready, 1)
                    dve.tensor_scalar(qT[:, c, cols], q, bqkv[:, c:c + 1], 0.0, ALU.add, ALU.max).then_inc(s.relu_ready, 1)
                for t in range(NT):
                    dve.wait_ge(s.v_mm, t + 1)
                    dve.tensor_tensor(v[:, t, 0:D], bank(m.ps, t % 2, 0, D), bv[:, :], ALU.add).then_inc(s.v_read, 1)

        with nc.Block() as block:
            s = s2

            @block.gpsimd
            def _(pool):
                clear(pool, s1)
                for k in range(NT):
                    pool.wait_ge(s.score_copied, k + 1)
                    diag = AT[:, k, k * P:(k + 1) * P]
                    pool.affine_select(out=diag, in_=diag, compare_op=ALU.is_ge, fill=0.0, base=0, pattern=[[1, P]],
                                       channel_multiplier=-1).then_inc(s.masked, 1)

            @block.tensor
            def _(pe):
                for k in range(NT + 1):
                    if k < NT:
                        if k >= 2:
                            pe.wait_ge(s.score_copied, k - 1)
                        for lo, hi in halves(k * P, T):
                            for c in range(KC):
                                last = pe.matmul(bank(m.ps, 2 * (k % 2), lo, hi), kT[:, c, k * P:(k + 1) * P],
                                                 qT[:, c, lo:hi], start=(c == 0), stop=(c == KC - 1))
                        last.then_inc(s.score_mm, 1)
                    if k >= 1:
                        t = k - 1
                        pe.wait_ge(s.masked, t + 1)
                        if t >= 2:
                            pe.wait_ge(s.y_ready, t - 1)
                        for k2 in range(t + 1):
                            last = pe.matmul(bank(m.ps, 4 + t % 2, 0, D + 2), AT[:, k2, t * P:(t + 1) * P], v[:, k2, :],
                                             start=(k2 == 0), stop=(k2 == t))
                        last.then_inc(s.out_mm, 1)

            @block.scalar
            def _(act):
                for k in range(NT):
                    if k == 4:
                        fetch_sd(act, m, s)
                    act.wait_ge(s.score_mm, k + 1)
                    act.copy(AT[:, k, k * P:T], bank(m.ps, 2 * (k % 2), k * P, T)).then_inc(s.score_copied, 1)

            @block.vector
            def _(dve):
                fetch_stats(dve, m, s)
                for t in range(NT):
                    if t == 4:
                        fetch_norm(dve, m, s)
                    dve.wait_ge(s.out_mm, t + 1)
                    dve.tensor_scalar(den[:, t, 0:1], bank(m.ps, 4 + t % 2, D, D + 1), DEN_EPS, None, ALU.add).then_inc(s.den, 1)
                    dve.wait_ge(s.den, t + 1)
                    dve.reciprocal(den[:, t, 1:2], den[:, t, 0:1]).then_inc(s.rden, 1)
                    dve.wait_ge(s.rden, t + 1)
                    dve.scalar_tensor_tensor(y[:, t, :], bank(m.ps, 4 + t % 2, 0, D), den[:, t, 1:2], m.x[:, t, :],
                                             ALU.mult, ALU.add).then_inc(s.y_ready, 1)

            @block.sync
            def _(sp):
                fetch_load(sp, m, s, src[(b + 1) % SEQS])
                store(sp, s, y, dst[b])

    return ld, s0, s1, s2



GATES2 = ("transposed xT_ready x_copied x_hi x_parts even_ve_in odd_ve_in ve_hi ve_lo logits exp_in exp_out chain gm_ready "
          "value_mm value_masked v_ready pool_chain pool_v_ready")
ATTN2 = ("qk_mm qk_hi qk_parts max_mm max_read shift_ready score_mm exp_ready pv_mm o_read den_read "
         "even_den_out odd_den_out oe_in" + FETCH)
OUT2 = ("even_weight_in odd_weight_in weight_rounded weight_compared weight_checked worst ve_in oe_in1 oe_in2 oe_in3 oe_hi oe_lo dens_turned chain hilo_ready gmT_mm gmT_ready mask_mm routed "
        "routed_hi routed_lo out_mm y_ready y_out")
CLAMP = 80.0


def layer2(nc, ctx, m, I, src, dst):
    sb = lambda name, shape, dt=F32: ctx.enter_context(nc.sbuf_tensor("l2_" + name, shape, dt))
    wq, wk, wg = sb("wq", [P, KC, H0 * DH0]), sb("wk", [P, KC, H0 * DH0]), sb("wg", [P, KC, H0 * NE])
    prio = sb("prio", [P, NE])
    pick = sb("pick", [P, H0 * NE])
    xT = sb("xT", [P, KC, T])
    vx = sb("vx", [P, NT, H0, P])
    oT = sb("oT", [P, H0 // 2, T])
    N = NT * H0 * NE
    gm = sb("gm", [P, N])
    dens = sb("dens", [H0, T])
    sel = sb("sel", [P, H0 // 2 * NE, P], F32R)
    ve, oe = sb("ve", [P, 2, KC, HALF]), sb("oe", [P, NE, D])
    half = lambda odd: slice(DH0 * odd, DH0 * odd + DH0)
    vcol = lambda h: half(h % 2)
    den_row = lambda h: slice(DH0 * (1 - h % 2), DH0 * (1 - h % 2) + 1)
    by_head = lambda x: x[:, :].rearrange("p (n e) -> p n e", e=NE)
    every = lambda x: x[:, :].unsqueeze(2).to_broadcast([P, NT * H0, NE])
    ld = signals(nc, ctx, "l2_load", "weights ones sel")
    s0 = signals(nc, ctx, "l2_first", FETCH)
    s1 = signals(nc, ctx, "l2_gates", GATES2)
    s2 = signals(nc, ctx, "l2_attn", ATTN2)
    s3 = signals(nc, ctx, "l2_out", OUT2)

    def load(sp):
        pairs = [(wq, "wq2"), (wk, "wk2"), (wg, "wg2"), (prio, "prio"), (pick, "pick")]
        for tile, name in pairs:
            sp.dma_start(tile[:], I[name]).then_inc(ld.weights, 16)
        for h in range(2):
            sp.dma_start(ve[:, h, :, :], I["ve2"][:, :, h]).then_inc(ld.weights, 16)
        sp.wait_ge(ld.weights, 16 * (len(pairs) + 2))

    def prepare(dve):
        dve.memset(vx[:, :, :, :], 1.0).then_inc(ld.ones, 1)
        dve.wait_ge(ld.weights, 16 * 7)
        dve.tensor_copy(sel[:, :, :].rearrange("p n (a k) -> p (n a) k", a=2),
                        pick[:, :].unsqueeze(2).to_broadcast([P, H0 * NE, DH0])).then_inc(ld.sel, 1)

    fetch_first(nc, m, s0, src[0], load, prepare)

    def gates_and_values(own):
        sb = lambda name, shape, dt=F32: own.enter_context(nc.sbuf_tensor("l2a_" + name, shape, dt))
        z, e, g, first = sb("z", [P, N]), sb("e", [P, N]), sb("g", [P, N]), sb("first", [P, N])
        top, win = sb("top", [P, NT * H0]), sb("win", [P, NT * H0])
        xhi, xlo = sb("xhi", [P, KC, T], F32R), sb("xlo", [P, KC, T], F32R)
        vhi, vlo = sb("vhi", [P, 2, KC, HALF], F32R), sb("vlo", [P, 2, KC, HALF], F32R)
        VM = 6
        vm = sb("vm", [P, VM, HALF])
        RING = 7
        order = [(h, t) for h in range(H0) for t in range(NT)]
        pooled = lambda n: n % 3 == 2
        pools_to = lambda n: (n + 1) // 3
        dves_to = lambda n: n + 1 - pools_to(n)
        s = s1
        with nc.Block() as block:
            @block.sync
            def _(sp):
                for h in range(2, H0):
                    sp.wait_ge(s.ve_lo, h - 1)
                    sp.dma_start(ve[:, h % 2, :, :], I["ve2"][:, :, h]).then_inc((s.even_ve_in, s.odd_ve_in)[h % 2], 16)

            @block.tensor
            def _(pe):
                entry_transpose(pe, m, s)
                for t in range(NT):
                    pe.wait_ge(s.xT_ready, t + 1)
                    for c in range(KC):
                        last = pe.matmul(bank(m.ps, 7, t * 64, t * 64 + 64), xT[:, c, t * P:(t + 1) * P], wg[:, c, :],
                                         start=(c == 0), stop=(c == KC - 1))
                last.then_inc(s.logits, 1)
                for n, (h, t) in enumerate(order):
                    if h == 0:
                        pe.wait_ge(s.x_parts, t + 1)
                    if t == 0:
                        pe.wait_ge(s.ve_lo, h + 1)
                    if n >= RING:
                        pe.wait_ge(s.value_masked, n - RING + 1)
                    for c in range(KC):
                        for x, v in ((xhi, vhi), (xhi, vlo), (xlo, vhi)):
                            last = pe.matmul(bank(m.ps, n % RING), x[:, c, t * P:(t + 1) * P], v[:, h % 2, c, :],
                                             start=(c == 0 and x is xhi and v is vhi), stop=(c == KC - 1 and x is xlo))
                    last.then_inc(s.value_mm, 1)

            @block.scalar
            def _(act):
                def expert_hi(h):
                    if h >= 2:
                        act.wait_ge((s.even_ve_in, s.odd_ve_in)[h % 2], 16 * (h // 2))
                        act.wait_ge(s.value_mm, NT * (h - 1))
                    act.copy(vhi[:, h % 2, :, :], ve[:, h % 2, :, :]).then_inc(s.ve_hi, 1)

                expert_hi(0)
                entry_copy(act, m, s, xT)
                act.wait_ge(s.exp_in, 1)
                act.activation(e[:, :], z[:, :], ACT.Exp).then_inc(s.exp_out, 1)
                for h in range(1, H0):
                    expert_hi(h)

            @block.vector
            def _(dve):
                step = Chain(dve, s.chain)
                for t in range(NT):
                    cols = slice(t * P, (t + 1) * P)
                    dve.wait_ge(s.xT_ready, t + 1)
                    dve.tensor_copy(xhi[:, :, cols], xT[:, :, cols]).then_inc(s.x_hi, 1)
                    dve.wait_ge(s.x_hi, t + 1)
                    dve.tensor_tensor(xlo[:, :, cols], xT[:, :, cols], xhi[:, :, cols].bitcast(F32), ALU.subtract).then_inc(s.x_parts, 1)
                dve.wait_ge(s.logits, 1)
                dve.tensor_scalar(z[:, :], bank(m.ps, 7), -1.0, CLAMP, ALU.mult, ALU.min).then_inc(s.exp_in, 1)
                dve.wait_ge(s.exp_out, 1)
                step(dve.tensor_scalar(z[:, :], e[:, :], 1.0, None, ALU.add))
                step(dve.reciprocal(g[:, :], z[:, :]))
                step(dve.tensor_reduce(top[:, :], by_head(g), AX_X, ALU.max))
                step(dve.tensor_tensor(by_head(first), by_head(g), every(top), ALU.is_equal))
                step(dve.tensor_tensor(by_head(first), by_head(first),
                                       prio[:, :].unsqueeze(1).to_broadcast([P, NT * H0, NE]), ALU.mult))
                step(dve.tensor_reduce(win[:, :], by_head(first), AX_X, ALU.max))
                step(dve.tensor_tensor(by_head(first), by_head(first), every(win), ALU.is_equal))
                dve.tensor_tensor(gm[:, :], first[:, :], g[:, :], ALU.mult).then_inc(s.gm_ready, 1)
                dve.wait_ge(s.gm_ready, 1)
                for n, (h, t) in enumerate(order):
                    dve.wait_ge(s.value_mm, n + 1)
                    if n >= VM:
                        k = n - VM
                        dve.wait_ge(s.pool_v_ready if pooled(k) else s.v_ready, pools_to(k) if pooled(k) else dves_to(k))
                    at = (t * H0 + h) * NE
                    dve.tensor_tensor(vm[:, n % VM, :].rearrange("p (e k) -> p e k", e=NE),
                                      bank(m.ps, n % RING).rearrange("p (e k) -> p e k", e=NE),
                                      gm[:, at:at + NE].unsqueeze(2).to_broadcast([P, NE, DH0]), ALU.mult).then_inc(s.value_masked, 1)
                    if not pooled(n):
                        dve.wait_ge(s.value_masked, n + 1)
                        dve.tensor_reduce(vx[:, t, h, vcol(h)], vm[:, n % VM, :].rearrange("p (e k) -> p k e", e=NE),
                                          AX_X, ALU.add).then_inc(s.v_ready, 1)

            @block.gpsimd
            def _(pool):
                clear(pool, s3)
                step = Chain(pool, s.pool_chain)

                def expert_lo(h):
                    pool.wait_ge(s.ve_hi, h + 1)
                    pool.tensor_tensor(vlo[:, h % 2, :, :], ve[:, h % 2, :, :], vhi[:, h % 2, :, :].bitcast(F32),
                                       ALU.subtract).then_inc(s.ve_lo, 1)

                expert_lo(0)
                entry_residual(pool, m, s)
                expert_lo(1)
                for n, (h, t) in enumerate(order):
                    if t == 1 and 1 <= h < H0 - 1:
                        expert_lo(h + 1)
                    if pooled(n):
                        pool.wait_ge(s.value_masked, n + 1)
                        slot = vm[:, n % VM, :]
                        step(pool.tensor_tensor(slot[:, 0:256], slot[:, 0:256], slot[:, 256:512], ALU.add))
                        step(pool.tensor_tensor(slot[:, 0:128], slot[:, 0:128], slot[:, 128:256], ALU.add))
                        pool.tensor_tensor(vx[:, t, h, vcol(h)], slot[:, 0:64], slot[:, 64:128], ALU.add).then_inc(s.pool_v_ready, 1)

    def attention(own, b):
        sb = lambda name, shape, dt=F32: own.enter_context(nc.sbuf_tensor("l2b_" + name, shape, dt))
        RK = 4
        kst, qst, qlo = (sb(n, [P, RK, T], F32R) for n in ("kst", "qst", "qlo"))
        shift = sb("shift", [P, 2, T], F32R)
        prob = sb("prob", [P, 2, T])
        mx = sb("mx", [P, H0, NT])
        den = sb("den", [P, 2, T])
        s = s2
        units = [(k, lo, hi) for k in range(NT) for lo, hi in halves(k * P, T)]
        U = len(units)
        through = lambda k: sum(kk <= k for kk, _lo, _hi in units)
        parts = [(kind, n) for kind in "kq" for n in range(NH)]
        part_at = {0: 0, 1: 1, 2: 2, 4: 3}
        MAX, PV, PROJ = 3, 5, 7

        def proj_bank(c, j):
            return PROJ if c else (PROJ, 0, 1, 2)[j]

        def max_bank(h, k):
            if h == 0:
                return PV if k % 2 else MAX
            return MAX + (k % 2 if k >= NT // 2 else 0)

        with nc.Block() as block:
            @block.sync
            def _(sp):
                fetch_load(sp, m, s, src[(b + 1) % SEQS])
                sp.dma_start(oe[:, :, :], I["oe2"][:, 0]).then_inc(s.oe_in, 16)
                for h in range(H0):
                    sp.wait_ge(s.den_read, h + 1)
                    sp.dma_start(dens[h:h + 1, :], den[den_row(h), h % 2, :]).then_inc((s.even_den_out, s.odd_den_out)[h % 2], 16)
                sp.wait_ge(s.even_den_out, 16 * (H0 // 2))
                sp.wait_ge(s.odd_den_out, 16 * (H0 // 2))
                sp.wait_ge(s.oe_in, 16)

            @block.tensor
            def _(pe):
                def project(c, j):
                    kind, n = parts[j]
                    done = 4 * c + j
                    if c:
                        pe.wait_ge(s.qk_parts, done)
                    for kc in range(KC):
                        last = pe.matmul(bank(m.ps, proj_bank(c, j)), (wk if kind == "k" else wq)[:, kc, c * P:(c + 1) * P],
                                         xT[:, kc, n * HALF:(n + 1) * HALF], start=(kc == 0), stop=(kc == KC - 1))
                    last.then_inc(s.qk_mm, 1)

                def maxima(h, k):
                    t = NT - 1 - k
                    if k == 0:
                        pe.wait_ge(s.qk_parts, 4 * (h // 2 + 1))
                    if h and k <= NT // 2:
                        pe.wait_ge(s.max_read, NT * h + k)
                    elif k >= 2:
                        pe.wait_ge(s.max_read, NT * h + k - 1)
                    for lo, hi in halves(0, (t + 1) * P):
                        pe.matmul(bank(m.ps, max_bank(h, k), lo, hi), qst[:, h % RK, t * P:(t + 1) * P], kst[:, h % RK, lo:hi],
                                  start=True, stop=True)
                    pe.matmul(bank(m.ps, max_bank(h, k), t * P, (t + 1) * P), m.ident16[:, :], m.mask_qk[:, :],
                              start=False, stop=True, skip_group_check=True).then_inc(s.max_mm, 1)

                def scores(h, k):
                    for n, (kk, lo, hi) in enumerate(units, U * h):
                        if kk != k:
                            continue
                        if n % U == 0:
                            pe.wait_ge(s.shift_ready, NT * (h + 1))
                        if n >= 3:
                            pe.wait_ge(s.exp_ready, n - 2)
                        out, keys = bank(m.ps, n % 3, 0, hi - lo), kst[:, h % RK, k * P:(k + 1) * P]
                        pe.matmul(out, keys, qst[:, h % RK, lo:hi], start=True, stop=False)
                        pe.matmul(out, keys, qlo[:, h % RK, lo:hi], start=False, stop=False)
                        if lo == k * P:
                            pe.matmul(bank(m.ps, n % 3, 0, P), m.ident16[:, :], m.mask_kq[:, :], start=False, stop=False)
                        pe.matmul(out, m.negones[:, :], shift[:, h % 2, lo:hi], start=False, stop=True).then_inc(s.score_mm, 1)

                def weighted(h, k):
                    pe.wait_ge(s.exp_ready, U * h + through(k))
                    if k == 0 and h:
                        pe.wait_ge(s.o_read, h)
                        pe.wait_ge(s.den_read, h)
                    for lo, hi in halves(k * P, T):
                        last = pe.matmul(bank(m.ps, PV, lo, hi), vx[:, k, h, :], prob[:, k % 2, lo:hi], start=(k == 0),
                                         stop=True, skip_group_check=True)
                    last.then_inc(s.pv_mm, 1)

                for step in range(H0 + 2):
                    h1, h2 = step - 1, step - 2
                    for k in range(NT):
                        if h2 >= 0:
                            scores(h2, k)
                        if step % 2 == 0 and step < H0 and k in part_at:
                            project(step // 2, part_at[k])
                        if 0 <= h1 < H0 and k < NT - 1:
                            maxima(h1, k)
                        if h2 >= 0 and k >= 1:
                            weighted(h2, k - 1)
                        if 0 <= h1 < H0 and k == NT - 2:
                            maxima(h1, NT - 1)
                    if h2 >= 0:
                        weighted(h2, NT - 1)

            @block.scalar
            def _(act):
                def exps(h, k):
                    for n, (kk, lo, hi) in enumerate(units, U * h):
                        if kk != k:
                            continue
                        act.wait_ge(s.score_mm, n + 1)
                        if NT * h + k >= 2:
                            act.wait_ge(s.pv_mm, NT * h + k - 1)
                        act.activation(prob[:, k % 2, lo:hi], bank(m.ps, n % 3, 0, hi - lo), ACT.Exp,
                                       scale=SCALE0).then_inc(s.exp_ready, 1)

                def hi_parts(c, j):
                    kind, n = parts[j]
                    cols = slice(n * HALF, (n + 1) * HALF)
                    act.wait_ge(s.qk_mm, 4 * c + j + 1)
                    if c >= 2:
                        act.wait_ge(s.score_mm, U * (2 * c - 2))
                    for odd in (0, 1):
                        got, slot = bank(m.ps, proj_bank(c, j), 0, HALF, half(odd)), (2 * c + odd) % RK
                        if kind == "k":
                            last = act.copy(kst[half(odd), slot, cols], got)
                        else:
                            for to in (0, 1):
                                last = act.copy(qst[half(to), slot, cols], got)
                    last.then_inc(s.qk_hi, 1)

                def den_out(h):
                    act.wait_ge(s.pv_mm, NT * (h + 1))
                    if h >= 2:
                        act.wait_ge((s.even_den_out, s.odd_den_out)[h % 2], 16 * (h // 2))
                    act.copy(den[den_row(h), h % 2, :], bank(m.ps, PV, 0, T, den_row(h))).then_inc(s.den_read, 1)

                for step in range(H0 + 2):
                    h2 = step - 2
                    for k in range(NT):
                        if h2 >= 0:
                            exps(h2, k)
                        if k == 0 and h2 >= 1:
                            den_out(h2 - 1)
                        if k == 3 and step == H0 + 1:
                            fetch_sd(act, m, s)
                        if step % 2 == 0 and step < H0 and k in part_at:
                            hi_parts(step // 2, part_at[k])
                den_out(H0 - 1)

            @block.vector
            def _(dve):
                def lo_parts(c, j):
                    kind, n = parts[j]
                    cols = slice(n * HALF, (n + 1) * HALF)
                    dve.wait_ge(s.qk_hi, 4 * c + j + 1)
                    for odd in (0, 1):
                        got, slot = bank(m.ps, proj_bank(c, j), 0, HALF, half(odd)), (2 * c + odd) % RK
                        if kind == "k":
                            last = dve.tensor_tensor(kst[half(1 - odd), slot, cols], got, kst[half(odd), slot, cols].bitcast(F32),
                                                     ALU.subtract)
                        else:
                            for to in (0, 1):
                                last = dve.tensor_tensor(qlo[half(to), slot, cols], got, qst[half(odd), slot, cols].bitcast(F32),
                                                         ALU.subtract)
                    last.then_inc(s.qk_parts, 1)

                def head_out(h):
                    dve.wait_ge(s.pv_mm, NT * (h + 1))
                    dve.tensor_copy(oT[vcol(h), h // 2, :], bank(m.ps, PV, 0, T, vcol(h))).then_inc(s.o_read, 1)

                for step in range(H0 + 2):
                    h1, h2 = step - 1, step - 2
                    for k in range(NT):
                        if k == 0 and h2 >= 1:
                            head_out(h2 - 1)
                        if 0 <= h1 < H0:
                            t = NT - 1 - k
                            dve.wait_ge(s.max_mm, NT * h1 + k + 1)
                            dve.reduce_max(mx[:, h1, t:t + 1], bank(m.ps, max_bank(h1, k), 0, (t + 1) * P), AX_X).then_inc(s.max_read, 1)
                        if step % 2 == 0 and step < H0 and k in part_at:
                            lo_parts(step // 2, part_at[k])
                fetch_stats(dve, m, s)
                fetch_norm(dve, m, s)
                head_out(H0 - 1)

            @block.gpsimd
            def _(pool):
                clear(pool, s1)
                for h in range(H0):
                    if h >= 2:
                        pool.wait_ge(s.score_mm, U * (h - 1))
                    for k in range(NT):
                        t = NT - 1 - k
                        pool.wait_ge(s.max_read, NT * h + k + 1)
                        pool.tensor_scalar(shift[:, h % 2, t * P:(t + 1) * P], m.ident[:, :], mx[:, h, t:t + 1], None,
                                           ALU.mult).then_inc(s.shift_ready, 1)

    def output_experts(own, b):
        sb = lambda name, shape, dt=F32: own.enter_context(nc.sbuf_tensor("l2c_" + name, shape, dt))
        gn, gn_hi, hilo = sb("gn", [P, N]), sb("gn_hi", [P, N], F32R), sb("hilo", [P, NT, 2, H0 * NE])
        rden = sb("rden", [P, NT * H0])
        gmT = sb("gmT", [P, T], F32R)
        ohi, olo = sb("ohi", [P, 2, NE, D], F32R), sb("olo", [P, 2, NE, D], F32R)
        RT, AHEAD = 4, 3
        routed = sb("routed", [P, RT, HALF])
        rhi, rlo = sb("rhi", [P, RT, HALF], F32R), sb("rlo", [P, RT, HALF], F32R)
        blocks = [(c, e, n) for c in range(H0 // 2) for e in range(NE) for n in range(NH)]
        PER_C = NE * NH
        oe_in = (None, s3.oe_in1, s3.oe_in2, s3.oe_in3)
        EH = NE // 2
        split_at = {(c - 1) * PER_C + 4 + 4 * j: (c, j) for c in range(2, H0 // 2) for j in range(2)}
        CHECKS = 8
        W = m.weights_copy.shape[1] // (SEQS * CHECKS)
        word, rounded = sb("word", [P, 2, W]), sb("rounded", [P, 2, W], F32R)
        worst = sb("worst", [P, CHECKS + 1])
        check_at = {8 + 6 * j: j for j in range(CHECKS)}
        weight_in = (s3.even_weight_in, s3.odd_weight_in)
        s = s3
        with nc.Block() as block:
            @block.sync
            def _(sp):
                def weight_chunk(j):
                    if j >= 2:
                        sp.wait_ge(s.weight_checked, j - 1)
                    sp.dma_start(word[:, j % 2, :],
                                 m.weights_copy.rearrange("p (b j n) -> b j p n", b=SEQS, n=W)[b, j]).then_inc(weight_in[j % 2], 16)

                for h in range(2):
                    sp.dma_start(ve[:, h, :, :], I["ve2"][:, :, h]).then_inc(s.ve_in, 16)
                sp.wait_ge(m.weights_copied, 16 * len(WEIGHTS4))
                for j in range(2):
                    weight_chunk(j)
                for c in range(1, H0 // 2):
                    sp.wait_ge(s.oe_lo, 2 * c)
                    sp.dma_start(oe[:, :, :], I["oe2"][:, c]).then_inc(oe_in[c], 16)
                    if c == 2:
                        for j in range(2, 4):
                            weight_chunk(j)
                for j in range(4, CHECKS):
                    weight_chunk(j)
                sp.wait_ge(s.ve_in, 32)
                store(sp, s, m.x, dst[b])

            @block.gpsimd
            def _(pool):
                clear(pool, s2)
                for i in range(len(blocks)):
                    pool.wait_ge(s.routed_hi, i + 1)
                    if i >= RT:
                        pool.wait_ge(s.out_mm, i - RT + 1)
                    pool.tensor_tensor(rlo[:, i % RT, :], routed[:, i % RT, :], rhi[:, i % RT, :].bitcast(F32),
                                       ALU.subtract).then_inc(s.routed_lo, 1)

            @block.scalar
            def _(act):
                def expert_hi(c, j):
                    es = slice(j * EH, (j + 1) * EH)
                    if c:
                        act.wait_ge(oe_in[c], 16)
                    if c >= 2:
                        act.wait_ge(s.out_mm, PER_C * (c - 1))
                    act.copy(ohi[:, c % 2, es, :], oe[:, es, :]).then_inc(s.oe_hi, 1)

                expert_hi(0, 0)
                expert_hi(0, 1)
                for n in range(NH):
                    act.wait_ge(s.gmT_mm, n + 1)
                    act.copy(gmT[:, n * HALF:(n + 1) * HALF], bank(m.ps, 5 + n)).then_inc(s.gmT_ready, 1)
                for i in range(len(blocks)):
                    if i in (4, 8):
                        expert_hi(1, (i - 4) // 4)
                    if i in split_at:
                        expert_hi(*split_at[i])
                    act.wait_ge(s.routed, i + 1)
                    if i >= RT:
                        act.wait_ge(s.out_mm, i - RT + 1)
                    act.copy(rhi[:, i % RT, :], routed[:, i % RT, :]).then_inc(s.routed_hi, 1)
                    if i in check_at:
                        j = check_at[i]
                        act.wait_ge(weight_in[j % 2], 16 * (j // 2 + 1))
                        if j >= 2:
                            act.wait_ge(s.weight_compared, j - 1)
                        act.copy(rounded[:, j % 2, :], word[:, j % 2, :]).then_inc(s.weight_rounded, 1)

            @block.vector
            def _(dve):
                step = Chain(dve, s.chain)

                def expert_lo(c, j):
                    es = slice(j * EH, (j + 1) * EH)
                    dve.wait_ge(s.oe_hi, 2 * c + j + 1)
                    dve.tensor_tensor(olo[:, c % 2, es, :], oe[:, es, :], ohi[:, c % 2, es, :].bitcast(F32),
                                      ALU.subtract).then_inc(s.oe_lo, 1)

                expert_lo(0, 0)
                expert_lo(0, 1)
                dve.wait_ge(s.dens_turned, 1)
                step(dve.reciprocal(rden[:, :], bank(m.ps, 4, 0, NT * H0)))
                step(dve.tensor_tensor(by_head(gn), by_head(gm), every(rden), ALU.mult))
                step(dve.tensor_copy(gn_hi[:, :], gn[:, :]))
                tiles = lambda x: x.rearrange("p (t n) -> p t n", t=NT)
                dve.tensor_copy(hilo[:, :, 0, :], tiles(gn_hi[:, :].bitcast(F32)))
                dve.tensor_tensor(hilo[:, :, 1, :], tiles(gn[:, :]), tiles(gn_hi[:, :].bitcast(F32)),
                                  ALU.subtract).then_inc(s.hilo_ready, 1)
                for i, (c, e, n) in enumerate(blocks):
                    if i in (6, 10):
                        expert_lo(1, (i - 6) // 4)
                    if i in split_at:
                        expert_lo(*split_at[i])
                    dve.wait_ge(s.mask_mm, i + 1)
                    if i >= RT:
                        dve.wait_ge(s.routed_lo, i - RT + 1)
                    dve.tensor_tensor(routed[:, i % RT, :], oT[:, c, n * HALF:(n + 1) * HALF], bank(m.ps, 4 + i % 4),
                                      ALU.mult).then_inc(s.routed, 1)
                    if i - 1 in check_at:
                        j = check_at[i - 1]
                        dve.wait_ge(s.weight_rounded, j + 1)
                        dve.wait_ge(weight_in[j % 2], 16 * (j // 2 + 1))
                        dve.tensor_tensor(word[:, j % 2, :], word[:, j % 2, :], rounded[:, j % 2, :].bitcast(F32),
                                          ALU.not_equal).then_inc(s.weight_compared, 1)
                    if i - 2 in check_at:
                        j = check_at[i - 2]
                        dve.wait_ge(s.weight_compared, j + 1)
                        dve.reduce_max(worst[:, j:j + 1], word[:, j % 2, :], AX_X).then_inc(s.weight_checked, 1)
                dve.wait_ge(s.weight_checked, CHECKS)
                dve.reduce_max(worst[:, CHECKS:], worst[:, 0:CHECKS], AX_X).then_inc(s.worst, 1)
                dve.wait_ge(s.worst, 1)
                dve.tensor_tensor(m.misfit[:, :], m.misfit[:, :], worst[:, CHECKS:], ALU.max).then_inc(s.worst, 1)
                dve.wait_ge(s.out_mm, len(blocks))
                for t in range(NT):
                    dve.tensor_tensor(m.x[:, t, :], m.x[:, t, :], m.ps[:, t * D:(t + 1) * D], ALU.add).then_inc(s.y_ready, 1)

            @block.tensor
            def _(pe):
                for t in range(NT):
                    last = pe.transpose(bank(m.ps, 4, t * H0, (t + 1) * H0), dens[:, t * P:(t + 1) * P], m.ident[0:H0, 0:H0])
                last.then_inc(s.dens_turned, 1)
                pe.wait_ge(s.hilo_ready, 1)
                for t in range(NT):
                    last = pe.transpose(bank(m.ps, 5, t * P, (t + 1) * P), hilo[:, t, :, :].rearrange("p a b -> p (a b)"),
                                        m.ident[:, :])
                    if t % 4 == 3:
                        last.then_inc(s.gmT_mm, 1)
                for i in range(len(blocks) + AHEAD):
                    if i < len(blocks):
                        c, e, n = blocks[i]
                        pe.wait_ge(s.gmT_ready, NH)
                        if i >= 4:
                            pe.wait_ge(s.routed, i - 3)
                        pe.matmul(bank(m.ps, 4 + i % 4), sel[:, c * NE + e, :], gmT[:, n * HALF:(n + 1) * HALF],
                                  start=True, stop=True).then_inc(s.mask_mm, 1)
                    if i >= AHEAD:
                        k = i - AHEAD
                        c, e, n = blocks[k]
                        pe.wait_ge(s.oe_lo, 2 * c + e // EH + 1)
                        pe.wait_ge(s.routed_lo, k + 1)
                        for j in range(HALF // P):
                            t, cols = n * (HALF // P) + j, slice(j * P, (j + 1) * P)
                            for r, w in ((rhi, ohi), (rhi, olo), (rlo, ohi)):
                                last = pe.matmul(m.ps[:, t * D:(t + 1) * D], r[:, k % RT, cols], w[:, c % 2, e, :],
                                                 start=(c == e == 0 and t % 2 == 0 and r is rhi and w is ohi),
                                                 stop=(c == H0 // 2 - 1 and e == NE - 1 and r is rlo), skip_group_check=True)
                        last.then_inc(s.out_mm, 1)

    with nc.Fori(0, SEQS) as b:
        with ExitStack() as own:
            gates_and_values(own)
        with ExitStack() as own:
            attention(own, b)
        with ExitStack() as own:
            output_experts(own, b)

    return ld, s0, s1, s2, s3



PROJ3 = ("transposed xT_ready x_copied qk_mm z_ready lo_ready stack_mm act_stacked dve_stacked h_mm v_mm v_read chain var_ready sd_ready hn_ready gelu_ready drift_ready "
         "g_ready g_gelu gate_in gate_ready vx_ready")
ATTN3 = "max_mm max_read shift_ready late_shift_ready score_mm exp_ready pv_mm o_read" + FETCH
OUT3 = "bias_added turned rden o_ready turned_back oT_ready out_mm y_ready y_out"


def layer3(nc, ctx, m, I, src, dst):
    sb = lambda name, shape, dt=F32: ctx.enter_context(nc.sbuf_tensor("l3_" + name, shape, dt))
    GROUPS = H1 // G1
    R = 4 * DH1
    HPC = P // R
    QC = H1 // HPC
    HF = 128
    GF = 16
    wq, wk, wv, wo = sb("wq", [P, KC, D]), sb("wk", [P, KC, D]), sb("wv", [P, KC, D]), sb("wo", [P, KC, D])
    bq, bk, bv, bo = sb("bq", [P, KC]), sb("bk", [P, KC]), sb("bv", [P, D]), sb("bo", [P, D])
    w1 = sb("w1", [P, KC, HF])
    hv = sb("hv", [P, 4, HF])
    gv = sb("gv", [P, 3, GF])
    b2 = sb("b2", [P, 2])
    select = sb("select", [P, 2, 2, 4, P], F32R)
    qst, kst = sb("qst", [P, QC, T], F32R), sb("kst", [P, QC, T], F32R)
    vx = sb("vx", [P, NT, H1, 2 * DH1])
    ld = signals(nc, ctx, "l3_load", "weights ones select")
    s0 = signals(nc, ctx, "l3_first", FETCH)
    s1 = signals(nc, ctx, "l3_proj", PROJ3)
    s2 = signals(nc, ctx, "l3_attn", ATTN3)
    s3 = signals(nc, ctx, "l3_out", OUT3)

    with ExitStack() as own:
        given = own.enter_context(nc.sbuf_tensor("l3_select_given", [P, 2 * 2 * 4 * P], F32))
        def load(sp):
            pairs = [(wq, "wq3"), (wk, "wk3"), (wv, "wv3"), (wo, "wo3"), (bq, "bq3"), (bk, "bk3"), (bv, "bv3"), (bo, "bo3"),
                     (w1, "w13"), (hv, "hv3"), (gv, "gv3"), (b2, "b23")]
            for tile, name in pairs:
                sp.dma_start(tile[:], I[name]).then_inc(ld.weights, 16)
            sp.dma_start(given[:, :], I["select3"]).then_inc(ld.weights, 16)
            sp.wait_ge(ld.weights, 16 * (len(pairs) + 1))

        def prepare(dve):
            dve.memset(vx[:, :, :, :], 1.0).then_inc(ld.ones, 1)
            dve.wait_ge(ld.weights, 16 * 13)
            dve.tensor_copy(select[:, :, :, :, :].rearrange("p a b r n -> p (a b r n)"),
                            given[:, :]).then_inc(ld.select, 1)

        fetch_first(nc, m, s0, src[0], load, prepare)

    def projections(own):
        sb = lambda name, shape, dt=F32: own.enter_context(nc.sbuf_tensor("l3a_" + name, shape, dt))
        xT = sb("xT", [P, KC, T])
        RZ = 4
        z, zhi, zlo = sb("z", [P, RZ, HALF]), sb("zhi", [P, RZ, HALF], F32R), sb("zlo", [P, RZ, HALF], F32R)
        v = sb("v", [P, NT, D])
        h = sb("h", [P, NT, HF])
        g = sb("g", [P, NT, GF])
        st, mom, sd, r = sb("st", [P, NT, 6]), sb("mom", [P, NT, 2]), sb("sd", [P, NT]), sb("r", [P, NT])
        drift, gate = sb("drift", [P, NT]), sb("gate", [P, NT])
        items = [(c, n, kind) for c in range(KC) for n in range(NH) for kind in (0, 1)]
        VECTOR_FROM = 3
        by_vector = lambda j: j % 2 == 1 and j // 2 >= VECTOR_FROM
        vectors_to = lambda j: sum(by_vector(jj) for jj in range(j + 1))
        scalars_to = lambda j: j + 1 - vectors_to(j)
        PROJ, HIDDEN, VALUE = 6, 4, 4
        GELU_AFTER, G_GELU_AFTER, TANH_AFTER = 1, 2, 3

        def spread(j):
            c, n, kind = items[j // 2]
            at, first = 2 * (j % 2), 4 * c + 2 * (j % 2)
            return (m.ps[:, at * HALF:(at + 2) * HALF].rearrange("p (a n) -> p a n", a=2),
                    (kst if kind else qst)[:, first:first + 2, n * HALF:(n + 1) * HALF])

        s = s1
        with nc.Block() as block:
            @block.tensor
            def _(pe):
                entry_transpose(pe, m, s)
                for t in range(NT):
                    pe.wait_ge(s.xT_ready, t + 1)
                    for c in range(KC):
                        last = pe.matmul(bank(m.ps, HIDDEN, t * HF, (t + 1) * HF), xT[:, c, t * P:(t + 1) * P], w1[:, c, :],
                                         start=(c == 0), stop=(c == KC - 1))
                    last.then_inc(s.h_mm, 1)
                def project(i):
                    c, n, kind = items[i]
                    if i >= 2:
                        pe.wait_ge(s.z_ready, i - 1)
                    for kc in range(KC):
                        last = pe.matmul(bank(m.ps, PROJ + i % 2), (wk if kind else wq)[:, kc, c * P:(c + 1) * P],
                                         xT[:, kc, n * HALF:(n + 1) * HALF], start=(kc == 0), stop=(kc == KC - 1))
                    last.then_inc(s.qk_mm, 1)

                for i in range(2):
                    project(i)
                for i, (c, n, kind) in enumerate(items):
                    if i + 2 < len(items):
                        project(i + 2)
                    pe.wait_ge(s.lo_ready, i + 1)
                    for j in (2 * i, 2 * i + 1):
                        if j >= 2:
                            k = j - 2
                            pe.wait_ge(s.dve_stacked if by_vector(k) else s.act_stacked,
                                       vectors_to(k) if by_vector(k) else scalars_to(k))
                        for a in range(2):
                            r = 2 * (j % 2) + a
                            pe.matmul(bank(m.ps, r), select[:, kind, 0, r, :], zhi[:, i % RZ, :], start=True, stop=False)
                            last = pe.matmul(bank(m.ps, r), select[:, kind, 1, r, :], zlo[:, i % RZ, :], start=False, stop=True)
                        last.then_inc(s.stack_mm, 1)
                    t = i
                    if t < 2:
                        pe.wait_ge(s.var_ready, NT)
                    else:
                        pe.wait_ge(s.v_read, t - 1)
                    for kc in range(KC):
                        last = pe.matmul(bank(m.ps, VALUE + t % 2, 0, D), xT[:, kc, t * P:(t + 1) * P], wv[:, kc, :],
                                         start=(kc == 0), stop=(kc == KC - 1))
                    last.then_inc(s.v_mm, 1)

            @block.scalar
            def _(act):
                entry_copy(act, m, s, xT)
                act.wait_ge(s.var_ready, NT)
                act.activation(sd[:, :], mom[:, :, 1], ACT.Sqrt, bias=m.eps[:, 0:1]).then_inc(s.sd_ready, 1)
                def split(i):
                    c, n, kind = items[i]
                    act.wait_ge(s.qk_mm, i + 1)
                    if i >= RZ:
                        act.wait_ge(s.stack_mm, 2 * (i - RZ + 1))
                    for out in (zhi, z):
                        last = act.activation(out[:, i % RZ, :], bank(m.ps, PROJ + i % 2), ACT.Identity,
                                              bias=(bk if kind else bq)[:, c:c + 1])
                    last.then_inc(s.z_ready, 1)

                for i in range(2):
                    split(i)
                for i in range(len(items)):
                    if i + 2 < len(items):
                        split(i + 2)
                    for j in (2 * i, 2 * i + 1):
                        if not by_vector(j):
                            act.wait_ge(s.stack_mm, j + 1)
                            got, to = spread(j)
                            act.copy(to, got).then_inc(s.act_stacked, 1)
                    if i == GELU_AFTER:
                        act.wait_ge(s.hn_ready, 1)
                        act.activation(h[:, :, :], h[:, :, :], ACT.Gelu).then_inc(s.gelu_ready, 1)
                    if i == G_GELU_AFTER:
                        act.wait_ge(s.g_ready, 1)
                        act.activation(g[:, :, :], g[:, :, :], ACT.Gelu).then_inc(s.g_gelu, 1)
                    if i == TANH_AFTER:
                        act.wait_ge(s.gate_in, 1)
                        act.activation(gate[:, :], drift[:, :], ACT.Tanh, bias=b2[:, 1:2]).then_inc(s.gate_ready, 1)

            @block.gpsimd
            def _(pool):
                clear(pool, s3)
                entry_residual(pool, m, s)
                for i in range(len(items)):
                    pool.wait_ge(s.z_ready, i + 1)
                    pool.tensor_tensor(zlo[:, i % RZ, :], z[:, i % RZ, :], zhi[:, i % RZ, :].bitcast(F32),
                                       ALU.subtract).then_inc(s.lo_ready, 1)

            @block.vector
            def _(dve):
                step = Chain(dve, s.chain)
                over_t = lambda row, w: row.unsqueeze(1).to_broadcast([P, NT, w])
                over_f = lambda col, w: col.unsqueeze(2).to_broadcast([P, NT, w])

                def stack(i):
                    j = 2 * i + 1
                    dve.wait_ge(s.stack_mm, j + 1)
                    got, to = spread(j)
                    dve.tensor_copy(to, got).then_inc(s.dve_stacked, 1)

                def value(t):
                    dve.wait_ge(s.v_mm, t + 1)
                    dve.tensor_tensor(v[:, t, :], bank(m.ps, VALUE + t % 2, 0, D), bv[:, :], ALU.add).then_inc(s.v_read, 1)

                def gated(t):
                    dve.wait_ge(s.v_read, t + 1)
                    dve.tensor_scalar(vx[:, t, :, 0:DH1], v[:, t, :].rearrange("p (h k) -> p h k", h=H1), gate[:, t:t + 1],
                                      None, ALU.mult).then_inc(s.vx_ready, 1)

                dve.wait_ge(s.h_mm, NT)
                step(dve.tensor_tensor(h[:, :, :], bank(m.ps, HIDDEN, 0, NT * HF).rearrange("p (t f) -> p t f", t=NT),
                                       over_t(hv[:, 0, :], HF), ALU.add))
                for t in range(NT):
                    last = dve.bn_stats(st[:, t, :], h[:, t, :])
                step(last)
                for t in range(NT):
                    dve.bn_aggr(mom[:, t, :], st[:, t, :]).then_inc(s.var_ready, 1)
                dve.wait_ge(s.sd_ready, 1)
                inverse_sd(step, dve, m, r[:, :], mom[:, :, 1], sd[:, :])
                step(dve.tensor_tensor(h[:, :, :], h[:, :, :], over_f(mom[:, :, 0], HF), ALU.subtract))
                step(dve.tensor_tensor(h[:, :, :], h[:, :, :], over_f(r[:, :], HF), ALU.mult))
                step(dve.tensor_tensor(h[:, :, :], h[:, :, :], over_t(hv[:, 1, :], HF), ALU.mult))
                dve.tensor_tensor(h[:, :, :], h[:, :, :], over_t(hv[:, 2, :], HF), ALU.add).then_inc(s.hn_ready, 1)
                value(0)
                value(1)
                dve.wait_ge(s.gelu_ready, 1)
                step(dve.tensor_tensor(h[:, :, :], h[:, :, :], over_t(hv[:, 3, :], HF), ALU.mult))
                step(dve.tensor_reduce(drift[:, :], h[:, :, :], AX_X, ALU.add))
                step(dve.tensor_scalar(drift[:, :], drift[:, :], b2[:, 0:1], None, ALU.add))
                step(dve.tensor_tensor(g[:, :, :], over_f(drift[:, :], GF), over_t(gv[:, 0, :], GF), ALU.mult))
                dve.tensor_tensor(g[:, :, :], g[:, :, :], over_t(gv[:, 1, :], GF), ALU.add).then_inc(s.g_ready, 1)
                value(2)
                dve.wait_ge(s.g_gelu, 1)
                step(dve.tensor_tensor(g[:, :, :], g[:, :, :], over_t(gv[:, 2, :], GF), ALU.mult))
                dve.tensor_reduce(drift[:, :], g[:, :, :], AX_X, ALU.add).then_inc(s.gate_in, 1)
                for i in range(VECTOR_FROM, NT):
                    stack(i)
                    value(i)
                    if i == VECTOR_FROM:
                        dve.wait_ge(s.gate_ready, 1)
                        for t in range(VECTOR_FROM):
                            gated(t)
                    gated(i)

    def attention(own, oraw, b):
        sb = lambda name, shape, dt=F32: own.enter_context(nc.sbuf_tensor("l3b_" + name, shape, dt))
        shift = sb("shift", [P, 2, G1, T], F32R)
        prob = sb("prob", [P, 2, G1, T])
        mx = sb("mx", [P, H1, NT])
        s = s2
        WIDE = HALF // P
        units = [(k, (i,)) for k in range(WIDE) for i in range(G1)] + \
                [(k, (i, i + 1)) for k in range(WIDE, NT) for i in range(0, G1, 2)]
        U = len(units)
        beside = [[n] for n in range(U - 4)] + [[U - 4, U - 3], [U - 2, U - 1], [], []]

        def through(k):
            return 2 * sum(kk <= k for kk, _ in units)

        def two_parts(heads, lo, hi):
            return [(i, a, z) for i in heads for a, z in halves(lo, hi)]

        def rows(h):
            return slice(R * (h % HPC), R * (h % HPC) + R)

        def max_region(n, heads, hi):
            if len(heads) == 1:
                return bank(m.ps, MAX[n % 2], 0, hi)
            return m.ps[:, MAX[n % 2] * HALF:(MAX[n % 2] + 2) * HALF].rearrange("p (a n) -> p a n", a=2)[:, :, 0:hi]

        LATE = 4
        SCORE, MAX = (2, 3), (4, 6)

        with nc.Block() as block:
            @block.sync
            def _(sp):
                fetch_load(sp, m, s, src[(b + 1) % SEQS])

            @block.tensor
            def _(pe):
                def maxima_part(g, n, j):
                    k, heads = units[n % U]
                    t = NT - 1 - k
                    if j == 0 and n >= 2:
                        pe.wait_ge(s.max_read, n - 1)
                    parts = two_parts(heads, 0, (t + 1) * P)
                    i, lo, hi = parts[j]
                    h, rr = G1 * g + i, rows(G1 * g + i)
                    at = MAX[n % 2] + (j if len(heads) == 2 else 0)
                    last = pe.matmul(bank(m.ps, at, lo, hi), qst[rr, h // HPC, t * P:(t + 1) * P], kst[rr, h // HPC, lo:hi],
                                     start=True, stop=True)
                    if hi == (t + 1) * P:
                        last = pe.matmul(bank(m.ps, at, t * P, hi), m.ident16[:, :], m.mask_qk[:, :],
                                         start=False, stop=True, skip_group_check=True)
                    if j == 1:
                        last.then_inc(s.max_mm, 1)

                def scores_part(g, n, j):
                    k, heads = units[n % U]
                    part = 2 * n + j
                    if part >= 2:
                        pe.wait_ge(s.exp_ready, part - 1)
                    if n % U == 0 and j == 0:
                        pe.wait_ge(s.shift_ready, (U - LATE) * (g + 1))
                        pe.wait_ge(s.late_shift_ready, LATE * (g + 1))
                    i, lo, hi = two_parts(heads, k * P, T)[j]
                    h, rr = G1 * g + i, rows(G1 * g + i)
                    out = bank(m.ps, SCORE[j], 0, hi - lo)
                    pe.matmul(out, kst[rr, h // HPC, k * P:(k + 1) * P], qst[rr, h // HPC, lo:hi], start=True, stop=False)
                    if lo == k * P:
                        pe.matmul(bank(m.ps, SCORE[j], 0, P), m.ident16[:, :], m.mask_kq[:, :], start=False, stop=False)
                    pe.matmul(out, m.negones[:, :], shift[:, g % 2, i, lo:hi], start=False, stop=True).then_inc(s.score_mm, 1)

                def weighted(g, k):
                    pe.wait_ge(s.exp_ready, 2 * U * g + through(k))
                    if k == 0 and g:
                        pe.wait_ge(s.o_read, g)
                    for lo, hi in halves(k * P, T):
                        for i in range(G1):
                            last = pe.matmul(bank(m.ps, 0, lo, hi, slice(32 * i, 32 * i + 32)), vx[:, k, G1 * g + i, :],
                                             prob[:, k % 2, i, lo:hi], start=(k == 0), stop=True, skip_group_check=True)
                    last.then_inc(s.pv_mm, 1)

                for g in range(GROUPS + 1):
                    for n, (k, heads) in enumerate(units):
                        maxes = beside[n] if g < GROUPS else []
                        for j in range(2):
                            if g >= 1:
                                scores_part(g - 1, U * (g - 1) + n, j)
                            if maxes:
                                maxima_part(g, U * g + maxes[0], j)
                        for more in maxes[1:]:
                            for j in range(2):
                                maxima_part(g, U * g + more, j)
                        if g >= 1 and k >= 1 and 1 in heads:
                            weighted(g - 1, k - 1)
                    if g >= 1:
                        weighted(g - 1, NT - 1)

            @block.scalar
            def _(act):
                for g in range(GROUPS):
                    if g == 2:
                        fetch_sd(act, m, s)
                    for n, (k, heads) in enumerate(units, U * g):
                        for j, (i, lo, hi) in enumerate(two_parts(heads, k * P, T)):
                            act.wait_ge(s.score_mm, 2 * n + j + 1)
                            if heads[0] == 0 and NT * g + k >= 2:
                                act.wait_ge(s.pv_mm, NT * g + k - 1)
                            act.activation(prob[:, k % 2, i, lo:hi], bank(m.ps, SCORE[j], 0, hi - lo), ACT.Exp,
                                           scale=SCALE1).then_inc(s.exp_ready, 1)

            @block.vector
            def _(dve):
                def group_out(g):
                    dve.wait_ge(s.pv_mm, NT * (g + 1))
                    dve.tensor_copy(oraw[:, g, :], bank(m.ps, 0, 0, T)).then_inc(s.o_read, 1)

                for g in range(GROUPS):
                    for n, (k, heads) in enumerate(units, U * g):
                        if g == 1 and n == U * g + 4:
                            fetch_stats(dve, m, s)
                        if g == 3 and n == U * g + 4:
                            fetch_norm(dve, m, s)
                        t, h = NT - 1 - k, G1 * g + heads[0]
                        dve.wait_ge(s.max_mm, n + 1)
                        out = mx[:, h, t:t + 1] if len(heads) == 1 else mx[:, h:h + 2, t]
                        dve.reduce_max(out, max_region(n, heads, (t + 1) * P), AX_X).then_inc(s.max_read, 1)
                        if n % U >= U - LATE:
                            dve.wait_ge(s.max_read, n + 1)
                            if g >= 2:
                                dve.wait_ge(s.score_mm, 2 * U * (g - 1))
                            for i in heads:
                                last = dve.tensor_scalar(shift[:, g % 2, i, t * P:(t + 1) * P], m.ident[:, :],
                                                         mx[:, G1 * g + i, t:t + 1], None, ALU.mult)
                            last.then_inc(s.late_shift_ready, 1)
                        if g >= 2 and n == U * g:
                            group_out(g - 2)
                for g in range(GROUPS - 2, GROUPS):
                    group_out(g)

            @block.gpsimd
            def _(pool):
                clear(pool, s1)
                for g in range(GROUPS):
                    if g >= 2:
                        pool.wait_ge(s.score_mm, 2 * U * (g - 1))
                    for n, (k, heads) in enumerate(units[:U - LATE], U * g):
                        t = NT - 1 - k
                        pool.wait_ge(s.max_read, n + 1)
                        for i in heads:
                            last = pool.tensor_scalar(shift[:, g % 2, i, t * P:(t + 1) * P], m.ident[:, :],
                                                      mx[:, G1 * g + i, t:t + 1], None, ALU.mult)
                        last.then_inc(s.shift_ready, 1)

    def output(own, oraw, b):
        sb = lambda name, shape, dt=F32: own.enter_context(nc.sbuf_tensor("l3c_" + name, shape, dt))
        y = sb("y", [P, NT, D])
        rden = sb("rden", [P, 2, H1])
        o = sb("o", [P, 2, D])
        oT = sb("oT", [P, 2, KC, P])
        s = s3
        with nc.Block() as block:
            @block.tensor
            def _(pe):
                for step in range(NT + 2):
                    if step < NT:
                        t = step
                        if t >= 2:
                            pe.wait_ge(s.o_ready, t - 1)
                        for g in range(GROUPS):
                            last = pe.transpose(bank(m.ps, t % 2, g * P, (g + 1) * P), oraw[:, g, t * P:(t + 1) * P], m.ident[:, :])
                        last.then_inc(s.turned, 1)
                    if 1 <= step <= NT:
                        t = step - 1
                        pe.wait_ge(s.o_ready, t + 1)
                        if t >= 2:
                            pe.wait_ge(s.oT_ready, t - 1)
                        for c in range(KC):
                            last = pe.transpose(bank(m.ps, 2 + t % 2, c * P, (c + 1) * P), o[:, t % 2, c * P:(c + 1) * P], m.ident[:, :])
                        last.then_inc(s.turned_back, 1)
                    if step >= 2:
                        t = step - 2
                        pe.wait_ge(s.oT_ready, t + 1)
                        if t >= 2:
                            pe.wait_ge(s.y_ready, t - 1)
                        for c in range(KC):
                            last = pe.matmul(bank(m.ps, 4 + t % 2, 0, D), oT[:, t % 2, c, :], wo[:, c, :],
                                             start=(c == 0), stop=(c == KC - 1))
                        last.then_inc(s.out_mm, 1)

            @block.scalar
            def _(act):
                for t in range(NT):
                    act.wait_ge(s.turned_back, t + 1)
                    if t >= 2:
                        act.wait_ge(s.out_mm, t - 1)
                    act.copy(oT[:, t % 2, :, :], bank(m.ps, 2 + t % 2, 0, D).rearrange("p (c q) -> p c q", c=KC)).then_inc(s.oT_ready, 1)

            @block.vector
            def _(dve):
                dve.tensor_tensor(m.x[:, :, :], m.x[:, :, :], bo[:, :].unsqueeze(1).to_broadcast([P, NT, D]), ALU.add).then_inc(s.bias_added, 1)
                for step in range(NT + 2):
                    if step < NT:
                        t = step
                        heads = bank(m.ps, t % 2).rearrange("p (h k) -> p h k", h=H1)
                        dve.wait_ge(s.turned, t + 1)
                        dve.reciprocal(rden[:, t % 2, :], heads[:, :, DH1]).then_inc(s.rden, 1)
                        dve.wait_ge(s.rden, t + 1)
                        if t >= 2:
                            dve.wait_ge(s.turned_back, t - 1)
                        dve.tensor_tensor(o[:, t % 2, :].rearrange("p (h k) -> p h k", h=H1), heads[:, :, 0:DH1],
                                          rden[:, t % 2, :].unsqueeze(2).to_broadcast([P, H1, DH1]), ALU.mult).then_inc(s.o_ready, 1)
                    if step >= 2:
                        t = step - 2
                        dve.wait_ge(s.bias_added, 1)
                        dve.wait_ge(s.out_mm, t + 1)
                        dve.tensor_tensor(y[:, t, :], bank(m.ps, 4 + t % 2, 0, D), m.x[:, t, :], ALU.add).then_inc(s.y_ready, 1)

            @block.gpsimd
            def _(pool):
                clear(pool, s2)

            @block.sync
            def _(sp):
                store(sp, s, y, dst[b])

    with nc.Fori(0, SEQS) as b:
        with ExitStack() as own:
            projections(own)
        with ExitStack() as own:
            oraw = own.enter_context(nc.sbuf_tensor("l3_oraw", [P, GROUPS, T], F32))
            with ExitStack() as inner:
                attention(inner, oraw, b)
            with ExitStack() as inner:
                output(inner, oraw, b)

    return ld, s0, s1, s2, s3



LOAD4 = "w1_in w2_in h1_in h2_in w3_in scales_in ones total flag_ready"
NET4 = ("mm silu_ready mul_ready gelu_ready hi_ready h_ready out_mm scaled y_ready y_out x_hi "
        "y_stats y_moments y_sd y_chain" + ENTRY + FETCH)
WEIGHTS4 = [("w14", KC, HID), ("w24", KC, HID), ("h14", HC, HID), ("h24", HC, HID), ("w34", HC, D)]


def layer4(nc, ctx, m, I, src, dst):
    sb = lambda name, shape, dt=F32: ctx.enter_context(nc.sbuf_tensor("l4_" + name, shape, dt))
    weights = [sb(name, [P, c, n], F32R) for name, c, n in WEIGHTS4]
    w1, w2, h1, h2, w3 = weights
    scale = sb("scale", [P, 4, HC])
    s3v = sb("s3", [P, D])
    flag = sb("flag", [1, 1], mybir.dt.int32)
    ld = signals(nc, ctx, "l4_load", LOAD4)
    s0 = signals(nc, ctx, "l4_first", FETCH)
    s1 = signals(nc, ctx, "l4_net", NET4)

    arrived = (ld.w1_in, ld.w2_in, ld.h1_in, ld.h2_in, ld.w3_in)

    ones = sb("ones", [P, 1])

    def load(sp):
        sp.wait_ge(m.weights_copied, 16 * len(WEIGHTS4))
        at = 0
        for weight, come, (_name, c, n) in zip(weights, arrived, WEIGHTS4):
            sp.dma_start(weight[:, :, :].rearrange("p c n -> p (c n)").bitcast(F32),
                         m.weights_copy[:, at:at + c * n]).then_inc(come, 16)
            at += c * n
        sp.dma_start(scale[:], I["scale4"]).then_inc(ld.scales_in, 16)
        sp.dma_start(s3v[:], I["s34"]).then_inc(ld.scales_in, 16)

    def prepare(dve):
        dve.memset(ones[:, :], 1.0).then_inc(ld.ones, 1)

    fetch_first(nc, m, s0, src[0], load, prepare)
    with nc.Block() as block:
        @block.vector
        def _(dve):
            dve.wait_ge(ld.total, 1)
            dve.tensor_copy(flag[:, :], bank(m.ps, 0, 0, 1, slice(0, 1))).then_inc(ld.flag_ready, 1)

        @block.tensor
        def _(pe):
            pe.matmul(bank(m.ps, 0, 0, 1, slice(0, 1)), m.misfit[:, :], ones[:, :], start=True,
                      stop=True).then_inc(ld.total, 1)

    def net(own, b):
        sb = lambda name, shape, dt=F32: own.enter_context(nc.sbuf_tensor("l4a_" + name, shape, dt))
        xhi, xlo = sb("xhi", [P, KC, T], F32R), sb("xlo", [P, KC, T], F32R)
        uhi, ulo = sb("uhi", [P, 2, HC, HALF], F32R), sb("ulo", [P, 2, HC, HALF], F32R)
        RT = 3
        sil, made = sb("sil", [P, 2, HALF]), sb("made", [P, RT, HALF])
        s = s1
        OUTS = HALF // P
        ystats, ymom = sb("ystats", [P, NH, OUTS, 6]), sb("ymom", [P, NH, OUTS, 2])
        ysd, yr = sb("ysd", [P, NH, OUTS]), sb("yr", [P, NH, OUTS])
        per_n = 4 * HC
        RB = 6

        def at(n, stage, o):
            return per_n * n + (2 * o if stage == 0 else 2 * HC + (stage - 1) * HC + o)

        def chunk(n, stage, o):
            return HC * (3 * n + stage) + o

        def slot(n, stage):
            return (3 * n + stage) % 2

        with nc.Block() as block:
            @block.tensor
            def _(pe):
                entry_transpose(pe, m, s)
                misfit = pe.value_load(flag[0:1, 0:1])

                def wait_free(i):
                    n, r = divmod(i - RB, per_n)
                    if r < 2 * HC:
                        pe.wait_ge(s.mul_ready if r % 2 else s.silu_ready, HC * n + r // 2 + 1)
                    else:
                        pe.wait_ge(s.gelu_ready, 2 * HC * n + r - 2 * HC + 1)

                def run(passes):
                    def product(i, w, kc, o, hi, lo, ready=None):
                        if i >= RB:
                            wait_free(i)
                        for c in range(kc):
                            if ready is not None:
                                pe.wait_ge(s.h_ready, ready + c + 1)
                            for part in (hi, lo):
                                last = passes(bank(m.ps, i % RB), w[:, c, o * P:(o + 1) * P], part(c), c == 0 and part is hi,
                                              c == kc - 1 and part is lo)
                        last.then_inc(s.mm, 1)

                    pe.wait_ge(s.xT_ready, NT)
                    pe.wait_ge(ld.w1_in, 16)
                    pe.wait_ge(ld.w2_in, 16)
                    for n in range(NH):
                        cols = slice(n * HALF, (n + 1) * HALF)
                        for o in range(HC):
                            for j, w in enumerate((w1, w2)):
                                product(at(n, 0, o) + j, w, KC, o, lambda c: xhi[:, c, cols], lambda c: xlo[:, c, cols])
                        for stage, w in ((1, h1), (2, h2)):
                            u = slot(n, stage - 1)
                            pe.wait_ge((ld.h1_in, ld.h2_in)[stage - 1], 16)
                            for o in range(HC):
                                product(at(n, stage, o), w, HC, o, lambda c: uhi[:, u, c, :], lambda c: ulo[:, u, c, :],
                                        ready=chunk(n, stage - 1, 0) if o == 0 else None)
                        u = slot(n, 2)
                        pe.wait_ge(ld.w3_in, 16)
                        for j in range(OUTS):
                            t = n * OUTS + j
                            if t >= 2:
                                pe.wait_ge(s.scaled, t - 1)
                            for c in range(HC):
                                if j == 0:
                                    pe.wait_ge(s.h_ready, chunk(n, 2, c) + 1)
                                for part in (uhi, ulo):
                                    last = passes(bank(m.ps, 6 + t % 2, 0, D), part[:, u, c, j * P:(j + 1) * P], w3[:, c, :],
                                                  c == 0 and part is uhi, c == HC - 1 and part is ulo)
                            last.then_inc(s.out_mm, 1)

                with pe.If(misfit > 0):
                    run(lambda out, a, x, first, last: pe.matmul(out, a.bitcast(F32), x.bitcast(F32), start=first, stop=last))
                with pe.Else():
                    run(lambda out, a, x, first, last: pe.matmul(out, a, x, start=first, stop=last))

            @block.scalar
            def _(act):
                for t in range(NT):
                    act.wait_ge(s.transposed, t + 1)
                    act.copy(xhi[:, :, t * P:(t + 1) * P],
                             bank(m.ps, t % ENTRY_BANKS, 0, D).rearrange("p (c q) -> p c q", c=KC)).then_inc(s.x_hi, 1)
                act.wait_ge(ld.scales_in, 32)

                def hi_part(n, stage, o, ready, count):
                    act.wait_ge(ready, count)
                    k = chunk(n, stage, o)
                    act.copy(uhi[:, slot(n, stage), o, :], made[:, k % RT, :]).then_inc(s.hi_ready, 1)

                for n in range(NH):
                    for o in range(HC + 1):
                        if o < HC:
                            i, k = at(n, 0, o), HC * n + o
                            act.wait_ge(s.mm, i + 1)
                            if k >= 2:
                                act.wait_ge(s.mul_ready, k - 1)
                            act.activation(sil[:, k % 2, :], bank(m.ps, i % RB), ACT.Silu,
                                           scale=scale[:, 0, o:o + 1]).then_inc(s.silu_ready, 1)
                        if o >= 1:
                            hi_part(n, 0, o - 1, s.mul_ready, HC * n + o)
                    for stage in (1, 2):
                        for o in range(HC):
                            i, k = at(n, stage, o), chunk(n, stage, o)
                            act.wait_ge(s.mm, i + 1)
                            act.wait_ge(s.h_ready, k - RT + 1)
                            act.activation(made[:, k % RT, :], bank(m.ps, i % RB), ACT.Gelu,
                                           scale=scale[:, 1 + stage, o:o + 1]).then_inc(s.gelu_ready, 1)
                            hi_part(n, stage, o, s.gelu_ready, HC * (2 * n + stage - 1) + o + 1)
                    if n == 0:
                        fetch_sd(act, m, s)
                    act.wait_ge(s.y_moments, n + 1)
                    act.activation(ysd[:, n, :], ymom[:, n, :, 1], ACT.Sqrt, bias=m.eps[:, 0:1]).then_inc(s.y_sd, 1)

            @block.vector
            def _(dve):
                step = Chain(dve, s.y_chain)

                def split(k, slot_, o):
                    dve.wait_ge(s.hi_ready, k + 1)
                    dve.tensor_tensor(ulo[:, slot_, o, :], made[:, k % RT, :], uhi[:, slot_, o, :].bitcast(F32),
                                      ALU.subtract).then_inc(s.h_ready, 1)

                def outputs(n):
                    for j in range(OUTS):
                        t = n * OUTS + j
                        dve.wait_ge(s.out_mm, t + 1)
                        dve.tensor_tensor(made[:, j % RT, 0:D], bank(m.ps, 6 + t % 2, 0, D), s3v[:, :], ALU.mult).then_inc(s.scaled, 1)
                        dve.wait_ge(s.scaled, t + 1)
                        step(dve.tensor_tensor(m.x[:, t, :], made[:, j % RT, 0:D], m.x[:, t, :], ALU.add))
                        last = dve.bn_stats(ystats[:, n, j, :], m.x[:, t, :])
                    last.then_inc(s.y_stats, 1)
                    dve.wait_ge(s.y_stats, n + 1)
                    for j in range(OUTS):
                        last = dve.bn_aggr(ymom[:, n, j, :], ystats[:, n, j, :])
                    last.then_inc(s.y_moments, 1)

                def normed(n):
                    dve.wait_ge(s.y_sd, n + 1)
                    inverse_sd(step, dve, m, yr[:, n, :], ymom[:, n, :, 1], ysd[:, n, :])
                    for j in range(OUTS):
                        t = n * OUTS + j
                        dve.tensor_scalar(m.x[:, t, :], m.x[:, t, :], ymom[:, n, j, 0:1], yr[:, n, j:j + 1], ALU.subtract,
                                          ALU.mult).then_inc(s.y_ready, 1)

                for t in range(NT):
                    dve.wait_ge(s.x_hi, t + 1)
                    cols = slice(t * P, (t + 1) * P)
                    dve.tensor_tensor(xlo[:, :, cols], bank(m.ps, t % ENTRY_BANKS, 0, D).rearrange("p (c q) -> p c q", c=KC),
                                      xhi[:, :, cols].bitcast(F32), ALU.subtract).then_inc(s.xT_ready, 1)
                dve.wait_ge(s.x_copied, 1)
                dve.wait_ge(ld.scales_in, 32)
                for n in range(NH):
                    for o in range(HC + 1):
                        if o < HC:
                            i, k = at(n, 0, o) + 1, chunk(n, 0, o)
                            dve.wait_ge(s.mm, i + 1)
                            dve.wait_ge(s.silu_ready, HC * n + o + 1)
                            if k >= RT:
                                dve.wait_ge(s.h_ready, k - RT + 1)
                            dve.scalar_tensor_tensor(made[:, k % RT, :], bank(m.ps, i % RB), scale[:, 1, o:o + 1],
                                                     sil[:, (HC * n + o) % 2, :], ALU.mult, ALU.mult).then_inc(s.mul_ready, 1)
                        if o >= 1:
                            split(chunk(n, 0, o - 1), slot(n, 0), o - 1)
                        if n == 1 and o == 1:
                            normed(0)
                            fetch_norm(dve, m, s)
                    for stage in (1, 2):
                        for o in range(HC):
                            split(chunk(n, stage, o), slot(n, stage), o)
                        if n == 0 and stage == 1:
                            fetch_stats(dve, m, s)
                    outputs(n)
                normed(NH - 1)

            @block.gpsimd
            def _(pool):
                entry_residual(pool, m, s)

            @block.sync
            def _(sp):
                sp.wait_ge(s.transposed, NT)
                sp.wait_ge(s.x_copied, 1)
                fetch_load(sp, m, s, src[(b + 1) % SEQS])
                store(sp, s, m.x, dst[b])

    with nc.Fori(0, SEQS) as b:
        with ExitStack() as own:
            net(own, b)
        with nc.Block() as block:
            @block.gpsimd
            def _(pool):
                clear(pool, s1)

    return ld, s0, s1



def program(nc, I, layers, src, scratch):
    with ExitStack() as ctx:
        sb = lambda name, shape, dt=F32: ctx.enter_context(nc.sbuf_tensor("sb_" + name, shape, dt))
        m = Memory(nc, ctx)
        mask_kq, mask_qk = sb("mask_kq32", [P, P]), sb("mask_qk32", [P, P])
        ld = signals(nc, ctx, "load", "consts made")
        with nc.Block() as block:
            @block.sync
            def _(sp):
                for tile, name in ((m.ident, "ident"), (mask_kq, "mask_kq"), (mask_qk, "mask_qk")):
                    sp.dma_start(tile[:, :], I[name]).then_inc(ld.consts, 16)
                sp.wait_ge(ld.consts, 48)

            @block.vector
            def _(dve):
                dve.memset(m.eps[:, :], EPS).then_inc(ld.made, 1)
                dve.memset(m.misfit[:, :], 0.0).then_inc(ld.made, 1)
                dve.memset(m.x[:, 0, 0:P], -1.0).then_inc(ld.made, 1)
                dve.wait_ge(ld.made, 3)
                dve.tensor_copy(m.negones[:, :], m.x[:, 0, 0:P]).then_inc(ld.made, 1)
                dve.wait_ge(ld.consts, 48)
                dve.tensor_copy(m.ident16[:, :], m.ident[:, :]).then_inc(ld.made, 1)
                dve.tensor_copy(m.mask_kq[:, :], mask_kq[:, :]).then_inc(ld.made, 1)
                dve.tensor_copy(m.mask_qk[:, :], mask_qk[:, :]).then_inc(ld.made, 1)

        m.weights_copied = ctx.enter_context(nc.semaphore("weights_copied"))
        m.weights_copy = nc.dram_tensor("weights_copy", (P, sum(c * n for _name, c, n in WEIGHTS4)), F32, kind="Internal").ap()
        m.weights_given = [I[name] for name, _c, _n in WEIGHTS4]

        rows = lambda dram: dram.rearrange("(b t p) d -> b p t d", b=SEQS, p=P)
        here = src
        for layer, there in zip(layers, scratch):
            with ExitStack() as own:
                used = layer(nc, own, m, I, rows(here), rows(there))
                with nc.Block() as block:
                    @block.gpsimd
                    def _(pool):
                        for stage in used:
                            clear(pool, stage)
            here = there



def lay(w):
    return w.reshape(w.shape[0] // P, P, -1).transpose(1, 0, 2)


def by_partition(v):
    return v.reshape(-1, P).T


def to_all(v):
    return np.broadcast_to(v.reshape(1, -1), (P, v.size))


def constants():
    k, q = np.meshgrid(np.arange(P), np.arange(P), indexing="ij")
    hidden = np.float32(-2.0 ** 100)
    return {
        "ident": np.eye(P, dtype=np.float32), "mask_kq": np.where(q < k, hidden, np.float32(0.0)),
        "mask_qk": np.where(k < q, hidden, np.float32(0.0)),
    }


def layout1(i):
    return {
        "wqkv": lay(i["L0_attn_qkv_w"]), "wgate": lay(i["L0_attn_gate_w"]), "bqkv": by_partition(i["L0_attn_qkv_b"]),
        "bgate": by_partition(i["L0_attn_gate_b"]), "bv": to_all(i["L0_attn_qkv_b"][2 * D:]),
        "lng": by_partition(i["L0_attn_ln_g"]), "lnb": by_partition(i["L0_attn_ln_b"]),
    }


def layout2(i):
    pick = np.zeros((P, H0 // 2, NE, 2), np.float32)
    for c in range(H0 // 2):
        for e in range(NE):
            for a in range(2):
                pick[(2 * c + a) * NE + e::H0 * NE, c, e, a] = 1.0
    ve = i["L0_ffn_value_experts"].transpose(2, 1, 0, 3)
    oe = i["L0_ffn_output_experts"].reshape(NE, H0 // 2, P, D).transpose(2, 1, 0, 3)
    return {
        "wq2": lay(i["L0_ffn_w_q"]), "wk2": lay(i["L0_ffn_w_k"]), "wg2": lay(i["L0_ffn_w_gate"]),
        "ve2": lay(ve.reshape(D, -1)).reshape(P, KC, H0, NE * DH0), "oe2": oe,
        "prio": to_all(np.arange(NE, 0, -1, dtype=np.float32)),
        "pick": pick.reshape(P, -1),
    }


def layout3(i):
    out = np.arange(P)
    copy = out % (4 * DH1) // DH1
    select = np.zeros((P, 2, 2, 4, P), np.float32)
    for r in range(4):
        source = (2 * r + out // (4 * DH1)) * DH1 + out % DH1
        for kind, lo in ((0, copy >= 2), (1, copy % 2 == 1)):
            select[source, kind, lo.astype(int), r, out] = 1.0
    return {
        "wq3": lay(i["L1_attn_Wq"]), "wk3": lay(i["L1_attn_Wk"]), "wv3": lay(i["L1_attn_Wv"]),
        "wo3": lay(i["L1_attn_Wo"]), "bq3": by_partition(i["L1_attn_bq"]), "bk3": by_partition(i["L1_attn_bk"]),
        "bv3": to_all(i["L1_attn_bv"]), "bo3": to_all(i["L1_attn_bo"]), "w13": lay(i["L1_attn_dp_w1"]),
        "hv3": np.stack([to_all(i["L1_attn_" + n]) for n in ("dp_b1", "ln_g", "ln_b", "dp_w2")], 1),
        "gv3": np.stack([to_all(i["L1_attn_" + n]) for n in ("g_w1", "g_b1", "g_w2")], 1),
        "b23": np.concatenate([to_all(i["L1_attn_dp_b2"]), to_all(i["L1_attn_g_b2"])], 1),
        "select3": select.reshape(P, -1),
    }


def layout4(i):
    n = lambda name: i["L1_ffn_" + name]
    return {
        "w14": lay(n("w1_w").T), "w24": lay(n("w2_w").T), "h14": lay(n("h1_w").T), "h24": lay(n("h2_w").T),
        "w34": lay(n("w3_w").T), "scale4": np.stack([by_partition(n(x)) for x in ("w1_s", "w2_s", "h1_s", "h2_s")], 1),
        "s34": to_all(n("w3_s")),
    }


def kernel(**inputs):
    import concourse.bacc as bacc
    from concourse.bass_utils import run_bass_kernel_spmd

    given = {name: np.asarray(a) for name, a in inputs.items()}
    arrays = {"tokens": given["L0_attn_x"].reshape(SEQS * T, D), **constants(), **layout1(given), **layout2(given),
              **layout3(given), **layout4(given)}
    arrays = {name: np.ascontiguousarray(a) for name, a in arrays.items()}
    nc = bacc.Bacc("TRN2", target_bir_lowering=False, num_devices=1)
    I = {name: nc.dram_tensor(name, a.shape, mybir.dt.from_np(a.dtype), kind="ExternalInput").ap() for name, a in arrays.items()}
    scratch = [nc.dram_tensor(f"sums{n}", (SEQS * T, D), F32, kind="Internal").ap() for n in range(1, 4)]
    out = nc.dram_tensor("normed", (SEQS * T, D), F32, kind="ExternalOutput").ap()
    program(nc, I, [layer1, layer2, layer3, layer4], I["tokens"], [*scratch, out])
    got = run_bass_kernel_spmd(nc, [arrays], core_ids=[0]).results[0]["normed"]
    return got.reshape(SEQS, T, D)
```
